# Optimizing a Trainium2 kernel written in Bass

```python
import numpy as np
import jax
import jax.numpy as jnp

def _softmax(x, axis=-1):
    return jax.nn.softmax(x, axis=axis)

def _gelu(x):
    return jax.nn.gelu(x, approximate=True)

def _silu(x):
    return jax.nn.silu(x)

def _sigmoid(x):
    return jax.nn.sigmoid(x)

def _layernorm(x, axis=-1, eps=1e-05):
    m = jnp.mean(x, axis=axis, keepdims=True)
    v = jnp.var(x, axis=axis, keepdims=True)
    return (x - m) / jnp.sqrt(v + eps)

def _scatter_add(tgt, idx, src, axis=0):
    return tgt.at[idx].add(src)

def _segment_sum(src, seg, n):
    return jax.ops.segment_sum(src, seg, n)
kernel_name = 'mk_xattn_ffn_d4_seqx_r8_ccc1ac'

def setup_inputs(seed: int=0):
    np.random.seed(seed)
    _w = jnp.asarray

    def _rec_inputs():
        import jax
        import jax.numpy as jnp
        _rk = jax.random.key(seed)
        x = -0.0005207 + 1.001 * jax.random.normal(jax.random.fold_in(_rk, 1), (16, 64, 512), jnp.float32)
        _lenS = 64 - jax.random.randint(jax.random.fold_in(_rk, 7), (16,), 0, max(1, 64 // 4) + 1, jnp.int32)
        _lenS2 = 64 - jax.random.randint(jax.random.fold_in(_rk, 8), (16,), 0, max(1, 64 // 4) + 1, jnp.int32)
        _ctx_4096P = jax.random.normal(jax.random.fold_in(_rk, 11), (16, 16, 512), jnp.float32)
        _ctx_4096c = jax.random.dirichlet(jax.random.fold_in(_rk, 511), 0.3 * jnp.ones((16,), jnp.float32), (16, 64))
        _ctx_4096t = jnp.einsum('bsk,bkd->bsd', _ctx_4096c, _ctx_4096P)
        _ctx_4096t = _ctx_4096t * jax.lax.rsqrt(jnp.mean(jnp.square(_ctx_4096t)) + 1e-12) * 0.953939
        ctx_4096 = -0.00010331 + 0.999899 * (_ctx_4096t + 0.3 * jax.random.normal(jax.random.fold_in(_rk, 611), (16, 64, 512), jnp.float32))
        _validS = jnp.arange(64)[None, :] < _lenS[:, None]
        _validS2 = jnp.arange(64)[None, :] < _lenS2[:, None]
        _causal = jnp.tril(jnp.ones((64, 64), dtype=bool))
        mask_1x1xSxS2_ff0 = jnp.where(jnp.ones((1, 1, 64, 64), dtype=bool), 0.0, -1000000000.0).astype(jnp.float32)
        return (x, ctx_4096, mask_1x1xSxS2_ff0)
    x, ctx_4096, mask_1x1xSxS2_ff0 = _rec_inputs()

    def _L0_xattn_setup():
        import jax, jax.numpy as jnp
        import numpy as np
        import math
        HIDDEN = 512
        N_HEADS = 32
        HEAD_DIM = 128
        N_KV_HEADS = 4
        N_GROUPS = N_HEADS // N_KV_HEADS
        key = jax.random.key(seed)
        ks = jax.random.split(key, 6)
        B, NL, S = (8, 64, 512)
        latents = jax.random.normal(ks[0], (B, NL, HIDDEN), dtype=jnp.float32)
        context = jax.random.normal(ks[1], (B, S, HIDDEN), dtype=jnp.float32)
        scale = 1.0 / math.sqrt(HIDDEN)
        Wq = jax.random.normal(ks[2], (HIDDEN, N_HEADS * HEAD_DIM), dtype=jnp.float32) * scale
        Wk = jax.random.normal(ks[3], (HIDDEN, N_KV_HEADS * HEAD_DIM), dtype=jnp.float32) * scale
        Wv = jax.random.normal(ks[4], (HIDDEN, N_KV_HEADS * HEAD_DIM), dtype=jnp.float32) * scale
        Wo = jax.random.normal(ks[5], (N_HEADS * HEAD_DIM, HIDDEN), dtype=jnp.float32) * scale
        return {'latents': latents, 'context': context, 'Wq': Wq, 'Wk': Wk, 'Wv': Wv, 'Wo': Wo}
    _L0_xattn_all = _L0_xattn_setup()
    _L0_xattn_in = {k: v for k, v in _L0_xattn_all.items() if k in ('Wq', 'Wk', 'Wv', 'Wo')}
    del _L0_xattn_all

    def _L0_ffn_setup():
        import jax, jax.numpy as jnp
        import numpy as np
        N_EXPERTS = 28
        TOP_K = 2
        RANK = 8
        LORA_ALPHA = 16
        SCALING = LORA_ALPHA / RANK
        TEMP = 1.0
        key = jax.random.key(seed)
        ks = jax.random.split(key, 5)
        B, S, D_IN, D_OUT = (4, 256, 512, 512)
        x = jax.random.normal(ks[0], (B, S, D_IN), dtype=jnp.float32)
        base_W = jax.random.normal(ks[1], (D_OUT, D_IN), dtype=jnp.float32) * (1.0 / np.sqrt(D_IN))
        gate_W = jax.random.normal(ks[2], (N_EXPERTS, D_IN), dtype=jnp.float32) * (1.0 / np.sqrt(D_IN))
        lora_A = jax.random.normal(ks[3], (N_EXPERTS, RANK, D_IN), dtype=jnp.float32) * (1.0 / np.sqrt(D_IN))
        lora_B = jax.random.normal(ks[4], (N_EXPERTS, D_OUT, RANK), dtype=jnp.float32) * 0.01
        return {'x': x, 'base_W': base_W, 'gate_W': gate_W, 'lora_A': lora_A, 'lora_B': lora_B}
    _L0_ffn_all = _L0_ffn_setup()
    _L0_ffn_in = {k: v for k, v in _L0_ffn_all.items() if k in ('base_W', 'gate_W', 'lora_A', 'lora_B')}
    del _L0_ffn_all

    def _L1_xattn_setup():
        import jax, jax.numpy as jnp
        import numpy as np
        B, Q, K, D = (1, 128, 6404, 512)
        H, KVH, HD = (32, 8, 128)
        GROUPS = H // KVH
        EPS = 1e-05

        def _rmsnorm(x, w):
            xf = x.astype(jnp.float32)
            var = jnp.mean(xf * xf, axis=-1, keepdims=True)
            return (xf * jax.lax.rsqrt(var + EPS)).astype(x.dtype) * w
        key = jax.random.key(seed)
        ks = jax.random.split(key, 8)
        s = 0.02
        return {'hidden_states': jax.random.normal(ks[0], (B, Q, D), jnp.float32), 'cross_attention_states': jax.random.normal(ks[1], (B, K, D), jnp.float32), 'attention_mask': jnp.zeros((B, 1, Q, K), jnp.float32), 'Wq': jax.random.normal(ks[2], (H * HD, D), jnp.float32) * s, 'Wk': jax.random.normal(ks[3], (KVH * HD, D), jnp.float32) * s, 'Wv': jax.random.normal(ks[4], (KVH * HD, D), jnp.float32) * s, 'Wo': jax.random.normal(ks[5], (D, H * HD), jnp.float32) * s, 'q_norm_w': jnp.ones((HD,), jnp.float32), 'k_norm_w': jnp.ones((HD,), jnp.float32)}
    _L1_xattn_all = _L1_xattn_setup()
    _L1_xattn_in = {k: v for k, v in _L1_xattn_all.items() if k in ('Wq', 'Wk', 'Wv', 'Wo', 'q_norm_w', 'k_norm_w')}
    del _L1_xattn_all

    def _L1_ffn_setup():
        import jax, jax.numpy as jnp
        import numpy as np
        E = 8
        R = 8
        DIN = 512
        DOUT = 512
        TOP_K = 2
        SCALING = 2.0

        def _moe_lora(xf, gate_W, A, B):
            gate_probs = jax.nn.softmax(xf @ gate_W.T, axis=-1)
            weights, sel = jax.lax.top_k(gate_probs, TOP_K)
            weights = weights / jnp.sum(weights, axis=-1, keepdims=True)
            T = xf.shape[0]
            w_dense = jnp.zeros((T, E), xf.dtype).at[jnp.arange(T)[:, None], sel].add(weights)
            h = jnp.einsum('td,erd->ter', xf, A)
            h = h * (w_dense[:, :, None] * SCALING)
            return jnp.einsum('ter,eor->to', h, B)
        key = jax.random.key(seed)
        k0, k1, k2, k3, k4 = jax.random.split(key, 5)
        x = jax.random.normal(k0, (4, 256, DIN), jnp.float32)
        W_base = jax.random.normal(k1, (DOUT, DIN), jnp.float32) * 0.02
        gate_W = jax.random.normal(k2, (E, DIN), jnp.float32) * 0.02
        A = jax.random.normal(k3, (E, R, DIN), jnp.float32) * 0.02
        B = jax.random.normal(k4, (E, DOUT, R), jnp.float32) * 0.02
        return {'x': x, 'W_base': W_base, 'gate_W': gate_W, 'A': A, 'B': B}
    _L1_ffn_all = _L1_ffn_setup()
    _L1_ffn_in = {k: v for k, v in _L1_ffn_all.items() if k in ('W_base', 'gate_W', 'A', 'B')}
    del _L1_ffn_all

    def _L2_xattn_setup():
        import jax, jax.numpy as jnp
        import numpy as np
        EMB_DIM = 64
        HEADS = 8
        key = jax.random.key(seed)
        kq, kk, kv = jax.random.split(key, 3)
        B, C, N = (8, EMB_DIM, 512)
        q = jax.random.normal(kq, (B, C, N), dtype=jnp.float32)
        k = jax.random.normal(kk, (B, C, N), dtype=jnp.float32)
        v = jax.random.normal(kv, (B, C, N), dtype=jnp.float32)
        return {'q': q, 'k': k, 'v': v}
    _L2_xattn_all = _L2_xattn_setup()
    _L2_xattn_in = {k: v for k, v in _L2_xattn_all.items() if k in ()}
    del _L2_xattn_all

    def _L2_ffn_setup():
        import jax, jax.numpy as jnp
        import numpy as np
        LORA_SCALE = 16.0 / jnp.sqrt(16.0)
        TOP_K = 2
        key = jax.random.key(seed)
        k1, k2, k3, k4 = jax.random.split(key, 4)
        B_, S, D, O, E, R = (4, 256, 512, 512, 4, 16)
        x = jax.random.normal(k1, (B_, S, D), dtype=jnp.float32)
        router_w = jax.random.normal(k2, (E, D), dtype=jnp.float32) * 0.02
        A = jax.random.normal(k3, (E, R, D), dtype=jnp.float32) * 0.02
        B = jax.random.normal(k4, (O,), dtype=jnp.float32)
        B = jax.random.normal(k4, (E, O, R), dtype=jnp.float32) * 0.02
        return {'x': x, 'router_w': router_w, 'A': A, 'B': B}
    _L2_ffn_all = _L2_ffn_setup()
    _L2_ffn_in = {k: v for k, v in _L2_ffn_all.items() if k in ('router_w', 'A', 'B')}
    del _L2_ffn_all

    def _L3_xattn_setup():
        import jax, jax.numpy as jnp
        import numpy as np
        EPS = 1e-06

        def rmsnorm(x, w):
            xf = x.astype(jnp.float32)
            var = jnp.mean(xf * xf, axis=-1, keepdims=True)
            return (xf * jax.lax.rsqrt(var + EPS)).astype(x.dtype) * w
        key = jax.random.key(seed)
        ks = jax.random.split(key, 6)
        B, T, S, Dt, Df = (4, 128, 72, 512, 512)
        text = jax.random.normal(ks[0], (B, T, Dt), dtype=jnp.float32)
        features = jax.random.normal(ks[1], (B, S, Df), dtype=jnp.float32)
        lim_q = float(np.sqrt(6.0 / (Dt + Df)))
        lim_k = float(np.sqrt(6.0 / (Df + Df)))
        Wq_w = jax.random.uniform(ks[2], (Df, Dt), minval=-lim_q, maxval=lim_q, dtype=jnp.float32)
        Wk_w = jax.random.uniform(ks[3], (Df, Df), minval=-lim_k, maxval=lim_k, dtype=jnp.float32)
        bq = 1.0 / np.sqrt(Dt)
        bk = 1.0 / np.sqrt(Df)
        Wq_b = jax.random.uniform(ks[4], (Df,), minval=-bq, maxval=bq, dtype=jnp.float32)
        Wk_b = jax.random.uniform(ks[5], (Df,), minval=-bk, maxval=bk, dtype=jnp.float32)
        fn_w = jnp.ones((Df,), dtype=jnp.float32)
        qn_w = jnp.ones((Df,), dtype=jnp.float32)
        kn_w = jnp.ones((Df,), dtype=jnp.float32)
        return {'text': text, 'features': features, 'Wq_w': Wq_w, 'Wq_b': Wq_b, 'Wk_w': Wk_w, 'Wk_b': Wk_b, 'fn_w': fn_w, 'qn_w': qn_w, 'kn_w': kn_w}
    _L3_xattn_all = _L3_xattn_setup()
    _L3_xattn_in = {k: v for k, v in _L3_xattn_all.items() if k in ('Wq_w', 'Wq_b', 'Wk_w', 'Wk_b', 'fn_w', 'qn_w', 'kn_w')}
    del _L3_xattn_all

    def _L3_ffn_setup():
        import jax, jax.numpy as jnp
        import numpy as np
        IN_F = 512
        OUT_F = 512
        N_CLUSTERS = 64
        THRESHOLD = 0.01
        TEMPERATURE = 0.1
        BATCH, SEQ = (4, 256)
        key = jax.random.key(seed)
        k1, k2, k3, k4, k5 = jax.random.split(key, 5)
        s = 1.0 / np.sqrt(IN_F)
        return {'input': jax.random.normal(k1, (BATCH, SEQ, IN_F), dtype=jnp.float32), 'weight': jax.random.normal(k2, (OUT_F, IN_F), dtype=jnp.float32) * s, 'bias': jax.random.uniform(k3, (OUT_F,), dtype=jnp.float32, minval=-s, maxval=s), 'centroids': jax.random.normal(k4, (N_CLUSTERS, IN_F), dtype=jnp.float32) * s, 'assignments': jax.random.randint(k5, (OUT_F,), 0, N_CLUSTERS, dtype=jnp.int32)}
    _L3_ffn_all = _L3_ffn_setup()
    _L3_ffn_in = {k: v for k, v in _L3_ffn_all.items() if k in ('weight', 'bias', 'centroids', 'assignments')}
    del _L3_ffn_all
    return {'x': x, 'ctx_4096': ctx_4096, 'mask_1x1xSxS2_ff0': mask_1x1xSxS2_ff0, 'L0_xattn_Wq': _L0_xattn_in['Wq'], 'L0_xattn_Wk': _L0_xattn_in['Wk'], 'L0_xattn_Wv': _L0_xattn_in['Wv'], 'L0_xattn_Wo': _L0_xattn_in['Wo'], 'L0_ffn_base_W': _L0_ffn_in['base_W'], 'L0_ffn_gate_W': _L0_ffn_in['gate_W'], 'L0_ffn_lora_A': _L0_ffn_in['lora_A'], 'L0_ffn_lora_B': _L0_ffn_in['lora_B'], 'L1_xattn_Wq': _L1_xattn_in['Wq'], 'L1_xattn_Wk': _L1_xattn_in['Wk'], 'L1_xattn_Wv': _L1_xattn_in['Wv'], 'L1_xattn_Wo': _L1_xattn_in['Wo'], 'L1_xattn_q_norm_w': _L1_xattn_in['q_norm_w'], 'L1_xattn_k_norm_w': _L1_xattn_in['k_norm_w'], 'L1_ffn_W_base': _L1_ffn_in['W_base'], 'L1_ffn_gate_W': _L1_ffn_in['gate_W'], 'L1_ffn_A': _L1_ffn_in['A'], 'L1_ffn_B': _L1_ffn_in['B'], 'L2_ffn_router_w': _L2_ffn_in['router_w'], 'L2_ffn_A': _L2_ffn_in['A'], 'L2_ffn_B': _L2_ffn_in['B'], 'L3_xattn_Wq_w': _L3_xattn_in['Wq_w'], 'L3_xattn_Wq_b': _L3_xattn_in['Wq_b'], 'L3_xattn_Wk_w': _L3_xattn_in['Wk_w'], 'L3_xattn_Wk_b': _L3_xattn_in['Wk_b'], 'L3_xattn_fn_w': _L3_xattn_in['fn_w'], 'L3_xattn_qn_w': _L3_xattn_in['qn_w'], 'L3_xattn_kn_w': _L3_xattn_in['kn_w'], 'L3_ffn_weight': _L3_ffn_in['weight'], 'L3_ffn_bias': _L3_ffn_in['bias'], 'L3_ffn_centroids': _L3_ffn_in['centroids'], 'L3_ffn_assignments': _L3_ffn_in['assignments']}

def reference(x, ctx_4096, mask_1x1xSxS2_ff0, L0_xattn_Wq, L0_xattn_Wk, L0_xattn_Wv, L0_xattn_Wo, L0_ffn_base_W, L0_ffn_gate_W, L0_ffn_lora_A, L0_ffn_lora_B, L1_xattn_Wq, L1_xattn_Wk, L1_xattn_Wv, L1_xattn_Wo, L1_xattn_q_norm_w, L1_xattn_k_norm_w, L1_ffn_W_base, L1_ffn_gate_W, L1_ffn_A, L1_ffn_B, L2_ffn_router_w, L2_ffn_A, L2_ffn_B, L3_xattn_Wq_w, L3_xattn_Wq_b, L3_xattn_Wk_w, L3_xattn_Wk_b, L3_xattn_fn_w, L3_xattn_qn_w, L3_xattn_kn_w, L3_ffn_weight, L3_ffn_bias, L3_ffn_centroids, L3_ffn_assignments):
    import jax
    import jax.numpy as jnp

    def _L0_xattn_ref(latents, context, Wq, Wk, Wv, Wo):
        import jax, jax.numpy as jnp
        import numpy as np
        import math
        HIDDEN = 512
        N_HEADS = 32
        HEAD_DIM = 128
        N_KV_HEADS = 4
        N_GROUPS = N_HEADS // N_KV_HEADS
        b, q_len, _ = latents.shape
        kv_len = q_len + context.shape[1]
        hidden_states = jnp.concatenate([context, latents], axis=1)
        q = (latents @ Wq).reshape(b, q_len, N_KV_HEADS, N_GROUPS, HEAD_DIM)
        k = (hidden_states @ Wk).reshape(b, kv_len, N_KV_HEADS, HEAD_DIM)
        v = (hidden_states @ Wv).reshape(b, kv_len, N_KV_HEADS, HEAD_DIM)
        scale = 1.0 / math.sqrt(HEAD_DIM)
        scores = jnp.einsum('bqhgd,bkhd->bhgqk', q, k) * scale
        attn = jax.nn.softmax(scores.astype(jnp.float32), axis=-1).astype(q.dtype)
        out = jnp.einsum('bhgqk,bkhd->bqhgd', attn, v)
        out = out.reshape(b, q_len, N_HEADS * HEAD_DIM)
        return out @ Wo

    def _L0_ffn_ref(x, base_W, gate_W, lora_A, lora_B):
        import jax, jax.numpy as jnp
        import numpy as np
        N_EXPERTS = 28
        TOP_K = 2
        RANK = 8
        LORA_ALPHA = 16
        SCALING = LORA_ALPHA / RANK
        TEMP = 1.0
        B, S, D_in = x.shape
        xf = x.reshape(B * S, D_in)
        base = xf @ base_W.T
        logits = xf @ gate_W.T
        top_vals, top_idx = jax.lax.top_k(logits, TOP_K)
        top_probs = jax.nn.softmax(top_vals / TEMP, axis=-1)
        N = xf.shape[0]
        gate_full = jnp.zeros((N, N_EXPERTS), dtype=xf.dtype).at[jnp.arange(N)[:, None], top_idx].add(top_probs)
        h = jnp.einsum('nd,erd->ner', xf, lora_A)
        h = h * (gate_full * SCALING)[:, :, None]
        lora_out = jnp.einsum('ner,eor->no', h, lora_B)
        out = base + lora_out
        return out.reshape(B, S, -1)

    def _L1_xattn_ref(hidden_states, cross_attention_states, attention_mask, Wq, Wk, Wv, Wo, q_norm_w, k_norm_w):
        import jax, jax.numpy as jnp
        import numpy as np
        B, Q, K, D = (1, 128, 6404, 512)
        H, KVH, HD = (32, 8, 128)
        GROUPS = H // KVH
        EPS = 1e-05

        def _rmsnorm(x, w):
            xf = x.astype(jnp.float32)
            var = jnp.mean(xf * xf, axis=-1, keepdims=True)
            return (xf * jax.lax.rsqrt(var + EPS)).astype(x.dtype) * w
        bsz, q_len, _ = hidden_states.shape
        kv_len = cross_attention_states.shape[1]
        q = (hidden_states @ Wq.T).reshape(bsz, q_len, H, HD).transpose(0, 2, 1, 3)
        k = (cross_attention_states @ Wk.T).reshape(bsz, kv_len, KVH, HD).transpose(0, 2, 1, 3)
        v = (cross_attention_states @ Wv.T).reshape(bsz, kv_len, KVH, HD).transpose(0, 2, 1, 3)
        q = _rmsnorm(q, q_norm_w)
        k = jnp.repeat(k, GROUPS, axis=1)
        v = jnp.repeat(v, GROUPS, axis=1)
        k = _rmsnorm(k, k_norm_w)
        scale = 1.0 / np.sqrt(HD)
        scores = jnp.einsum('bhqd,bhkd->bhqk', q, k) * scale
        scores = scores + attention_mask[:, :, :, :kv_len]
        probs = jax.nn.softmax(scores.astype(jnp.float32), axis=-1).astype(q.dtype)
        out = jnp.einsum('bhqk,bhkd->bhqd', probs, v)
        out = out.transpose(0, 2, 1, 3).reshape(bsz, q_len, H * HD)
        return out @ Wo.T

    def _L1_ffn_ref(x, W_base, gate_W, A, B):
        import jax, jax.numpy as jnp
        import numpy as np
        E = 8
        R = 8
        DIN = 512
        DOUT = 512
        TOP_K = 2
        SCALING = 2.0

        def _moe_lora(xf, gate_W, A, B):
            gate_probs = jax.nn.softmax(xf @ gate_W.T, axis=-1)
            weights, sel = jax.lax.top_k(gate_probs, TOP_K)
            weights = weights / jnp.sum(weights, axis=-1, keepdims=True)
            T = xf.shape[0]
            w_dense = jnp.zeros((T, E), xf.dtype).at[jnp.arange(T)[:, None], sel].add(weights)
            h = jnp.einsum('td,erd->ter', xf, A)
            h = h * (w_dense[:, :, None] * SCALING)
            return jnp.einsum('ter,eor->to', h, B)
        xf = x.reshape(-1, x.shape[-1])
        out = xf @ W_base.T + _moe_lora(xf, gate_W, A, B)
        return out.reshape(*x.shape[:-1], DOUT)

    def _L2_xattn_ref(q, k, v):
        import jax, jax.numpy as jnp
        import numpy as np
        EMB_DIM = 64
        HEADS = 8
        B, C, N = q.shape
        H = HEADS
        dh = C // H
        qh = q.transpose(0, 2, 1).reshape(B, N, H, dh)
        kh = k.transpose(0, 2, 1).reshape(B, N, H, dh)
        vh = v.transpose(0, 2, 1).reshape(B, N, H, dh)
        qh = jax.nn.softmax(qh, axis=3)
        kh = jax.nn.softmax(kh, axis=1)
        kvs = jnp.einsum('bnhd,bnhe->bhde', kh, vh)
        out = jnp.einsum('bnhd,bhde->bnhe', qh, kvs)
        return out.transpose(0, 2, 3, 1).reshape(B, C, N)

    def _L2_ffn_ref(x, router_w, A, B):
        import jax, jax.numpy as jnp
        import numpy as np
        LORA_SCALE = 16.0 / jnp.sqrt(16.0)
        TOP_K = 2
        D = x.shape[-1]
        flat = x.reshape(-1, D)
        logits = flat @ router_w.T
        topk_vals, topk_idx = jax.lax.top_k(logits, TOP_K)
        sparse = jnp.full_like(logits, -jnp.inf)
        rows = jnp.arange(logits.shape[0])[:, None]
        sparse = sparse.at[rows, topk_idx].set(topk_vals)
        gates = jax.nn.softmax(sparse, axis=-1)
        mid = jnp.einsum('tf,erf->ter', flat, A)
        all_deltas = jnp.einsum('ter,eor->teo', mid, B) * LORA_SCALE
        delta = jnp.einsum('te,teo->to', gates, all_deltas)
        return delta.reshape(*x.shape[:-1], -1)

    def _L3_xattn_ref(text, features, Wq_w, Wq_b, Wk_w, Wk_b, fn_w, qn_w, kn_w):
        import jax, jax.numpy as jnp
        import numpy as np
        EPS = 1e-06

        def rmsnorm(x, w):
            xf = x.astype(jnp.float32)
            var = jnp.mean(xf * xf, axis=-1, keepdims=True)
            return (xf * jax.lax.rsqrt(var + EPS)).astype(x.dtype) * w
        features_n = rmsnorm(features, fn_w)
        Q = jnp.einsum('btd,fd->btf', text, Wq_w) + Wq_b
        K = jnp.einsum('bsd,fd->bsf', features_n, Wk_w) + Wk_b
        Q = rmsnorm(Q, qn_w)
        K = rmsnorm(K, kn_w)
        scale = 1.0 / jnp.sqrt(jnp.asarray(K.shape[-1], dtype=Q.dtype))
        scores = jnp.einsum('btf,bsf->bts', Q, K) * scale
        attn = jax.nn.softmax(scores, axis=-1)
        attended = jnp.einsum('bts,bsf->btf', attn, features_n)
        return attended

    def _L3_ffn_ref(input, weight, bias, centroids, assignments):
        import jax, jax.numpy as jnp
        import numpy as np
        IN_F = 512
        OUT_F = 512
        N_CLUSTERS = 64
        THRESHOLD = 0.01
        TEMPERATURE = 0.1
        BATCH, SEQ = (4, 256)
        shape = input.shape
        x = input.reshape(-1, shape[-1])
        dots = jax.nn.softmax(x @ centroids.T / TEMPERATURE, axis=-1)
        hits = dots > THRESHOLD
        query_sel = jnp.any(hits, axis=1)
        cluster_sel = jnp.any(hits, axis=0)
        row_sel = cluster_sel[assignments]
        dense = x @ weight.T + bias
        out = jnp.where(query_sel[:, None] & row_sel[None, :], dense, jnp.zeros((), dense.dtype))
        return out.reshape(*shape[:-1], -1)
    x = x + _L0_xattn_ref(_layernorm(x, axis=-1), ctx_4096, L0_xattn_Wq, L0_xattn_Wk, L0_xattn_Wv, L0_xattn_Wo)
    x = x + _L0_ffn_ref(_layernorm(x, axis=-1), L0_ffn_base_W, L0_ffn_gate_W, L0_ffn_lora_A, L0_ffn_lora_B)
    x = x + _L1_xattn_ref(_layernorm(x, axis=-1), ctx_4096, mask_1x1xSxS2_ff0, L1_xattn_Wq, L1_xattn_Wk, L1_xattn_Wv, L1_xattn_Wo, L1_xattn_q_norm_w, L1_xattn_k_norm_w)
    x = x + _L1_ffn_ref(_layernorm(x, axis=-1), L1_ffn_W_base, L1_ffn_gate_W, L1_ffn_A, L1_ffn_B)
    x = x + _L2_xattn_ref(_layernorm(x, axis=-1), ctx_4096, ctx_4096)
    x = x + _L2_ffn_ref(_layernorm(x, axis=-1), L2_ffn_router_w, L2_ffn_A, L2_ffn_B)
    x = x + _L3_xattn_ref(_layernorm(x, axis=-1), ctx_4096, L3_xattn_Wq_w, L3_xattn_Wq_b, L3_xattn_Wk_w, L3_xattn_Wk_b, L3_xattn_fn_w, L3_xattn_qn_w, L3_xattn_kn_w)
    x = x + _L3_ffn_ref(_layernorm(x, axis=-1), L3_ffn_weight, L3_ffn_bias, L3_ffn_centroids, L3_ffn_assignments)
    return x

_drawn_inputs = setup_inputs


def setup_inputs(seed=0):
    import zlib

    import numpy as np

    out = dict(_drawn_inputs(seed))
    spreads = {'L1_xattn_q_norm_w': (1.0, 0.6),
     'L1_xattn_k_norm_w': (1.0, 0.6),
     'L3_xattn_fn_w': (1.0, 0.2),
     'L3_xattn_qn_w': (1.0, 0.6),
     'L3_xattn_kn_w': (1.0, 0.6)}
    factors = {'L0_ffn_gate_W': 3.12,
     'L0_ffn_lora_A': 3.048,
     'L0_ffn_lora_B': 3.046,
     'L1_ffn_gate_W': 4.354,
     'L1_ffn_A': 3.854,
     'L1_ffn_B': 3.901,
     'L3_xattn_Wq_b': 8.0,
     'L3_xattn_Wk_b': 8.0,
     'L3_ffn_bias': 6.569}
    for name, (base, spread) in spreads.items():
        noise = np.random.default_rng([zlib.crc32(name.encode()), seed]).standard_normal(out[name].shape)
        drawn = base * np.exp(spread * noise) if base else spread * noise
        out[name] = jnp.asarray(drawn.astype(out[name].dtype))
    for name, factor in factors.items():
        out[name] = (out[name] * factor).astype(out[name].dtype)
    return out
```

```python
import concourse.bass as bass
from concourse import mybir


P = 128
B, S, D = 16, 64, 512
TOK = B * S
NT = TOK // P
KT = D // P
HD = 128
HQ = 4
NHG = 32 // HQ
STEPS = NHG * NT
TEMPERATURE, THRESHOLD = 0.1, 0.01
LAG = 4
LN_SLOT = STEPS - 4
LN_EPS = 1e-5
RMS_EPS, RMS_EPS3 = 1e-5, 1e-6
HI, LO = 0, 1
PASSES = ((HI, HI), (HI, LO), (LO, HI))


class Step:

    def __init__(self, base, n, i=None, unroll=0, done=0):
        self.base, self.n, self.i, self.unroll = base, n, i, unroll
        self.done = done

    @property
    def c(self):
        at = self.base + self.done
        return at if self.i is None else self.i * self.unroll + at

    @property
    def t(self):
        return self.base if self.i is None else self.i * self.unroll + self.base

    @property
    def exists(self):
        return self.i is not None or 0 <= self.base < self.n

    @property
    def static(self):
        return self.i is None

    def back(self, k):
        return Step(self.base - k, self.n, self.i, self.unroll, self.done)

    def res(self, m):
        return self.base % m

    def div(self, m):
        q = self.base // m
        return q if self.i is None else self.i * (self.unroll // m) + q


def steps(eng, n, unroll, lag, done):
    loops = (n - lag - NT) // unroll
    if loops < 2:
        loops = 0
    for t in range(lag):
        yield Step(t, n, done=done)
    if loops:
        with eng.Fori(0, loops) as i:
            for t in range(lag, lag + unroll):
                yield Step(t, n, i, unroll, done)
    for t in range(lag + loops * unroll, n + lag):
        yield Step(t, n, done=done)


def need(eng, sem, value):
    if isinstance(value, int) and value <= 0:
        return
    eng.wait_ge(sem, value)


class Sems:

    def __init__(self, nc, layer):
        self._nc, self._layer, self._of = nc, layer, {}

    def __getitem__(self, what):
        if what not in self._of:
            self._of[what] = self._nc.alloc_semaphore(f"{self._layer}_{what}")
        return self._of[what]


def build(nc, io):
    f32, f32r, i32, u32 = mybir.dt.float32, mybir.dt.float32r, mybir.dt.int32, mybir.dt.uint32
    ALU, ACT, AX = mybir.AluOpType, mybir.ActivationFunctionType, mybir.AxisListType
    sb = lambda name, shape, dt=f32: nc.alloc_sbuf_tensor(name, [P, *shape], dt)
    ps = lambda name, shape: nc.alloc_psum_tensor(name, [P, *shape], f32)

    x = sb("x_res", [NT, D])
    hT = sb("hT", [2, KT, NT, 4, S], f32r)
    wq = sb("wq", [2, KT, D], f32r)
    wo = sb("wo", [2, KT, D], f32r)
    wkv = sb("wkv", [2, 2, D], f32r)
    stage_q = sb("stage_q", [KT, D])
    stage_o = sb("stage_o", [KT, D])
    stage_kv = sb("stage_kv", [2, D])
    arena = sb("arena", [8192], f32r)
    half = lambda n: arena[:, n * 4096:(n + 1) * 4096].rearrange("p (n h c) -> p n h c", n=NT, h=2)
    kT0, v0 = half(0), half(1)
    ctxT = arena[:].rearrange("p (h k t) -> p h k t", h=2, k=KT)
    kT1 = sb("kT1", [4, 2, HD], f32r)
    v1 = sb("v1", [4, 2, HD], f32r)
    q_sb = sb("q_sb", [D])
    k_sb = sb("k_sb", [2 * HD])
    qT = sb("qT", [2, 2, HQ, S], f32r)
    s_sb = sb("s_sb", [2 * P])
    prob = sb("prob", [D])
    pT = sb("pT", [2, D], f32r)
    oT = sb("oT", [2, HQ, P], f32r)
    xn = sb("xn", [2, D])
    ident = sb("ident", [P])
    minus_half = sb("minus_half", [8])
    bn = sb("bn", [2, 6])
    mv = sb("mv", [NT, 2])
    var_eps = sb("var_eps", [NT])
    rstd = sb("rstd", [NT])
    mx = sb("mx", [4])
    neg_mx = sb("neg_mx", [4])
    sums = sb("sums", [4])
    rsums = sb("rsums", [4])
    ssq = sb("ssq", [2, 5])
    ms_eps = sb("ms_eps", [2, 5])
    rms = sb("rms", [2, 5])
    mask = sb("mask", [S])
    wqk = sb("wqk", [3])
    wqk3 = sb("wqk3", [3, KT])
    wide = sb("wide", [D])
    ones = sb("ones", [P])
    ones_r = sb("ones_r", [P], f32r)
    iota = sb("iota", [32])
    row_id = sb("row_id", [1])
    block8 = sb("block8", [P])
    logits = sb("logits", [32])
    top = sb("top", [8])
    top_at = sb("top_at", [8], u32)
    top_f = sb("top_f", [2])
    pick = sb("pick", [2, 32])
    gate = sb("gate", [32])
    small = sb("small", [16])
    q_any = sb("q_any", [NT])

    psQ, psKV, psT, psS, psP, psY = (ps(n, [D]) for n in ("psQ", "psKV", "psT", "psS", "psP", "psY"))
    psO = ps("psO", [2, D])

    setup = Sems(nc, "setup")
    ld = Sems(nc, "ld")
    A = Sems(nc, "attn")
    ln_even, ln_odd = Sems(nc, "ln_even"), Sems(nc, "ln_odd")
    LNS = [ln_even, ln_odd, ln_even, ln_odd, Sems(nc, "ln_l2"), ln_odd, ln_even, ln_odd]
    out_done = nc.alloc_semaphore("out_done")

    FS = Sems(nc, "ffn")
    M, N3, C3 = Sems(nc, "m2"), Sems(nc, "a3"), Sems(nc, "c3")
    chain = nc.alloc_semaphore("dve_chain")

    def ln_at(ln, n):
        return sum(other is LNS[ln] for other in LNS[:ln]) * NT + n

    class Ffn:

        def __init__(self, index, ln, E, R, dense, scale, wkv_n, wo_n):
            self.index, self.ln, self.E, self.R = index, ln, E, R
            self.done = index * NT
            self.dense, self.scale = dense, scale
            self.width = E + E * R
            self.parts = 2 if E * R > P else 1
            self.rows = E * R // self.parts
            self.wkv_n, self.wo_n = wkv_n, wo_n

    FF = [Ffn(0, 1, 28, 8, True, 2.0, 10, 38), Ffn(1, 3, 8, 8, True, 2.0, 28, 71), Ffn(2, 5, 4, 16, False, 4.0, 30, 72)]
    WQ_DENSE = [9, 18]

    class Attn:
        def __init__(self, index):
            self.index = index
            self.done, self.kv_done = (0, 0) if index == 0 else (STEPS, STEPS // 2)
            self.rms = index == 1
            self.keys = 2 * S if index == 0 else S
            self.unroll = 2 * NT if index == 0 else NT
            self.kv_period = self.unroll
            self.kT, self.v, self.ring = (kT0, v0, NT) if index == 0 else (kT1, v1, 4)
            self.wq0, self.wo0, self.wkv0 = (1, 4, 0) if index == 0 else (10, 38, 10)

        def kv_new(self, st):
            return st.exists and st.res(self.kv_period) < NT

        def kv_n(self, st):
            return st.div(self.kv_period) * NT + (st.res(NT) + self.kv_done)

        scale = HD ** -0.5

    L0, L1 = Attn(0), Attn(1)

    def heads(ap):
        return ap.rearrange("p (h b t) -> p b h t", h=HQ, b=2)

    def tok(n):
        return slice(n * P, (n + 1) * P)

    def lat(hl, k, n):
        return hT[:, hl, k, n, 1:3].rearrange("p b t -> p (b t)")

    def lat_all(hl, n):
        return hT[:, hl, :, n, 1:3].rearrange("p k b t -> p k (b t)")

    def slices(bank):
        return bank[:].rearrange("p (k t) -> p k t", k=KT)

    def hidden(hl, k, n, b):
        return hT[:, hl, k, n, 2 * b:2 * b + 2].rearrange("p b t -> p (b t)")

    def ctx_part(hl, k, half):
        return hT[:, hl, k, half * 4:half * 4 + 4, 0:4:3, :]

    def xn_slot(ln, n):
        return {4: 0, 5: 1}.get(ln, n % 2)

    def ring3(n):
        return (psY, psS, psKV)[n % 3]

    eT, q2, kvs_r = (kT1[:].rearrange("p a h c -> p (a h c)").rearrange("p (h k c) -> p h k c", h=2, k=KT),
                     qT[:].rearrange("p h b g t -> p h (b g t)"),
                     v1[:].rearrange("p a h c -> p (a h c)").rearrange("p (a h c) -> p a h c", a=4, h=2))
    hidT = oT
    def cut(at, *shape):
        size, names = 1, "abc"[:len(shape)]
        for x_ in shape:
            size *= x_
        v_ = arena[:, at:at + size]
        return v_.rearrange(f"p ({' '.join(names)}) -> p {' '.join(names)}", **dict(zip(names, shape)))
    f_r, fT, kT3, qT3, pT3 = cut(0, 2, 2, D), cut(2048, 2, KT, P), cut(3072, 2, KT, P), cut(4096, 2, KT, P), cut(5120, 2, P)
    k3, k3w = prob, prob
    kvs = k_sb[:, HD:2 * HD]
    junk_k = prob[:, 3 * HD:4 * HD]
    junk_q = [pT[:, h // 2, (2 + h % 2) * HD:(3 + h % 2) * HD] for h in range(HQ)]
    junk_f3, junk_k3, junk_q3 = (t[:, a:a + 2].rearrange("p a h c -> p (a h c)") for t, a in ((kT1, 0), (kT1, 2), (v1, 0)))
    hit_ring = xn[:].rearrange("p a c -> p (a c)")

    def pick64(n):
        return hit_ring[:, (n % 2) * 64:(n % 2) * 64 + 64]

    bias_row = {"q": 0, "k": 32, "o": 64}

    def wkv_k(hl, k, width):
        return wkv[:, hl, k // 2, (k % 2) * width:(k % 2 + 1) * width]

    block_cm = nc.Block()
    block = block_cm.__enter__()

    @block.sync
    def _(sp):
        for n in range(NT):
            sp.dma_start(x[:, n], io["x"][:, n]).then_inc(ld[f"x{n}"], 16)
        sp.dma_start(stage_q[:], io["ctxT"][0]).then_inc(ld["wq_in"], 16)
        sp.dma_start(stage_o[:], io["ctxT"][1]).then_inc(ld["wo_in"], 16)
        sp.dma_start(stage_kv[:], io["wkv0"][0]).then_inc(ld["wkv_in"], 16)
        for b in range(2):
            sp.dma_start(mask[b * S:(b + 1) * S], io["mask"]).then_inc(ld["small"], 16)
        for c, what in enumerate(("qn1", "kn1")):
            sp.dma_start(wqk[:, c:c + 1], io[what]).then_inc(ld["small"], 16)
        for c, what in enumerate(("qn3", "kn3")):
            sp.dma_start(wqk3[:, c], io[what]).then_inc(ld["small"], 16)
        for c, what in enumerate(("bq3", "bk3", "bias3")):
            sp.dma_start(wide[32 * c:32 * c + 1], io[what]).then_inc(ld["vec_in"], 16)

        def load(what, stage, src, split_before):
            sp.wait_ge(ld[what + "_lo"], split_before)
            sp.dma_start(stage, src).then_inc(ld[what + "_in"], 16)

        def load_wq(src, loads_before):
            sp.wait_ge(ld["wq_lo"], loads_before * 2)
            sp.wait_ge(ld["wq_lo_v"], loads_before * 2)
            sp.dma_start(stage_q[:], src).then_inc(ld["wq_in"], 16)

        load_wq(io["wq0"][0], 1)
        load("wo", stage_o[:], io["wo0"][0], 4)
        with sp.Fori(0, 3) as kv:
            load_wq(io["wq0"][kv * 2 + 1], kv * 2 + 2)
            load("wkv", stage_kv[:], io["wkv0"][kv + 1], kv * 2 + 2)
            load("wo", stage_o[:], io["wo0"][kv * 2 + 1], kv * 8 + 8)
            load_wq(io["wq0"][kv * 2 + 2], kv * 2 + 3)
            load("wo", stage_o[:], io["wo0"][kv * 2 + 2], kv * 8 + 12)
        load_wq(io["wq0"][7], 8)
        load("wo", stage_o[:], io["wo0"][7], 32)
        load("wkv", stage_kv[:, :, 0:504], io["ga0"], 8)
        load_wq(io["base0"], 9)
        load("wo", stage_o[0:112, 0:2], io["b0"], 36)
        load("wkv", stage_kv[:], io["wkv1"][0], 10)
        load_wq(io["wq1"][0], 10)
        load("wo", stage_o[:], io["wo1"][0], 38)
        with sp.Fori(1, NHG) as hg:
            load("wkv", stage_kv[:], io["wkv1"][hg], hg * 2 + 10)
            load_wq(io["wq1"][hg], hg + 10)
            load("wo", stage_o[:], io["wo1"][hg], hg * 4 + 38)
        load("wkv", stage_kv[:, :, 0:144], io["ga1"], 26)
        load_wq(io["base1"], 18)
        load("wo", stage_o[0:64, 0:1], io["b1"], 70)
        load("wkv", stage_kv[:, :, 0:136], io["ga2"], 28)
        load_wq(io["wq3"], 19)
        load("wo", stage_o[0:64, 0:1], io["b2"], 71)
        sp.wait_ge(ld["wq_lo"], 40)
        sp.wait_ge(ld["wq_lo_v"], 40)
        for n in range(2 * NT):
            if n == NT:
                load("wo", stage_o[:], io["wk3"], 72)
                load("wkv", stage_kv[:, :, 0:128], io["cent"], 30)
                sp.wait_ge(ld["vec_lo"], 1)
                sp.dma_start(wide[:], io["fn_w"].to_broadcast([P, D])).then_inc(ld["fn_in"], 16)
            if n >= 4:
                if n - 4 < NT:
                    sp.wait_ge(M["e_tr"], n - 3)
                else:
                    sp.wait_ge(N3["f_lo"], n - 4 - NT + 1)
                    sp.wait_ge(N3["f_tr"], n - 4 - NT + 1)
            sp.dma_start(stage_q[:, n % 4], io["ctx"][:, n % NT]).then_inc(ld[f"c{n % 4}"], 16)
        load("wo", stage_o[:], io["w3"], 76)
        sp.wait_ge(N3["q_tr"], NT)
        sp.dma_start(q_sb[0:64].bitcast(i32), io["asg"].to_broadcast([64, D])).then_inc(ld["asg_in"], 16)
        for n in range(NT):
            sp.wait_ge(C3["out"], n + 1)
            sp.dma_start(io["out"][:, n], x[:, n]).then_inc(out_done, 16)
        sp.wait_ge(out_done, 16 * NT)
    @block.gpsimd
    def _(pool):
        g = nc.gpsimd
        g.memset(minus_half[:], -0.5).then_inc(setup["const"], 1)
        g.memset(ident[:], 0.0).then_inc(setup["const"], 1)
        pool.wait_ge(setup["const"], 2)
        g.affine_select(out=ident[:], in_=ident[:], compare_op=ALU.not_equal, fill=1.0, base=0,
                        pattern=[[-1, P]], channel_multiplier=1).then_inc(setup["const"], 1)

        def low(what, dst, stage, hi_count):
            pool.wait_ge(ld[what + "_hi"], hi_count)
            g.tensor_tensor(dst[LO], stage, dst[HI].bitcast(f32), ALU.subtract).then_inc(ld[what + "_lo"], 1)

        def low_ctx(what, stage, half, slices_):
            for k in slices_:
                low(what, (ctx_part(HI, k, half), ctx_part(LO, k, half)),
                    stage[:, k].rearrange("p (n b t) -> p n b t", n=4, b=2), k + 1)

        def halves(t, *at):
            return t[(slice(None), HI, *at)], t[(slice(None), LO, *at)]

        def ln_rstd(ln, n):
            pool.wait_ge(LNS[ln]["var"], ln_at(ln, n + 1))
            g.tensor_tensor(rstd[:, n:n + 1], var_eps[:, n:n + 1], minus_half[:, 0:1],
                            ALU.pow).then_inc(LNS[ln]["rstd"], 1)

        g.memset(ones[:], 1.0).then_inc(setup["ones"], 1)
        g.iota(iota[:], [[1, 32]], base=0, channel_multiplier=0,
               allow_small_or_imprecise_dtypes=True).then_inc(setup["iota"], 1)
        g.iota(row_id[:], [[0, 1]], base=0, channel_multiplier=1,
               allow_small_or_imprecise_dtypes=True).then_inc(setup["iota"], 1)
        g.memset(block8[:], 1.0).then_inc(setup["b8"], 1)
        groups = block8[:].rearrange("p (g e) -> p g e", e=8)
        pool.wait_ge(setup["b8"], 1)
        g.affine_select(out=groups, in_=groups, compare_op=ALU.is_ge, fill=0.0, base=0,
                        pattern=[[-8, 16], [0, 8]], channel_multiplier=1).then_inc(setup["b8"], 1)
        pool.wait_ge(setup["b8"], 2)
        g.affine_select(out=groups, in_=groups, compare_op=ALU.is_ge, fill=0.0, base=7,
                        pattern=[[8, 16], [0, 8]], channel_multiplier=-1).then_inc(setup["b8"], 1)

        for n in range(NT):
            ln_rstd(0, n)
        low_ctx("wq", stage_q, 0, range(2))
        low_ctx("wo", stage_o, 1, range(KT))

        def low_wq(load):
            for k in range(2):
                low("wq", halves(wq, k), stage_q[:, k], load * 4 + (k + 1))

        def low_wo(count, n=KT):
            for k in range(n):
                low("wo", halves(wo, k), stage_o[:, k], count + k + 1)

        def low_wkv(count, width=D):
            for k in range(2):
                low("wkv", halves(wkv, k, slice(0, width)), stage_kv[:, k, 0:width], count + k + 1)

        low_wkv(0)
        low_wq(1)
        with pool.Fori(0, 3) as kv:
            low_wo(kv * 8 + 4)
            low_wq(kv * 2 + 2)
            low_wo(kv * 8 + 8)
            low_wkv(kv * 2 + 2)
            low_wq(kv * 2 + 3)
        low_wo(28)
        low_wq(8)
        low_wo(32)
        for n in range(NT):
            ln_rstd(1, n)
            if n == 0:
                low_wkv(8, 504)
            if n == 3:
                low_wq(9)

        def low_b(f, count):
            for j in range(f.parts):
                low("wo", (wo[0:f.rows, HI, j], wo[0:f.rows, LO, j]), stage_o[0:f.rows, j], count + j + 1)

        low_b(FF[0], 36)
        for n in range(NT):
            if n == 6:
                low_wkv(10)
                low_wq(10)
            ln_rstd(2, n)
        s = A
        for t in steps(pool, STEPS, L1.unroll, LAG, L1.done):
            if t.static and 0 <= t.t - LN_SLOT < NT:
                ln_rstd(3, t.t - LN_SLOT)
            if t.exists:
                pool.wait_ge(s["ms"], t.t + 1)
                need(pool, s["k_read"], t.t + L1.kv_done - 1)
                g.tensor_tensor(rms[:, t.res(2)], ms_eps[:, t.res(2)], minus_half[:, 0:5],
                                ALU.pow).then_inc(s["rms"], 1)
            if t.res(8) == 7 and t.exists:
                low_wq(t.div(8) + 11)
                if t.static and t.t == STEPS - 1:
                    low_wkv(26, 144)
                else:
                    low_wkv(t.div(8) * 2 + 12)
            if t.res(8) == 2 and not (t.static and t.t >= 64):
                low_wo(t.div(8) * 4 + 38)
        low_b(FF[1], 70)
        for n in range(NT):
            ln_rstd(4, n)
        low_wkv(28, 136)
        low_wq(19)
        low_b(FF[2], 71)
        for n in range(NT):
            ln_rstd(5, n)
        for n in range(NT):
            ln_rstd(6, n)
        low_wo(72)
        low_wkv(30, 128)
        def power(what, n, col):
            pool.wait_ge(N3["ms_" + what], n + 1)
            g.tensor_tensor(small[:, col + 1:col + 2], small[:, col:col + 1], minus_half[:, 0:1],
                            ALU.pow).then_inc(N3["pw_" + what], 1)

        power("f", 0, 0)
        for t in range(NT + 2):
            if t + 1 < NT:
                power("f", t + 1, 0)
            if t < NT:
                power("k", t, 2)
                power("q", t, 4)
            if 0 <= t - 1 < NT:
                ln_rstd(7, t - 1)
        for k in range(2):
            low("wq", halves(wq, k), stage_o[:, k], 80 + k + 1)

    @block.tensor
    def _(pe):
        mm, tr = nc.tensor.matmul, nc.tensor.transpose

        def wq_split(load, k):
            pe.wait_ge(ld["wq_lo" if k < 2 else "wq_lo_v"], load * 2 + (k % 2 + 1))

        def ln_transpose(ln, n, free):
            s = LNS[ln]
            pe.wait_ge(s["xn"], ln_at(ln, n + 1))
            free()
            for k in range(KT):
                i = tr(psT[:, k * P:(k + 1) * P], xn[:, xn_slot(ln, n), k * P:(k + 1) * P], ident[:])
            i.then_inc(s["tr"], 1)

        def attention(a, next_ln):
            s, keys = A, a.keys

            def scores(u):
                pe.wait_ge(s["qT_lo"], u.c + 1)
                if a.kv_new(u):
                    pe.wait_ge(s["kT_lo"], a.kv_n(u) + 1)
                need(pe, s["exp"], u.c)
                n = u.res(NT)
                for b in range(2):
                    for hp in range(2):
                        at = ((b * 2 + hp) if a.index == 0 else (hp * 2 + b)) * keys
                        for i, (ql, kl) in enumerate(PASSES):
                            m = mm(psS[:, at:at + keys],
                                   qT[:, ql, b, 2 * hp:2 * hp + 2, :].rearrange("p h t -> p (h t)"),
                                   a.kT[:, u.res(a.ring), kl, b * keys:(b + 1) * keys], start=i == 0, stop=i == 2)
                m.then_inc(s["scores"], 1)

            def q_proj(st, first, last):
                n = st.res(NT)
                if first == 0:
                    need(pe, s["q_read"], st.c)
                for k in range(first, last):
                    if n == 0:
                        wq_split(st.div(NT) + a.wq0, k)
                    if st.static and st.t < NT and k == 0:
                        pe.wait_ge(LNS[2 * a.index]["lo"], ln_at(2 * a.index, n + 1))
                    for i, (xl, wl) in enumerate(PASSES):
                        m = mm(psQ[:], lat(xl, k, n), wq[:, wl, k, :],
                               start=k == 0 and i == 0, stop=k == KT - 1 and i == 2)
                    m.then_inc(s["wq_used"], 1)

            def kv_proj(st):
                if st.static and st.t == 0 and a.index == 1:
                    pe.wait_ge(setup["ctxT"], 8)
                need(pe, s["kT_lo"], a.kv_n(st))
                need(pe, s["v_lo"], a.kv_n(st))
                n = st.res(NT)
                if n == 0:
                    pe.wait_ge(ld["wkv_lo"], st.div(a.kv_period) * 2 + (a.wkv0 + 2))
                if st.static and a.index == 0 and st.t < NT:
                    pe.wait_ge(LNS[0]["lo"], ln_at(0, n + 1))
                    wq_split(0, 1)
                    wq_split(0, 3)
                    pe.wait_ge(ld["wo_lo"], 4)
                for b in range(2 if a.index == 0 else 1):
                    for k in range(KT):
                        for i, (xl, wl) in enumerate(PASSES):
                            lhsT = hidden(xl, k, n, b) if a.index == 0 else ctxT[:, xl, k, tok(n)]
                            m = mm(psKV[:, b * 256:(b + 1) * 256], lhsT, wkv_k(wl, k, 256),
                                   start=k == 0 and i == 0, stop=k == KT - 1 and i == 2)
                m.then_inc(s["kv"], 1)

            def q_transpose(st):
                pe.wait_ge(s["q_read"], st.c + 1)
                need(pe, s["qT_lo"], st.c)
                if st.static and st.t == 0:
                    pe.wait_ge(LNS[2 * a.index]["lo"], ln_at(2 * a.index, NT))
                if st.static and st.t - LN_SLOT >= 0:
                    pe.wait_ge(LNS[next_ln]["lo"], ln_at(next_ln, st.t - LN_SLOT + 1))
                for h in range(HQ):
                    i = tr(psT[:, h * P:(h + 1) * P], q_sb[:, h * P:(h + 1) * P], ident[:])
                i.then_inc(s["q_tr"], 1)

            def k_transpose(st):
                pe.wait_ge(s["k_read"], a.kv_n(st) + 1)
                pe.wait_ge(s["v_lo"], a.kv_n(st) + 1)
                for b in range(2 if a.index == 0 else 1):
                    i = tr(psKV[:, b * P:(b + 1) * P], k_sb[:, b * P:(b + 1) * P], ident[:])
                i.then_inc(s["k_tr"], 1)

            def p_transpose(u):
                pe.wait_ge(s["prob"], u.c + 1)
                need(pe, s["pT_lo"], u.c)
                for j in range(4 * keys // P):
                    i = tr(psP[:, j * P:(j + 1) * P], prob[:, j * P:(j + 1) * P], ident[:])
                i.then_inc(s["p_tr"], 1)

            def attend(u):
                pe.wait_ge(s["pT_lo"], u.c + 1)
                need(pe, s["oT_lo"], u.c)
                n = u.res(NT)
                for b in range(2):
                    for i, (vl, pl) in enumerate(PASSES):
                        if a.index == 0:
                            lhsT, rhs = a.v[:, n, vl, b * HD:(b + 1) * HD], pT[:, pl, b * 256:(b + 1) * 256]
                        else:
                            rows = slice(b * S, (b + 1) * S)
                            lhsT, rhs = a.v[rows, u.res(a.ring), vl, 0:HD], pT[rows, pl, 0:256]
                        m = mm(psO[:, b, 0:256], lhsT, rhs, start=i == 0, stop=i == 2)
                m.then_inc(s["pv"], 1)

            def out_proj(w, first, last):
                n = w.res(NT)
                if first == 0:
                    pe.wait_ge(s["oT_lo"], w.c + 1)
                    need(pe, s["x_add"], w.c)
                for h in range(first, last):
                    if n == 0:
                        pe.wait_ge(ld["wo_lo"], w.div(NT) * 4 + (a.wo0 + h + 1))
                    for i, (ol, wl) in enumerate(PASSES):
                        m = mm(psY[:], oT[:, ol, h, :], wo[:, wl, h, :],
                               start=h == 0 and i == 0, stop=h == HQ - 1 and i == 2)
                    m.then_inc(s["wo_used"], 1)

            for t in steps(pe, STEPS, a.unroll, LAG, a.done):
                t1, t2, t3 = t.back(1), t.back(2), t.back(3)
                if t.exists:
                    q_proj(t, 0, 2)
                if t2.exists:
                    p_transpose(t2)
                if t.exists:
                    q_proj(t, 2, 4)
                    if a.kv_new(t):
                        kv_proj(t)
                if t1.exists:
                    scores(t1)
                if t.static and t.t >= LN_SLOT:
                    n = t.t - LN_SLOT

                    def free():
                        pe.wait_ge(s["qT_lo"], min(t.c, a.done + STEPS))
                        need(pe, LNS[next_ln]["lo"], ln_at(next_ln, n))
                    ln_transpose(next_ln, n, free)
                if t2.exists:
                    attend(t2)
                if t3.exists:
                    out_proj(t3, 0, 4)
                if t.exists:
                    q_transpose(t)
                    if a.kv_new(t):
                        k_transpose(t)

        def ffn(f, next_ln):
            s, done = FS, f.done
            for t in range(NT + 3):
                if t < NT:
                    pe.wait_ge(LNS[f.ln]["lo"], ln_at(f.ln, t + 1))
                    need(pe, s["hid"], done + t)
                    if t == 0:
                        pe.wait_ge(ld["wkv_lo"], f.wkv_n)
                    for k in range(KT):
                        for i, (xl, wl) in enumerate(PASSES):
                            m = mm(psQ[:, 0:f.width], lat(xl, k, t), wkv_k(wl, k, f.width),
                                   start=k == 0 and i == 0, stop=k == KT - 1 and i == 2)
                    m.then_inc(s["gate_a"], 1)
                    if f.dense:
                        need(pe, s["x_add"], done + t - 2)
                        for k in range(KT):
                            if t == 0:
                                wq_split(WQ_DENSE[f.index], k)
                            for i, (xl, wl) in enumerate(PASSES):
                                m = mm(ring3(t)[:], lat(xl, k, t), wq[:, wl, k, :],
                                       start=k == 0 and i == 0, stop=False)
                        m.then_inc(s["dense"], 1)
                if 0 <= t - 1 < NT:
                    u = t - 1
                    pe.wait_ge(s["hid"], done + u + 1)
                    need(pe, s["hidT_lo"], done + u)
                    for j in range(f.parts):
                        i = tr(psP[0:f.rows, j * P:(j + 1) * P], s_sb[:, j * f.rows:(j + 1) * f.rows], ident[:])
                    i.then_inc(s["hid_tr"], 1)
                if 0 <= t - 2 < NT:
                    u = t - 2
                    pe.wait_ge(s["hidT_lo"], done + u + 1)
                    if u == 0:
                        pe.wait_ge(ld["wo_lo"], f.wo_n)
                    if not f.dense:
                        need(pe, s["x_add"], done + u - 2)
                    for j in range(f.parts):
                        for i, (hl, wl) in enumerate(PASSES):
                            m = mm(ring3(u)[:], hidT[0:f.rows, hl, j, :], wo[0:f.rows, wl, j, :],
                                   start=not f.dense and j == 0 and i == 0, stop=j == f.parts - 1 and i == 2)
                    m.then_inc(s["experts"], 1)
                if 0 <= t - 3 < NT and next_ln != 4:
                    ln_transpose(next_ln, t - 3, lambda: need(pe, LNS[next_ln]["lo"], ln_at(next_ln, t - 3)))

        def linear_attention(next_ln):
            s = M
            for t in range(NT + 3):
                if t < NT:
                    def free():
                        need(pe, s["q_shift"], t)
                        need(pe, LNS[next_ln]["lo"], ln_at(next_ln, t - 3))
                    ln_transpose(4, t, free)
                    pe.wait_ge(s["e"], t + 1)
                    need(pe, s["eT_lo"], t)
                    for k in range(KT):
                        i = tr(psS[:, k * P:(k + 1) * P], stage_q[:, t % 4, k * P:(k + 1) * P], ident[:])
                    i.then_inc(s["e_tr"], 1)
                if 0 <= t - 1 < NT:
                    u = t - 1
                    pe.wait_ge(s["q_soft"], u + 1)
                    need(pe, s["q2_lo"], u)
                    for k in range(KT):
                        i = tr(psP[:, k * P:(k + 1) * P], prob[:, k * P:(k + 1) * P], ident[:])
                    i.then_inc(s["q_tr"], 1)
                if t < NT:
                    pe.wait_ge(s["eT_lo"], t + 1)
                    need(pe, s["kvs"], t)
                    for k in range(KT):
                        for i, (el, cl) in enumerate(PASSES):
                            m = mm(psKV[:, 0:P], eT[:, el, k, :], ctxT[:, cl, k, tok(t)],
                                   start=k == 0 and i == 0, stop=k == KT - 1 and i == 2)
                    m.then_inc(s["kv"], 1)
                if 0 <= t - 1 < NT:
                    u = t - 1
                    pe.wait_ge(s["q2_lo"], u + 1)
                    pe.wait_ge(s["kvs_lo"], u + 1)
                    need(pe, s["x_add"], u)
                    for i, (kl, ql) in enumerate(PASSES):
                        m = mm(psY[:], kvs_r[:, u % 2, kl, :], q2[:, ql, :], start=i == 0, stop=i == 2)
                    m.then_inc(s["out"], 1)
                if 0 <= t - 3 < NT:
                    def free():
                        pe.wait_ge(s["q_shift"], min(t + 1, NT))
                        need(pe, LNS[next_ln]["lo"], ln_at(next_ln, t - 3))
                    ln_transpose(next_ln, t - 3, free)

        def add_bias(bank, what):
            r = bias_row[what]
            for i in range(2):
                m = mm(bank, ones_r[r:r + 1, :], pT[r:r + 1, i, :], start=False, stop=i == 1)
            return m

        def cross_attention(next_ln):
            s = N3

            def f_transpose(n):
                pe.wait_ge(s["f"], n + 1)
                need(pe, s["fT_lo"], n)
                for k in range(KT):
                    i = tr(psS[:, k * P:(k + 1) * P], stage_q[:, n % 4, k * P:(k + 1) * P], ident[:])
                i.then_inc(s["f_tr"], 1)

            f_transpose(0)
            for t in range(NT + 2):
                u = t - 1
                if 0 <= u < NT:
                    pe.wait_ge(s["qT_lo"], u + 1)
                    pe.wait_ge(s["kT_lo"], u + 1)
                    for k in range(KT):
                        for i, (ql, kl) in enumerate(PASSES):
                            m = mm(psO[:, 0, 0:P], qT3[:, ql, k, :], kT3[:, kl, k, :],
                                   start=k == 0 and i == 0, stop=k == KT - 1 and i == 2)
                    m.then_inc(s["scores"], 1)
                if t < NT:
                    pe.wait_ge(s["fT_lo"], t + 1)
                    if t == 0:
                        pe.wait_ge(ld["wo_lo"], 76)
                        pe.wait_ge(ld["vec_lo"], 1)
                    for k in range(KT):
                        for i, (xl, wl) in enumerate(PASSES):
                            mm(psKV[:], fT[:, xl, k, :], wo[:, wl, k, :], start=k == 0 and i == 0, stop=False)
                    add_bias(psKV[:], "k").then_inc(s["k"], 1)
                if 0 <= u < NT:
                    pe.wait_ge(s["prob"], u + 1)
                    tr(psO[:, 1, 0:P], s_sb[:, 0:P], ident[:]).then_inc(s["p_tr"], 1)
                if t < NT:
                    pe.wait_ge(LNS[6]["lo"], ln_at(6, t + 1))
                    for k in range(KT):
                        if t == 0:
                            wq_split(19, k)
                        for i, (xl, wl) in enumerate(PASSES):
                            mm(psQ[:], lat(xl, k, t), wq[:, wl, k, :], start=k == 0 and i == 0, stop=False)
                    add_bias(psQ[:], "q").then_inc(s["q"], 1)
                    pe.wait_ge(s["kn"], t + 1)
                    for k in range(KT):
                        i = tr(psP[:, k * P:(k + 1) * P], k3[:, k * P:(k + 1) * P], ident[:])
                    i.then_inc(s["k_tr"], 1)
                if 0 <= u < NT:
                    pe.wait_ge(s["pT_lo"], u + 1)
                    need(pe, s["x_add"], u)
                    for i, (pl, fl) in enumerate(PASSES):
                        m = mm(psY[:], pT3[:, pl, :], f_r[:, u % 2, fl, :], start=i == 0, stop=i == 2)
                    m.then_inc(s["attend"], 1)
                if t < NT:
                    pe.wait_ge(s["q_sb"], t + 1)
                    need(pe, LNS[next_ln]["lo"], ln_at(next_ln, min(t - 2, NT)))
                    need(pe, LNS[6]["lo"], ln_at(6, NT))
                    for k in range(KT):
                        i = tr(psT[:, k * P:(k + 1) * P], q_sb[:, k * P:(k + 1) * P], ident[:])
                    i.then_inc(s["q_tr"], 1)
                if t + 1 < NT:
                    f_transpose(t + 1)
                if 0 <= t - 2 < NT:
                    def free():
                        pe.wait_ge(s["qT_lo"], min(t + 1, NT))
                        need(pe, LNS[next_ln]["lo"], ln_at(next_ln, t - 2))
                    ln_transpose(next_ln, t - 2, free)

        def clustered(ln):
            s = C3
            pe.wait_ge(ld["wkv_lo"], 32)
            for t in range(NT + 1):
                if t < NT:
                    pe.wait_ge(LNS[ln]["lo"], ln_at(ln, t + 1))
                    need(pe, s["exp"], t)
                    for k in range(KT):
                        for i, (xl, wl) in enumerate(PASSES):
                            m = mm(psS[:, 0:64], lat(xl, k, t), wkv_k(wl, k, 64),
                                   start=k == 0 and i == 0, stop=k == KT - 1 and i == 2)
                    m.then_inc(s["sim"], 1)
                if t:
                    pe.wait_ge(s["hits"], t)
                    mm(psO[0:64, 0, 0:2], pick64(t - 1), ones[:, 0:2], start=t == 1,
                       stop=t == NT).then_inc(s["count"], 1)
            pe.wait_ge(s["sel"], 1)
            mm(psP[:], s_sb[0:64, 0:P], prob[0:64, :], start=True, stop=True).then_inc(s["rows"], 1)
            for t in range(NT):
                need(pe, s["masked"], t - 1)
                bank = (psQ, psY)[t % 2]
                for k in range(KT):
                    if t == 0:
                        wq_split(20, k)
                    for i, (xl, wl) in enumerate(PASSES):
                        mm(bank[:], lat(xl, k, t), wq[:, wl, k, :], start=k == 0 and i == 0, stop=False)
                add_bias(bank[:], "o").then_inc(s["dense"], 1)

        pe.wait_ge(setup["const"], 3)
        for n in range(NT):
            ln_transpose(0, n, lambda: need(pe, LNS[0]["lo"], ln_at(0, n)))
        attention(L0, 1)
        ffn(FF[0], 2)
        attention(L1, 3)
        ffn(FF[1], 4)
        linear_attention(5)
        ffn(FF[2], 6)
        cross_attention(7)
        clustered(7)

    @block.scalar
    def _(act):
        copy = lambda o, i: nc.scalar.activation(o, i, ACT.Copy)

        def ln_hi(ln, n):
            s = LNS[ln]
            act.wait_ge(s["tr"], ln_at(ln, n + 1))
            copy(lat_all(HI, n), slices(psT)).then_inc(s["hi"], 1)

        def high(what, dst, stage, in_count):
            act.wait_ge(ld[what + "_in"], in_count)
            copy(dst, stage).then_inc(ld[what + "_hi"], 1)

        def high_wq(load):
            for k in range(KT):
                high("wq", wq[:, HI, k], stage_q[:, k], (load + 1) * 16)

        def high_wo(load, n=KT):
            for k in range(n):
                high("wo", wo[:, HI, k], stage_o[:, k], (load + 1) * 16)

        def high_wkv(load, width=D):
            for k in range(2):
                high("wkv", wkv[:, HI, k, 0:width], stage_kv[:, k, 0:width], (load + 1) * 16)

        def attention(a, next_ln):
            s, keys = A, a.keys

            def squares(st):
                n = st.res(2)
                act.wait_ge(s["wq_used"], st.c * 4 + 4)
                for h in range(HQ):
                    i = nc.scalar.activation(junk_q[h], psQ[:, h * HD:(h + 1) * HD], ACT.Square,
                                             accum_out=ssq[:, n, h:h + 1])
                i.then_inc(s["squares"], 1)

            def exps(u):
                act.wait_ge(s["neg_max"], u.c + 1)
                need(act, s["p_tr"], u.c)
                need(act, s["rsums"], u.c)
                for j in range(4):
                    at = slice(j * keys, (j + 1) * keys)
                    if a.rms:
                        e = nc.scalar.activation(prob[:, at], s_sb[:, at], ACT.Exp,
                                                 bias=neg_mx[:, j:j + 1], scale=1.0, accum_out=sums[:, j:j + 1])
                    else:
                        e = nc.scalar.activation(prob[:, at], psS[:, at], ACT.Exp,
                                                 bias=neg_mx[:, j:j + 1], scale=a.scale,
                                                 accum_out=sums[:, j:j + 1])
                e.then_inc(s["exp"], 1)

            def q_read(st):
                act.wait_ge(s["wq_used"], st.c * 4 + 4)
                need(act, s["q_tr"], st.c)
                copy(q_sb[:], psQ[:]).then_inc(s["q_read"], 1)

            def qT_hi(st):
                act.wait_ge(s["q_tr"], st.c + 1)
                need(act, s["scores"], st.c)
                copy(qT[:, HI], heads(psT[:])).then_inc(s["qT_hi"], 1)

            def kT_hi(st):
                act.wait_ge(s["k_tr"], a.kv_n(st) + 1)
                src = k_sb[:, HD:2 * HD] if a.rms else psKV[:, 0:2 * keys]
                if a.rms:
                    act.wait_ge(s["k_scaled"], st.t + 1)
                copy(a.kT[:, st.res(a.ring), HI], src).then_inc(s["kT_hi"], 1)

            def kv_read(st):
                act.wait_ge(s["kv"], a.kv_n(st) + 1)
                need(act, s["k_tr"], a.kv_n(st))
                if a.rms:
                    need(act, s["ms"], st.t - 1)
                    nc.scalar.activation(junk_k, psKV[:, 0:HD], ACT.Square, accum_out=ssq[:, st.res(2), 4:5])
                    copy(a.v[:, st.res(a.ring), HI], psKV[:, HD:2 * HD]).then_inc(s["v_hi"], 1)
                    return
                kv = psKV[:].rearrange("p (b c) -> p b c", b=2)
                copy(k_sb[:].rearrange("p (b c) -> p b c", b=2), kv[:, :, 0:HD]).then_inc(s["k_read"], 1)
                copy(a.v[:, st.res(a.ring), HI].rearrange("p (b c) -> p b c", b=2), kv[:, :, HD:256]).then_inc(s["v_hi"], 1)

            def oT_hi(u):
                act.wait_ge(s["pv"], u.c + 1)
                need(act, s["wo_used"], u.c * 4)
                copy(oT[:, HI].rearrange("p h (b t) -> p b h t", b=2),
                     psO[:, :, 0:256].rearrange("p b (h t) -> p b h t", h=HQ)).then_inc(s["oT_hi"], 1)

            def pT_hi(u):
                act.wait_ge(s["p_tr"], u.c + 1)
                need(act, s["pv"], u.c)
                copy(pT[:, HI, 0:4 * keys], psP[:, 0:4 * keys]).then_inc(s["pT_hi"], 1)

            for t in steps(act, STEPS, a.unroll, LAG, a.done):
                t1, t2 = t.back(1), t.back(2)
                if t2.exists:
                    pT_hi(t2)
                if t.exists:
                    if a.rms:
                        squares(t)
                    else:
                        q_read(t)
                    if a.kv_new(t):
                        kv_read(t)
                    if t.res(8) == 7:
                        act.wait_ge(s["wq_used"], t.c * 4 + 4)
                        high_wq(t.div(8) + (11 if a.rms else 2))
                if t.static and t.t >= LN_SLOT:
                    ln_hi(next_ln, t.t - LN_SLOT)
                if t1.exists:
                    exps(t1)
                if t2.exists:
                    oT_hi(t2)
                if a.rms and t.res(8) == 7 and t.exists:
                    act.wait_ge(s["kv"], a.kv_n(t) + 1)
                    if t.static and t.t == STEPS - 1:
                        high_wkv(13, 144)
                    else:
                        high_wkv(t.div(8) + 6)
                if not a.rms and t.res(16) == 12 and t.exists:
                    act.wait_ge(s["kv"], t.div(16) * 8 + 8)
                    if t.static and t.t == 60:
                        high_wkv(4, 504)
                    else:
                        high_wkv(t.div(16) + 1)
                if t.res(8) == 2 and not (t.static and t.t >= STEPS):
                    need(act, s["wo_used"], t.div(8) * 32 + a.done * 4)
                    high_wo(t.div(8) + (10 if a.rms else 1))
                if t.exists:
                    if a.kv_new(t):
                        kT_hi(t)
                    qT_hi(t)

        for k in range(KT):
            high("wq", ctx_part(HI, k, 0), stage_q[:, k].rearrange("p (n b t) -> p n b t", n=4, b=2), 16)
        for n in range(4):
            ln_hi(0, n)
        for k in range(KT):
            high("wo", ctx_part(HI, k, 1), stage_o[:, k].rearrange("p (n b t) -> p n b t", n=4, b=2), 16)
        for n in range(4, NT):
            ln_hi(0, n)
        high_wkv(0)
        high_wq(1)
        attention(L0, 1)

        def high_b(f, load):
            for j in range(f.parts):
                high("wo", wo[0:f.rows, HI, j], stage_o[0:f.rows, j], (load + 1) * 16)

        def ffn(f, next_ln, after):
            s, done = FS, f.done
            for t in range(NT + 3):
                if t < NT:
                    act.wait_ge(s["shift"], done + t + 1)
                    if f.index == 1:
                        nc.scalar.activation(gate[:, 0:8], logits[:, 0:8], ACT.Exp, bias=small[:, 0:1], scale=1.0,
                                             accum_out=small[:, 1:2]).then_inc(s["exp"], 1)
                    else:
                        nc.scalar.activation(small[:, 1:2], small[:, 0:1], ACT.Exp).then_inc(s["exp"], 1)
                if 0 <= t - 1 < NT:
                    act.wait_ge(s["hid_tr"], done + t)
                    need(act, s["experts"], done + t - 1)
                    copy(hidT[0:f.rows, HI, 0:f.parts], psP[0:f.rows, 0:f.parts * P].rearrange(
                        "p (j t) -> p j t", t=P)).then_inc(s["hidT_hi"], 1)
                if 0 <= t - 3 < NT and next_ln != 4:
                    ln_hi(next_ln, t - 3)
                after(t)

        def after0(t):
            if t < 8:
                hl, k = t // 4, t % 4
                copy(ctxT[:, hl, k].rearrange("p (n b t) -> p n b t", n=NT, b=2),
                     hT[:, hl, k, :, 0:4:3, :].bitcast(f32)).then_inc(setup["ctxT"], 1)
            if t == 8:
                act.wait_ge(FS["gate_a"], NT)
                high_wkv(5)
                act.wait_ge(FS["dense"], NT)
                high_wq(10)

        def after1(t):
            if t == 8:
                act.wait_ge(FS["gate_a"], 2 * NT)
                high_wkv(14, 136)
                act.wait_ge(FS["dense"], 2 * NT)
                high_wq(19)
            if t == NT + 2:
                act.wait_ge(FS["experts"], 2 * NT)
                high_b(FF[2], 19)
                act.wait_ge(ld["vec_in"], 48)
                for r in bias_row.values():
                    i = copy(pT[r:r + 1, HI], wide[r:r + 1])
                i.then_inc(ld["vec_hi"], 1)
                copy(ones_r[:], ones[:]).then_inc(setup["ones_r"], 1)

        def after2(t):
            if t == 8:
                act.wait_ge(FS["gate_a"], 3 * NT)
            if t == NT + 2:
                act.wait_ge(FS["experts"], 3 * NT)
                high_wo(20)
                high_wkv(15, 128)

        def linear_attention(next_ln):
            s = M

            def e(n):
                act.wait_ge(s["k_max"], n + 1)
                nc.scalar.activation(stage_q[:, n % 4], stage_q[:, n % 4], ACT.Exp, bias=small[:, n % 2:n % 2 + 1],
                                     scale=1.0, accum_out=small[:, 2 + n % 2:3 + n % 2]).then_inc(s["e"], 1)

            e(0)
            for t in range(NT + 3):
                if t < NT:
                    act.wait_ge(s["e_tr"], t + 1)
                    need(act, s["kv"], t)
                    copy(eT[:, HI], slices(psS)).then_inc(s["eT_hi"], 1)
                    act.wait_ge(s["q_shift"], t + 1)
                    nc.scalar.activation(q_sb[:], q_sb[:], ACT.Exp).then_inc(s["q_exp"], 1)
                if 0 <= t - 1 < NT:
                    act.wait_ge(s["q_tr"], t)
                    need(act, s["out"], t - 1)
                    copy(q2[:, HI], psP[:]).then_inc(s["q2_hi"], 1)
                if t + 1 < NT:
                    e(t + 1)
                if t < NT:
                    act.wait_ge(s["kvs"], t + 1)
                    need(act, s["out"], t - 1)
                    copy(kvs_r[:, t % 2, HI], kvs).then_inc(s["kvs_hi"], 1)
                if 0 <= t - 3 < NT:
                    ln_hi(next_ln, t - 3)

        def cross_attention(next_ln):
            s = N3

            def f_squares(n):
                act.wait_ge(ld[f"c{n % 4}"], (n // 4 + 3) * 16)
                need(act, s["ms_f"], n)
                nc.scalar.activation(junk_f3, stage_q[:, n % 4], ACT.Square,
                                     accum_out=small[:, 6:7]).then_inc(s["f_sq"], 1)

            def f_hi(n):
                act.wait_ge(s["f"], n + 1)
                need(act, s["attend"], n - 1)
                copy(f_r[:, n % 2, HI], stage_q[:, n % 4]).then_inc(s["f_hi"], 1)

            def fT_hi(n):
                act.wait_ge(s["f_tr"], n + 1)
                need(act, s["k"], n)
                copy(fT[:, HI], slices(psS)).then_inc(s["fT_hi"], 1)

            f_squares(0)
            f_hi(0)
            fT_hi(0)
            for t in range(NT + 2):
                u = t - 1
                if t + 1 < NT:
                    f_squares(t + 1)
                if 0 <= u < NT:
                    act.wait_ge(s["neg_max"], u + 1)
                    for b in range(2):
                        rows = slice(b * S, (b + 1) * S)
                        i = nc.scalar.activation(s_sb[rows, b * S:(b + 1) * S], psO[rows, 0, b * S:(b + 1) * S], ACT.Exp,
                                                 bias=small[rows, 10:11], scale=small[rows, 9:10],
                                                 accum_out=small[rows, 11:12])
                    i.then_inc(s["exp"], 1)
                    act.wait_ge(s["p_tr"], u + 1)
                    need(act, s["attend"], u)
                    copy(pT3[:, HI], psO[:, 1, 0:P]).then_inc(s["pT_hi"], 1)
                if t < NT:
                    act.wait_ge(s["k"], t + 1)
                    need(act, s["ms_k"], t)
                    nc.scalar.activation(junk_k3, psKV[:], ACT.Square, accum_out=small[:, 7:8]).then_inc(s["k_sq"], 1)
                if t < NT:
                    act.wait_ge(s["q"], t + 1)
                    need(act, s["q_tr"], t)
                    copy(q_sb[:], psQ[:]).then_inc(s["q_sb"], 1)
                    need(act, s["ms_q"], t)
                    nc.scalar.activation(junk_q3, psQ[:], ACT.Square, accum_out=small[:, 8:9]).then_inc(s["q_sq"], 1)
                    act.wait_ge(s["kw"], t + 1)
                    copy(kT3[:, HI], slices(k3w)).then_inc(s["kT_hi"], 1)
                    act.wait_ge(s["q_tr"], t + 1)
                    copy(qT3[:, HI], slices(psT)).then_inc(s["qT_hi"], 1)
                if t + 1 < NT:
                    f_hi(t + 1)
                    fT_hi(t + 1)
                if 0 <= t - 2 < NT:
                    ln_hi(next_ln, t - 2)

        def clustered(ln):
            s = C3
            for k in range(KT):
                if k == 0:
                    act.wait_ge(N3["q"], NT)
                act.wait_ge(ld["wo_in"], 22 * 16)
                copy(wq[:, HI, k], stage_o[:, k]).then_inc(ld["wq_hi"], 1)
            for t in range(NT):
                act.wait_ge(s["neg_max"], t + 1)
                need(act, s["count"], t - 1)
                nc.scalar.activation(pick64(t), psS[:, 0:64], ACT.Exp, bias=small[:, 0:1], scale=10.0,
                                     accum_out=small[:, 1:2]).then_inc(s["exp"], 1)

        act.wait_ge(A["wo_used"], STEPS * 4)
        high_b(FF[0], 9)
        ffn(FF[0], 2, after0)
        attention(L1, 3)
        act.wait_ge(A["wo_used"], 2 * STEPS * 4)
        high_b(FF[1], 18)
        ffn(FF[1], 4, after1)
        linear_attention(5)
        ffn(FF[2], 6, after2)
        cross_attention(7)
        clustered(7)

    @block.vector
    def _(dve):
        V = nc.vector

        def sub_hi(dst_lo, src, dst_hi):
            return V.tensor_tensor(dst_lo, src, dst_hi.bitcast(f32), ALU.subtract)

        links = [0]

        def link(instruction):
            links[0] += 1
            instruction.then_inc(chain, 1)
            dve.wait_ge(chain, links[0])

        def low_wq(load, stage=stage_q):
            for k in range(2, KT):
                dve.wait_ge(ld["wq_hi"], load * 4 + (k + 1))
                sub_hi(wq[:, LO, k], stage[:, k], wq[:, HI, k]).then_inc(ld["wq_lo_v"], 1)

        def ln_stats(ln, n):
            s = LNS[ln]
            link(V.bn_stats(bn[:, n % 2], x[:, n]))
            link(V.bn_aggr(mv[:, n], bn[:, n % 2]))
            V.tensor_scalar(var_eps[:, n:n + 1], mv[:, n, 1:2], LN_EPS, None, ALU.add).then_inc(s["var"], 1)

        def ln_norm(ln, n):
            s = LNS[ln]
            dve.wait_ge(s["rstd"], ln_at(ln, n + 1))
            need(dve, s["tr"], ln_at(ln, n if ln in (4, 5) else n - 1))
            V.tensor_scalar(xn[:, xn_slot(ln, n)], x[:, n], mv[:, n, 0:1], rstd[:, n:n + 1], ALU.subtract,
                            ALU.mult).then_inc(s["xn"], 1)

        def ln_lo(ln, n):
            s = LNS[ln]
            dve.wait_ge(s["hi"], ln_at(ln, n + 1))
            sub_hi(lat_all(LO, n), slices(psT), lat_all(HI, n)).then_inc(s["lo"], 1)

        def attention(a, next_ln):
            s, keys = A, a.keys

            def blocks(t):
                return t[:, 0:4 * keys].rearrange("p (j c) -> p j c", j=4)

            def row_max(u):
                dve.wait_ge(s["scores"], u.c + 1)
                need(dve, s["exp"], u.c)
                src = psS
                if a.rms:
                    src = s_sb
                    V.scalar_tensor_tensor(blocks(s_sb), blocks(psS), a.scale, mask[:].unsqueeze(1).to_broadcast(
                        [P, 4, keys]), ALU.mult, ALU.add).then_inc(s["masked"], 1)
                    dve.wait_ge(s["masked"], u.t + 1)
                V.tensor_reduce(mx[:], blocks(src), AX.X, ALU.max).then_inc(s["max"], 1)
                dve.wait_ge(s["max"], u.c + 1)
                V.tensor_scalar(neg_mx[:], mx[:], -1.0 if a.rms else -a.scale, None, ALU.mult).then_inc(s["neg_max"], 1)

            def normalise(u):
                dve.wait_ge(s["exp"], u.c + 1)
                V.reciprocal(rsums[:], sums[:]).then_inc(s["rsums"], 1)
                dve.wait_ge(s["rsums"], u.c + 1)
                V.tensor_tensor(blocks(prob), blocks(prob), rsums[:].unsqueeze(2).to_broadcast([P, 4, keys]),
                                ALU.mult).then_inc(s["prob"], 1)

            def mean_squares(st):
                n = st.res(2)
                dve.wait_ge(s["squares"], st.t + 1)
                need(dve, s["rms"], st.t - 1)
                V.tensor_scalar(ms_eps[:, n], ssq[:, n], 1.0 / HD, RMS_EPS, ALU.mult,
                                ALU.add).then_inc(s["ms"], 1)

            def qk_normalise(st):
                n = st.res(2)
                dve.wait_ge(s["rms"], st.t + 1)
                need(dve, s["q_tr"], st.c)
                four = lambda t: t[:].rearrange("p (h c) -> p h c", h=HQ)
                V.tensor_tensor(four(q_sb), four(psQ), rms[:, n, 0:HQ].unsqueeze(2).to_broadcast([P, HQ, HD]),
                                ALU.mult).then_inc(s["q_read"], 1)
                need(dve, s["k_tr"], a.kv_n(st))
                V.tensor_scalar(k_sb[:, 0:HD], psKV[:, 0:HD], rms[:, n, 4:5], None, ALU.mult).then_inc(s["k_read"], 1)

            def k_scale(st):
                dve.wait_ge(s["k_tr"], a.kv_n(st) + 1)
                V.tensor_scalar(k_sb[:, HD:2 * HD], psKV[:, 0:HD], wqk[:, 2:3], None, ALU.mult).then_inc(s["k_scaled"], 1)

            def qT_lo(st):
                dve.wait_ge(s["qT_hi"], st.c + 1)
                sub_hi(qT[:, LO], heads(psT[:]), qT[:, HI]).then_inc(s["qT_lo"], 1)

            def kT_lo(st):
                dve.wait_ge(s["kT_hi"], a.kv_n(st) + 1)
                src = k_sb[:, HD:2 * HD] if a.rms else psKV[:, 0:2 * keys]
                sub_hi(a.kT[:, st.res(a.ring), LO], src, a.kT[:, st.res(a.ring), HI]).then_inc(s["kT_lo"], 1)

            def v_lo(st):
                dve.wait_ge(s["v_hi"], a.kv_n(st) + 1)
                if a.rms:
                    sub_hi(a.v[:, st.res(a.ring), LO], psKV[:, HD:2 * HD], a.v[:, st.res(a.ring), HI]).then_inc(s["v_lo"], 1)
                    return
                two = lambda ap: ap.rearrange("p (b c) -> p b c", b=2)
                sub_hi(two(a.v[:, st.res(a.ring), LO]), two(psKV[:])[:, :, HD:256],
                       two(a.v[:, st.res(a.ring), HI])).then_inc(s["v_lo"], 1)

            def x_add(w):
                n = w.res(NT)
                dve.wait_ge(s["wo_used"], w.c * 4 + 4)
                last = w.static and w.t >= STEPS - NT
                i = V.tensor_tensor(x[:, n], x[:, n], psY[:], ALU.add).then_inc(s["x_add"], 1)
                if last:
                    dve.wait_ge(s["x_add"], w.c + 1)
                    ln_stats(next_ln, n)

            def oT_lo(u):
                dve.wait_ge(s["oT_hi"], u.c + 1)
                out = oT[:, LO].rearrange("p h (b t) -> p b h t", b=2)
                hi = oT[:, HI].rearrange("p h (b t) -> p b h t", b=2)
                sub_hi(out, psO[:, :, 0:256].rearrange("p b (h t) -> p b h t", h=HQ), hi).then_inc(s["oT_lo"], 1)

            def pT_lo(u):
                dve.wait_ge(s["pT_hi"], u.c + 1)
                sub_hi(pT[:, LO, 0:4 * keys], psP[:, 0:4 * keys], pT[:, HI, 0:4 * keys]).then_inc(s["pT_lo"], 1)

            for t in steps(dve, STEPS, a.unroll, LAG, a.done):
                t1, t2, t3 = t.back(1), t.back(2), t.back(3)
                tail = t.static and t.t >= LN_SLOT
                if t2.exists:
                    pT_lo(t2)
                if t.exists and a.kv_new(t):
                    v_lo(t)
                if t.exists and a.rms:
                    mean_squares(t)
                if tail:
                    ln_norm(next_ln, t.t - LN_SLOT)
                if t1.exists:
                    row_max(t1)
                if tail:
                    ln_lo(next_ln, t.t - LN_SLOT)
                if t.exists and a.rms:
                    qk_normalise(t)
                if t.exists and t.res(8) == 7:
                    low_wq(t.div(8) + (11 if a.rms else 2))
                if t1.exists:
                    normalise(t1)
                if t3.exists:
                    x_add(t3)
                if t2.exists:
                    oT_lo(t2)
                if t.exists:
                    if a.kv_new(t):
                        if a.rms:
                            k_scale(t)
                        kT_lo(t)
                    qT_lo(t)

        def ffn(f, next_ln):
            s, done, E, R = FS, f.done, f.E, f.R

            def gates(t):
                dve.wait_ge(s["gate_a"], done + t + 1)
                link(V.tensor_copy(logits[:, 0:E], psQ[:, 0:E]))
                if f.index == 1:
                    link(V.max(top[:], logits[:, 0:E]))
                    V.tensor_scalar(small[:, 0:1], top[:, 0:1], -1.0, None, ALU.mult).then_inc(s["shift"], 1)
                    dve.wait_ge(s["exp"], done + t + 1)
                    link(V.reciprocal(small[:, 2:3], small[:, 1:2]))
                    link(V.tensor_scalar(logits[:, 0:E], gate[:, 0:E], small[:, 2:3], None, ALU.mult))
                wide_e = max(E, 8)
                link(V.max(top[:], logits[:, 0:wide_e]))
                if f.index != 1:
                    V.tensor_tensor(small[:, 0:1], top[:, 1:2], top[:, 0:1], ALU.subtract).then_inc(s["shift"], 1)
                link(V.max_index(top_at[:], top[:], logits[:, 0:wide_e]))
                link(V.tensor_copy(top_f[:], top_at[:, 0:2]))
                if f.index == 1:
                    first, second = top[:, 0:1], top[:, 1:2]
                    link(V.tensor_tensor(small[:, 2:3], first, second, ALU.add))
                else:
                    first, second = ones[:, 0:1], small[:, 1:2]
                    dve.wait_ge(s["exp"], done + t + 1)
                    link(V.tensor_scalar(small[:, 2:3], second, 1.0, None, ALU.add))
                link(V.reciprocal(small[:, 3:4], small[:, 2:3]))
                for c, share in enumerate((first, second)):
                    link(V.tensor_tensor(small[:, 4 + c:5 + c], share, small[:, 3:4], ALU.mult))
                for c in range(2):
                    link(V.tensor_scalar(pick[:, c, 0:E], iota[:, 0:E], top_f[:, c:c + 1], small[:, 4 + c:5 + c],
                                         ALU.is_equal, ALU.mult))
                link(V.tensor_tensor(gate[:, 0:E], pick[:, 0, 0:E], pick[:, 1, 0:E], ALU.add))

            def hid(t):
                need(dve, s["hid_tr"], done + t)
                by_expert = lambda ap: ap.rearrange("p (e r) -> p e r", e=E)
                V.scalar_tensor_tensor(by_expert(s_sb[:, 0:E * R]), by_expert(psQ[:, E:f.width]), f.scale,
                                       gate[:, 0:E].unsqueeze(2).to_broadcast([P, E, R]), ALU.mult,
                                       ALU.mult).then_inc(s["hid"], 1)

            if f.index == 0:
                dve.wait_ge(setup["iota"], 2)
                dve.wait_ge(setup["ones"], 1)
            if E < 8:
                link(V.memset(logits[:, E:8], -3e38))
            for t in range(NT + 3):
                if 0 <= t - 3 < NT and next_ln != 4:
                    ln_norm(next_ln, t - 3)
                if t < NT:
                    gates(t)
                    hid(t)
                if 0 <= t - 1 < NT:
                    dve.wait_ge(s["hidT_hi"], done + t)
                    sub_hi(hidT[0:f.rows, LO, 0:f.parts],
                           psP[0:f.rows, 0:f.parts * P].rearrange("p (j t) -> p j t", t=P),
                           hidT[0:f.rows, HI, 0:f.parts]).then_inc(s["hidT_lo"], 1)
                if 0 <= t - 2 < NT:
                    u = t - 2
                    dve.wait_ge(s["experts"], done + u + 1)
                    V.tensor_tensor(x[:, u], x[:, u], ring3(u)[:], ALU.add).then_inc(s["x_add"], 1)
                    dve.wait_ge(s["x_add"], done + u + 1)
                    ln_stats(next_ln, u)
                if 0 <= t - 3 < NT and next_ln != 4:
                    ln_lo(next_ln, t - 3)
                if f.dense and t == 8:
                    low_wq(WQ_DENSE[f.index] + 1)

        def linear_attention(next_ln):
            s = M
            by8 = lambda ap: ap.rearrange("p (g e) -> p g e", e=8)
            group = k_sb[:, 0:S]

            def k_max(n):
                dve.wait_ge(ld[f"c{n % 4}"], (n // 4 + 1) * 16)
                link(V.tensor_reduce(mx[:, 0:1], stage_q[:, n % 4], AX.X, ALU.max))
                V.tensor_scalar(small[:, n % 2:n % 2 + 1], mx[:, 0:1], -1.0, None, ALU.mult).then_inc(s["k_max"], 1)

            dve.wait_ge(ld["vec_hi"], 1)
            for r in bias_row.values():
                i = sub_hi(pT[r:r + 1, LO], wide[r:r + 1], pT[r:r + 1, HI])
            i.then_inc(ld["vec_lo"], 1)
            k_max(0)
            ln_norm(4, 0)
            dve.wait_ge(setup["b8"], 3)
            for t in range(NT + 4):
                u = t - 1
                if t < NT:
                    dve.wait_ge(LNS[4]["tr"], ln_at(4, t + 1))
                    link(V.tensor_reduce(group, by8(psT[:]), AX.X, ALU.max))
                    V.tensor_tensor(by8(q_sb[:]), by8(psT[:]), group.unsqueeze(2).to_broadcast([P, S, 8]),
                                    ALU.subtract).then_inc(s["q_shift"], 1)
                    dve.wait_ge(s["eT_hi"], t + 1)
                    sub_hi(eT[:, LO], slices(psS), eT[:, HI]).then_inc(s["eT_lo"], 1)
                if 0 <= u < NT:
                    dve.wait_ge(s["q2_hi"], u + 1)
                    sub_hi(q2[:, LO], psP[:], q2[:, HI]).then_inc(s["q2_lo"], 1)
                if t + 1 < NT:
                    k_max(t + 1)
                    ln_norm(4, t + 1)
                if t < NT:
                    dve.wait_ge(s["q_exp"], t + 1)
                    link(V.tensor_reduce(group, by8(q_sb[:]), AX.X, ALU.add))
                    link(V.reciprocal(group, group))
                    need(dve, s["q_tr"], t)
                    V.tensor_tensor(by8(prob[:]), by8(q_sb[:]), group.unsqueeze(2).to_broadcast([P, S, 8]),
                                    ALU.mult).then_inc(s["q_soft"], 1)
                    dve.wait_ge(s["kv"], t + 1)
                    link(V.reciprocal(small[:, 4:5], small[:, 2 + t % 2:3 + t % 2]))
                    V.scalar_tensor_tensor(kvs, psKV[:, 0:P], small[:, 4:5], block8[:], ALU.mult,
                                           ALU.mult).then_inc(s["kvs"], 1)
                    dve.wait_ge(s["kvs_hi"], t + 1)
                    sub_hi(kvs_r[:, t % 2, LO], kvs, kvs_r[:, t % 2, HI]).then_inc(s["kvs_lo"], 1)
                if 0 <= u < NT:
                    dve.wait_ge(s["out"], u + 1)
                    V.tensor_tensor(x[:, u], x[:, u], psY[:], ALU.add).then_inc(s["x_add"], 1)
                    dve.wait_ge(s["x_add"], u + 1)
                    ln_stats(next_ln, u)
                if 0 <= t - 3 < NT:
                    ln_norm(next_ln, t - 3)
                    ln_lo(next_ln, t - 3)

        def cross_attention(next_ln):
            s = N3
            col = lambda c: small[:, c:c + 1]

            def mean_square(what, n, src, dst):
                dve.wait_ge(s[what + "_sq"], n + 1)
                V.tensor_scalar(col(dst), col(src), 1.0 / D, RMS_EPS3, ALU.mult, ALU.add).then_inc(s["ms_" + what], 1)

            def features(n):
                dve.wait_ge(s["pw_f"], n + 1)
                V.scalar_tensor_tensor(stage_q[:, n % 4], stage_q[:, n % 4], col(1), wide[:], ALU.mult,
                                       ALU.mult).then_inc(s["f"], 1)

            def f_lo(n):
                dve.wait_ge(s["f_hi"], n + 1)
                sub_hi(f_r[:, n % 2, LO], stage_q[:, n % 4], f_r[:, n % 2, HI]).then_inc(s["f_lo"], 1)

            def fT_lo(n):
                dve.wait_ge(s["fT_hi"], n + 1)
                sub_hi(fT[:, LO], slices(psS), fT[:, HI]).then_inc(s["fT_lo"], 1)

            link(V.memset(s_sb[:, 0:P], 0.0))
            dve.wait_ge(ld["fn_in"], 16)
            mean_square("f", 0, 6, 0)
            features(0)
            f_lo(0)
            fT_lo(0)
            for t in range(NT + 2):
                u = t - 1
                if t + 1 < NT:
                    mean_square("f", t + 1, 6, 0)
                if 0 <= u < NT:
                    dve.wait_ge(s["scores"], u + 1)
                    for b in range(2):
                        rows = slice(b * S, (b + 1) * S)
                        i = V.tensor_reduce(mx[rows, 0:1], psO[rows, 0, rows], AX.X, ALU.max)
                    link(i)
                    V.tensor_scalar(col(10), mx[:, 0:1], col(9), -1.0, ALU.mult, ALU.mult).then_inc(s["neg_max"], 1)
                if t + 1 < NT:
                    features(t + 1)
                if 0 <= u < NT:
                    dve.wait_ge(s["exp"], u + 1)
                    link(V.reciprocal(col(12), col(11)))
                    V.tensor_scalar(s_sb[:, 0:P], s_sb[:, 0:P], col(12), None, ALU.mult).then_inc(s["prob"], 1)
                if t < NT:
                    mean_square("k", t, 7, 2)
                if t < NT:
                    dve.wait_ge(s["pw_k"], t + 1)
                    V.tensor_scalar(k3[:], psKV[:], col(3), None, ALU.mult).then_inc(s["kn"], 1)
                if 0 <= u < NT:
                    dve.wait_ge(s["pT_hi"], u + 1)
                    sub_hi(pT3[:, LO], psO[:, 1, 0:P], pT3[:, HI]).then_inc(s["pT_lo"], 1)
                if t < NT:
                    mean_square("q", t, 8, 4)
                    dve.wait_ge(s["k_tr"], t + 1)
                    V.tensor_tensor(slices(k3w), slices(psP), wqk3[:, 2].unsqueeze(2).to_broadcast([P, KT, P]),
                                    ALU.mult).then_inc(s["kw"], 1)
                    dve.wait_ge(s["kT_hi"], t + 1)
                    sub_hi(kT3[:, LO], slices(k3w), kT3[:, HI]).then_inc(s["kT_lo"], 1)
                    dve.wait_ge(s["qT_hi"], t + 1)
                    sub_hi(qT3[:, LO], slices(psT), qT3[:, HI]).then_inc(s["qT_lo"], 1)
                    dve.wait_ge(s["pw_q"], t + 1)
                    link(V.tensor_scalar(col(9), col(5), D ** -0.5, None, ALU.mult))
                if 0 <= u < NT:
                    dve.wait_ge(s["attend"], u + 1)
                    V.tensor_tensor(x[:, u], x[:, u], psY[:], ALU.add).then_inc(s["x_add"], 1)
                    dve.wait_ge(s["x_add"], u + 1)
                    ln_stats(next_ln, u)
                if t + 1 < NT:
                    f_lo(t + 1)
                    fT_lo(t + 1)
                if 0 <= t - 2 < NT:
                    ln_norm(next_ln, t - 2)
                    ln_lo(next_ln, t - 2)

        def clustered(ln):
            s = C3
            low_wq(20, stage_o)
            for t in range(NT):
                dve.wait_ge(s["sim"], t + 1)
                link(V.tensor_reduce(mx[:, 0:1], psS[:, 0:64], AX.X, ALU.max))
                V.tensor_scalar(small[:, 0:1], mx[:, 0:1], -1.0 / TEMPERATURE, None, ALU.mult).then_inc(s["neg_max"], 1)
                dve.wait_ge(s["exp"], t + 1)
                link(V.reciprocal(small[:, 2:3], small[:, 1:2]))
                V.tensor_scalar(pick64(t), pick64(t), small[:, 2:3], THRESHOLD, ALU.mult,
                                ALU.is_gt).then_inc(s["hits"], 1)
                dve.wait_ge(s["hits"], t + 1)
                link(V.tensor_reduce(q_any[:, t:t + 1], pick64(t), AX.X, ALU.max))
            dve.wait_ge(s["count"], NT)
            link(V.tensor_scalar(small[0:64, 3:4], psO[0:64, 0, 0:1], 0.5, None, ALU.is_ge))
            V.tensor_scalar(s_sb[0:64, 0:P], ones[0:64, :], small[0:64, 3:4], None, ALU.mult)
            dve.wait_ge(ld["asg_in"], 16)
            V.tensor_scalar(prob[0:64], q_sb[0:64].bitcast(i32), row_id[0:64], None, ALU.is_equal).then_inc(s["sel"], 1)
            dve.wait_ge(s["rows"], 1)
            link(V.tensor_copy(wide[:], psP[:]))
            for t in range(NT):
                dve.wait_ge(s["dense"], t + 1)
                need(dve, s["out"], t - 1)
                bank, kept = ((psQ, xn[:, 1]), (psY, prob[:]))[t % 2]
                V.scalar_tensor_tensor(kept, bank[:], q_any[:, t:t + 1], wide[:], ALU.mult,
                                       ALU.mult).then_inc(s["masked"], 1)
                dve.wait_ge(s["masked"], t + 1)
                V.tensor_tensor(x[:, t], x[:, t], kept, ALU.add).then_inc(s["out"], 1)

        for n in range(NT):
            dve.wait_ge(ld[f"x{n}"], 16)
            ln_stats(0, n)
        dve.wait_ge(ld["small"], 96)
        V.tensor_tensor(wqk[:, 2:3], wqk[:, 0:1], wqk[:, 1:2], ALU.mult)
        link(V.tensor_tensor(wqk3[:, 2], wqk3[:, 0], wqk3[:, 1], ALU.mult))
        for k in range(2, KT):
            dve.wait_ge(ld["wq_hi"], k + 1)
            sub_hi(ctx_part(LO, k, 0), stage_q[:, k].rearrange("p (n b t) -> p n b t", n=4, b=2),
                   ctx_part(HI, k, 0)).then_inc(ld["wq_lo_v"], 1)
        for n in range(NT):
            ln_norm(0, n)
            if n:
                ln_lo(0, n - 1)
        ln_lo(0, NT - 1)
        low_wq(1)
        attention(L0, 1)
        ffn(FF[0], 2)
        attention(L1, 3)
        ffn(FF[1], 4)
        linear_attention(5)
        ffn(FF[2], 6)
        cross_attention(7)
        clustered(7)

    block_cm.__exit__(None, None, None)


def arrays_of(inputs):
    import numpy as np
    f = {k: np.asarray(a) for k, a in inputs.items()}
    c = np.ascontiguousarray

    def by_slice(w):
        return c(w.reshape(KT, P, -1).transpose(1, 0, 2))

    def head_groups(w):
        return c(w.reshape(KT, P, NHG, D).transpose(2, 1, 0, 3))

    def out_groups(w):
        return c(w.reshape(NHG, HQ, P, D).transpose(0, 2, 1, 3))

    def kv_groups(wk, wv, n):
        both = np.concatenate([wk.reshape(KT, P, n, HD), wv.reshape(KT, P, n, HD)], axis=3)
        return c(both.transpose(2, 1, 0, 3).reshape(n, P, 2, 512))

    a = {}
    a["x"] = c(f["x"].reshape(NT, P, D).transpose(1, 0, 2))
    a["ctxT"] = c(f["ctx_4096"].reshape(2, 512, KT, P).transpose(0, 3, 2, 1))
    a["wq0"] = head_groups(f["L0_xattn_Wq"])
    a["wo0"] = out_groups(f["L0_xattn_Wo"])
    a["wkv0"] = kv_groups(f["L0_xattn_Wk"], f["L0_xattn_Wv"], 4)
    a["wq1"] = head_groups(f["L1_xattn_Wq"].T)
    a["wo1"] = out_groups(f["L1_xattn_Wo"].T)
    a["wkv1"] = kv_groups(f["L1_xattn_Wk"].T, f["L1_xattn_Wv"].T, NHG)
    a["mask"] = c(f["mask_1x1xSxS2_ff0"].reshape(S, S))

    def two_slices(w):
        return c(w.reshape(2, 2, P, -1).transpose(2, 0, 1, 3).reshape(P, 2, -1))

    def gate_a(gate, lora_a):
        return two_slices(np.concatenate([gate, lora_a.reshape(-1, D)]).T)

    def ranks(lora_b):
        return lora_b.transpose(0, 2, 1).reshape(-1, D)

    a["ga0"] = gate_a(f["L0_ffn_gate_W"], f["L0_ffn_lora_A"])
    a["ga1"] = gate_a(f["L1_ffn_gate_W"], f["L1_ffn_A"])
    a["ga2"] = gate_a(f["L2_ffn_router_w"], f["L2_ffn_A"])
    a["cent"] = two_slices(f["L3_ffn_centroids"].T)
    a["base0"], a["base1"] = by_slice(f["L0_ffn_base_W"].T), by_slice(f["L1_ffn_W_base"].T)
    a["wq3"], a["wk3"] = by_slice(f["L3_xattn_Wq_w"].T), by_slice(f["L3_xattn_Wk_w"].T)
    a["w3"] = by_slice(f["L3_ffn_weight"].T)
    a["b0"] = c(ranks(f["L0_ffn_lora_B"]).reshape(2, 112, D).transpose(1, 0, 2))
    a["b1"], a["b2"] = (c(ranks(f[n])[:, None]) for n in ("L1_ffn_B", "L2_ffn_B"))
    a["ctx"] = c(f["ctx_4096"].reshape(NT, P, D).transpose(1, 0, 2))
    a["qn1"], a["kn1"] = f["L1_xattn_q_norm_w"].reshape(P, 1), f["L1_xattn_k_norm_w"].reshape(P, 1)
    a["qn3"], a["kn3"] = (c(f[n].reshape(KT, P).T) for n in ("L3_xattn_qn_w", "L3_xattn_kn_w"))
    for name, n in (("bq3", "L3_xattn_Wq_b"), ("bk3", "L3_xattn_Wk_b"), ("bias3", "L3_ffn_bias"),
                    ("fn_w", "L3_xattn_fn_w"), ("asg", "L3_ffn_assignments")):
        a[name] = f[n].reshape(1, D)
    return a


def kernel(**inputs):
    import concourse.bacc as bacc
    from concourse.bass_utils import run_bass_kernel_spmd

    nc = bacc.Bacc("TRN2", target_bir_lowering=False, num_devices=1)
    arrays, io = {}, {}
    for name, a in arrays_of(inputs).items():
        arrays["in_" + name] = a
        io[name] = nc.dram_tensor("in_" + name, a.shape, mybir.dt.from_np(a.dtype), kind="ExternalInput").ap()
    io["out"] = nc.dram_tensor("out", (P, NT, D), mybir.dt.float32, kind="ExternalOutput").ap()
    build(nc, io)
    got = run_bass_kernel_spmd(nc, [arrays], core_ids=[0]).results[0]["out"]
    return got.transpose(1, 0, 2).reshape(B, S, D)
```

```python
import concourse.bass as bass
from concourse import mybir


P = 128
B, S, D = 16, 64, 512
TOK = B * S
NT = TOK // P
KT = D // P
HD = 128
HQ = 4
NHG = 32 // HQ
STEPS = NHG * NT
TEMPERATURE, THRESHOLD = 0.1, 0.01
LAG = 4
LN_SLOT = STEPS - 4
LN_EPS = 1e-5
RMS_EPS, RMS_EPS3 = 1e-5, 1e-6
HI, LO = 0, 1
PASSES = ((HI, HI), (HI, LO), (LO, HI))


class Step:

    def __init__(self, base, n, i=None, unroll=0, done=0):
        self.base, self.n, self.i, self.unroll = base, n, i, unroll
        self.done = done

    @property
    def c(self):
        at = self.base + self.done
        return at if self.i is None else self.i * self.unroll + at

    @property
    def t(self):
        return self.base if self.i is None else self.i * self.unroll + self.base

    @property
    def exists(self):
        return self.i is not None or 0 <= self.base < self.n

    @property
    def static(self):
        return self.i is None

    def back(self, k):
        return Step(self.base - k, self.n, self.i, self.unroll, self.done)

    def res(self, m):
        return self.base % m

    def div(self, m):
        q = self.base // m
        return q if self.i is None else self.i * (self.unroll // m) + q


def steps(eng, n, unroll, lag, done):
    loops = (n - lag - NT) // unroll
    if loops < 2:
        loops = 0
    for t in range(lag):
        yield Step(t, n, done=done)
    if loops:
        with eng.Fori(0, loops) as i:
            for t in range(lag, lag + unroll):
                yield Step(t, n, i, unroll, done)
    for t in range(lag + loops * unroll, n + lag):
        yield Step(t, n, done=done)


def need(eng, sem, value):
    if isinstance(value, int) and value <= 0:
        return
    eng.wait_ge(sem, value)


class Sems:

    def __init__(self, nc, layer):
        self._nc, self._layer, self._of = nc, layer, {}

    def __getitem__(self, what):
        if what not in self._of:
            self._of[what] = self._nc.alloc_semaphore(f"{self._layer}_{what}")
        return self._of[what]


def build(nc, io):
    f32, f32r, i32, u32 = mybir.dt.float32, mybir.dt.float32r, mybir.dt.int32, mybir.dt.uint32
    ALU, ACT, AX = mybir.AluOpType, mybir.ActivationFunctionType, mybir.AxisListType
    sb = lambda name, shape, dt=f32: nc.alloc_sbuf_tensor(name, [P, *shape], dt)
    ps = lambda name, shape: nc.alloc_psum_tensor(name, [P, *shape], f32)

    x = sb("x_res", [NT, D])
    hT = sb("hT", [2, KT, NT, 4, S], f32r)
    wq = sb("wq", [2, KT, D], f32r)
    wo = sb("wo", [2, KT, D], f32r)
    wkv = sb("wkv", [2, 2, D], f32r)
    stage_q = sb("stage_q", [KT, D])
    stage_o = sb("stage_o", [KT, D])
    stage_kv = sb("stage_kv", [2, D])
    arena = sb("arena", [8192], f32r)
    half = lambda n: arena[:, n * 4096:(n + 1) * 4096].rearrange("p (n h c) -> p n h c", n=NT, h=2)
    kT0, v0 = half(0), half(1)
    ctxT = arena[:].rearrange("p (h k t) -> p h k t", h=2, k=KT)
    kT1 = sb("kT1", [4, 2, HD], f32r)
    v1 = sb("v1", [4, 2, HD], f32r)
    q_sb = sb("q_sb", [D])
    k_sb = sb("k_sb", [2 * HD])
    qT = sb("qT", [2, 2, HQ, S], f32r)
    s_sb = sb("s_sb", [2 * P])
    prob = sb("prob", [D])
    pT = sb("pT", [2, D], f32r)
    oT = sb("oT", [2, HQ, P], f32r)
    xn = sb("xn", [2, D])
    ident = sb("ident", [P])
    minus_half = sb("minus_half", [8])
    bn = sb("bn", [2, 6])
    mv = sb("mv", [NT, 2])
    var_eps = sb("var_eps", [NT])
    rstd = sb("rstd", [NT])
    mx = sb("mx", [4])
    neg_mx = sb("neg_mx", [4])
    sums = sb("sums", [4])
    rsums = sb("rsums", [4])
    ssq = sb("ssq", [2, 5])
    ms_eps = sb("ms_eps", [2, 5])
    rms = sb("rms", [2, 5])
    mask = sb("mask", [S])
    wqk = sb("wqk", [3])
    wqk3 = sb("wqk3", [3, KT])
    wide = sb("wide", [D])
    ones = sb("ones", [P])
    ones_r = sb("ones_r", [P], f32r)
    iota = sb("iota", [32])
    row_id = sb("row_id", [1])
    block8 = sb("block8", [P])
    logits = sb("logits", [32])
    top = sb("top", [8])
    top_at = sb("top_at", [8], u32)
    top_f = sb("top_f", [2])
    pick = sb("pick", [2, 32])
    gate = sb("gate", [32])
    small = sb("small", [16])
    q_any = sb("q_any", [NT])

    psQ, psKV, psT, psS, psP, psY = (ps(n, [D]) for n in ("psQ", "psKV", "psT", "psS", "psP", "psY"))
    psO = ps("psO", [2, D])

    setup = Sems(nc, "setup")
    ld = Sems(nc, "ld")
    A = Sems(nc, "attn")
    ln_even, ln_odd = Sems(nc, "ln_even"), Sems(nc, "ln_odd")
    LNS = [ln_even, ln_odd, ln_even, ln_odd, Sems(nc, "ln_l2"), ln_odd, ln_even, ln_odd]
    out_done = nc.alloc_semaphore("out_done")

    FS = Sems(nc, "ffn")
    M, N3, C3 = Sems(nc, "m2"), Sems(nc, "a3"), Sems(nc, "c3")
    chain = nc.alloc_semaphore("dve_chain")

    def ln_at(ln, n):
        return sum(other is LNS[ln] for other in LNS[:ln]) * NT + n

    class Ffn:

        def __init__(self, index, ln, E, R, dense, scale, wkv_n, wo_n):
            self.index, self.ln, self.E, self.R = index, ln, E, R
            self.done = index * NT
            self.dense, self.scale = dense, scale
            self.width = E + E * R
            self.parts = 2 if E * R > P else 1
            self.rows = E * R // self.parts
            self.wkv_n, self.wo_n = wkv_n, wo_n

    FF = [Ffn(0, 1, 28, 8, True, 2.0, 10, 34), Ffn(1, 3, 8, 8, True, 2.0, 28, 67), Ffn(2, 5, 4, 16, False, 4.0, 30, 68)]
    WQ_DENSE = [8, 17]

    class Attn:
        def __init__(self, index):
            self.index = index
            self.done, self.kv_done = (0, 0) if index == 0 else (STEPS, STEPS // 2)
            self.rms = index == 1
            self.keys = 2 * S if index == 0 else S
            self.unroll = 2 * NT if index == 0 else NT
            self.kv_period = self.unroll
            self.kT, self.v, self.ring = (kT0, v0, NT) if index == 0 else (kT1, v1, 4)
            self.wq0, self.wo0, self.wkv0 = (0, 0, 0) if index == 0 else (9, 34, 10)

        def kv_new(self, st):
            return st.exists and st.res(self.kv_period) < NT

        def kv_n(self, st):
            return st.div(self.kv_period) * NT + (st.res(NT) + self.kv_done)

        scale = HD ** -0.5

    L0, L1 = Attn(0), Attn(1)

    def heads(ap):
        return ap.rearrange("p (h b t) -> p b h t", h=HQ, b=2)

    def tok(n):
        return slice(n * P, (n + 1) * P)

    def lat(hl, k, n):
        return hT[:, hl, k, n, 1:3].rearrange("p b t -> p (b t)")

    def lat_all(hl, n):
        return hT[:, hl, :, n, 1:3].rearrange("p k b t -> p k (b t)")

    def slices(bank):
        return bank[:].rearrange("p (k t) -> p k t", k=KT)

    def hidden(hl, k, n, b):
        return hT[:, hl, k, n, 2 * b:2 * b + 2].rearrange("p b t -> p (b t)")

    def ctx_part(hl, k, half):
        return hT[:, hl, k, half * 4:half * 4 + 4, 0:4:3, :]

    def xn_slot(ln, n):
        return {4: 0, 5: 1}.get(ln, n % 2)

    def ln_bank(ln, n):
        return (psT, psY)[n % 2] if ln == 0 else psQ if ln == 5 else psT

    def ring3(n):
        return (psY, psS, psKV)[n % 3]

    eT, q2, kvs_r = (kT1[:].rearrange("p a h c -> p (a h c)").rearrange("p (h k c) -> p h k c", h=2, k=KT),
                     qT[:].rearrange("p h b g t -> p h (b g t)"),
                     v1[:].rearrange("p a h c -> p (a h c)").rearrange("p (a h c) -> p a h c", a=4, h=2))
    hidT = oT
    def cut(at, *shape):
        size, names = 1, "abc"[:len(shape)]
        for x_ in shape:
            size *= x_
        v_ = arena[:, at:at + size]
        return v_.rearrange(f"p ({' '.join(names)}) -> p {' '.join(names)}", **dict(zip(names, shape)))
    f_r, fT, kT3, qT3, pT3 = cut(0, 3, 2, D), cut(3072, 2, KT, P), cut(4096, 2, KT, P), cut(5120, 2, KT, P), cut(6144, 2, P)
    k3, k3w = prob, prob
    kvs = k_sb[:, HD:2 * HD]
    junk_k = prob[:, 3 * HD:4 * HD]
    junk_q = [pT[:, h // 2, (2 + h % 2) * HD:(3 + h % 2) * HD] for h in range(HQ)]
    junk_f3, junk_k3, junk_q3 = (t[:, a:a + 2].rearrange("p a h c -> p (a h c)") for t, a in ((kT1, 0), (kT1, 2), (v1, 0)))
    hit_exp = mask
    hits = v1[:, 2:4].rearrange("p a h c -> p (a h c)")

    def hit(n):
        return hits[:, n * 64:(n + 1) * 64]

    def dense_bank(n):
        return (psQ, psKV, psS, psP)[n % 4]

    bias_row = {"q": 0, "k": 32, "o": 64}

    def wkv_k(hl, k, width):
        return wkv[:, hl, k // 2, (k % 2) * width:(k % 2 + 1) * width]

    block_cm = nc.Block()
    block = block_cm.__enter__()

    @block.sync
    def _(sp):
        def load(what, stage, src, split_before):
            sp.wait_ge(ld[what + "_lo"], split_before)
            sp.dma_start(stage, src).then_inc(ld[what + "_in"], 16)

        def load_wq(src, loads_before):
            need(sp, ld["wq_lo"], loads_before * 2)
            need(sp, ld["wq_lo_v"], loads_before * 2)
            sp.dma_start(stage_q[:], src).then_inc(ld["wq_in"], 16)

        for n in range(2):
            sp.dma_start(x[:, n], io["x"][:, n]).then_inc(ld[f"x{n}"], 16)
        load_wq(io["wq0"][0], 0)
        sp.dma_start(stage_o[:], io["ctxT"][0]).then_inc(ld["ctx_in"], 16)
        sp.dma_start(stage_kv[:], io["wkv0"][0]).then_inc(ld["wkv_in"], 16)
        sp.dma_start(x[:, 2:NT], io["x"][:, 2:NT]).then_inc(ld["x_rest"], 16)
        for b in range(2):
            sp.dma_start(mask[b * S:(b + 1) * S], io["mask"]).then_inc(ld["small"], 16)
        for c, what in enumerate(("qn1", "kn1")):
            sp.dma_start(wqk[:, c:c + 1], io[what]).then_inc(ld["small"], 16)
        for c, what in enumerate(("qn3", "kn3")):
            sp.dma_start(wqk3[:, c], io[what]).then_inc(ld["small"], 16)
        for c, what in enumerate(("bq3", "bk3", "bias3")):
            sp.dma_start(wide[32 * c:32 * c + 1], io[what]).then_inc(ld["vec_in"], 16)

        for half in range(2):
            sp.wait_ge(ld["ctx_lo"], half * 2 + 2)
            sp.wait_ge(ld["ctx_lo_v"], half * 2 + 2)
            if half == 0:
                sp.dma_start(stage_o[:], io["ctxT"][1]).then_inc(ld["ctx_in"], 16)
        sp.dma_start(stage_o[:], io["wo0"][0]).then_inc(ld["wo_in"], 16)
        with sp.Fori(0, 3) as kv:
            load_wq(io["wq0"][kv * 2 + 1], kv * 2 + 1)
            load("wkv", stage_kv[:], io["wkv0"][kv + 1], kv * 2 + 2)
            load("wo", stage_o[:], io["wo0"][kv * 2 + 1], kv * 8 + 4)
            load_wq(io["wq0"][kv * 2 + 2], kv * 2 + 2)
            load("wo", stage_o[:], io["wo0"][kv * 2 + 2], kv * 8 + 8)
        load_wq(io["wq0"][7], 7)
        load("wo", stage_o[:], io["wo0"][7], 28)
        load("wkv", stage_kv[:, :, 0:504], io["ga0"], 8)
        load_wq(io["base0"], 8)
        load("wo", stage_o[0:112, 0:2], io["b0"], 32)
        load("wkv", stage_kv[:], io["wkv1"][0], 10)
        load_wq(io["wq1"][0], 9)
        load("wo", stage_o[:], io["wo1"][0], 34)
        with sp.Fori(1, NHG) as hg:
            load("wkv", stage_kv[:], io["wkv1"][hg], hg * 2 + 10)
            load_wq(io["wq1"][hg], hg + 9)
            load("wo", stage_o[:], io["wo1"][hg], hg * 4 + 34)
        load("wkv", stage_kv[:, :, 0:144], io["ga1"], 26)
        load_wq(io["base1"], 17)
        load("wo", stage_o[0:64, 0:1], io["b1"], 66)
        sp.wait_ge(ld["wq_lo"], 36)
        sp.wait_ge(ld["wq_lo_v"], 36)
        for n in range(2 * NT):
            if n == 4:
                load("wkv", stage_kv[:, :, 0:136], io["ga2"], 28)
                load("wo", stage_o[0:64, 0:1], io["b2"], 67)
                load("wo", stage_o[:], io["wq3"], 68)
            if n == NT:
                sp.wait_ge(ld["wq_lo"], 38)
                sp.wait_ge(ld["wq_lo_v"], 38)
                sp.dma_start(stage_o[:], io["wk3"]).then_inc(ld["wo_in"], 16)
                load("wkv", stage_kv[:, :, 0:128], io["cent"], 30)
                sp.wait_ge(ld["vec_lo"], 1)
                sp.dma_start(wide[:], io["fn_w"].to_broadcast([P, D])).then_inc(ld["fn_in"], 16)
            if n >= 4:
                if n - 4 < NT:
                    sp.wait_ge(M["e_tr"], n - 3)
                else:
                    sp.wait_ge(N3["f_lo"], n - 4 - NT + 1)
                    sp.wait_ge(N3["f_tr"], n - 4 - NT + 1)
            sp.dma_start(stage_q[:, n % 4], io["ctx"][:, n % NT]).then_inc(ld[f"c{n % 4}"], 16)
        load("wo", stage_o[:], io["w3"], 72)
        sp.wait_ge(N3["q_tr"], NT)
        sp.dma_start(q_sb[0:64].bitcast(i32), io["asg"].to_broadcast([64, D])).then_inc(ld["asg_in"], 16)
        for n in range(NT):
            sp.wait_ge(C3["out"], n + 1)
            sp.dma_start(io["out"][:, n], x[:, n]).then_inc(out_done, 16)
        sp.wait_ge(out_done, 16 * NT)
    @block.gpsimd
    def _(pool):
        g = nc.gpsimd
        g.memset(minus_half[:], -0.5).then_inc(setup["const"], 1)
        g.memset(ident[:], 0.0).then_inc(setup["const"], 1)
        pool.wait_ge(setup["const"], 2)
        g.affine_select(out=ident[:], in_=ident[:], compare_op=ALU.not_equal, fill=1.0, base=0,
                        pattern=[[-1, P]], channel_multiplier=1).then_inc(setup["const"], 1)

        def low(what, dst, stage, hi_count):
            pool.wait_ge(ld[what + "_hi"], hi_count)
            g.tensor_tensor(dst[LO], stage, dst[HI].bitcast(f32), ALU.subtract).then_inc(ld[what + "_lo"], 1)

        def low_ctx(half):
            for k in range(2):
                low("ctx", (ctx_part(HI, k, half), ctx_part(LO, k, half)),
                    stage_o[:, k].rearrange("p (n b t) -> p n b t", n=4, b=2), half * 4 + k + 1)

        def halves(t, *at):
            return t[(slice(None), HI, *at)], t[(slice(None), LO, *at)]

        def ln_rstd(ln, n):
            pool.wait_ge(LNS[ln]["var"], ln_at(ln, n + 1))
            g.tensor_tensor(rstd[:, n:n + 1], var_eps[:, n:n + 1], minus_half[:, 0:1],
                            ALU.pow).then_inc(LNS[ln]["rstd"], 1)

        g.memset(ones[:], 1.0).then_inc(setup["ones"], 1)
        g.iota(iota[:], [[1, 32]], base=0, channel_multiplier=0,
               allow_small_or_imprecise_dtypes=True).then_inc(setup["iota"], 1)
        g.iota(row_id[:], [[0, 1]], base=0, channel_multiplier=1,
               allow_small_or_imprecise_dtypes=True).then_inc(setup["iota"], 1)
        g.memset(block8[:], 1.0).then_inc(setup["b8"], 1)
        groups = block8[:].rearrange("p (g e) -> p g e", e=8)
        pool.wait_ge(setup["b8"], 1)
        g.affine_select(out=groups, in_=groups, compare_op=ALU.is_ge, fill=0.0, base=0,
                        pattern=[[-8, 16], [0, 8]], channel_multiplier=1).then_inc(setup["b8"], 1)
        pool.wait_ge(setup["b8"], 2)
        g.affine_select(out=groups, in_=groups, compare_op=ALU.is_ge, fill=0.0, base=7,
                        pattern=[[8, 16], [0, 8]], channel_multiplier=-1).then_inc(setup["b8"], 1)


        def low_wq(load, stage=stage_q):
            for k in range(2):
                low("wq", halves(wq, k), stage[:, k], load * 4 + (k + 1))

        def low_wo(count, n=KT):
            for k in range(n):
                low("wo", halves(wo, k), stage_o[:, k], count + k + 1)

        def low_wkv(count, width=D):
            for k in range(2):
                low("wkv", halves(wkv, k, slice(0, width)), stage_kv[:, k, 0:width], count + k + 1)

        ln_rstd(0, 0)
        low_wq(0)
        ln_rstd(0, 1)
        low_ctx(0)
        low_wkv(0)
        for n in range(2, NT):
            ln_rstd(0, n)
            if n == 3:
                low_ctx(1)
        with pool.Fori(0, 3) as kv:
            low_wo(kv * 8)
            low_wq(kv * 2 + 1)
            low_wo(kv * 8 + 4)
            low_wkv(kv * 2 + 2)
            low_wq(kv * 2 + 2)
        low_wo(24)
        low_wq(7)
        low_wo(28)
        for n in range(NT):
            ln_rstd(1, n)
            if n == 0:
                low_wkv(8, 504)
            if n == 3:
                low_wq(8)

        def power(what, n, col):
            pool.wait_ge(N3["ms_" + what], n + 1)
            g.tensor_tensor(small[:, col + 1:col + 2], small[:, col:col + 1], minus_half[:, 0:1],
                            ALU.pow).then_inc(N3["pw_" + what], 1)

        def low_b(f, count):
            for j in range(f.parts):
                low("wo", (wo[0:f.rows, HI, j], wo[0:f.rows, LO, j]), stage_o[0:f.rows, j], count + j + 1)

        low_b(FF[0], 32)
        for n in range(NT):
            if n == 6:
                low_wkv(10)
                low_wq(9)
            ln_rstd(2, n)
        s = A
        for t in steps(pool, STEPS, L1.unroll, LAG, L1.done):
            if t.static and 0 <= t.t - LN_SLOT < NT:
                ln_rstd(3, t.t - LN_SLOT)
            if t.exists:
                pool.wait_ge(s["ms"], t.t + 1)
                need(pool, s["k_read"], t.t + L1.kv_done - 1)
                g.tensor_tensor(rms[:, t.res(2)], ms_eps[:, t.res(2)], minus_half[:, 0:5],
                                ALU.pow).then_inc(s["rms"], 1)
            if t.res(8) == 7 and t.exists:
                low_wq(t.div(8) + 10)
                if t.static and t.t == STEPS - 1:
                    low_wkv(26, 144)
                else:
                    low_wkv(t.div(8) * 2 + 12)
            if t.res(8) == 2 and not (t.static and t.t >= 64):
                low_wo(t.div(8) * 4 + 34)
        low_b(FF[1], 66)
        for n in range(NT):
            ln_rstd(4, n)
        low_wkv(28, 136)
        low_b(FF[2], 67)
        for n in range(NT):
            ln_rstd(5, n)
            if n == 2:
                low_wq(18, stage_o)
        for n in range(NT):
            if n == NT - 1:
                power("f", 0, 0)
            ln_rstd(6, n)
        for c, k in enumerate((1, 2, 3, 0)):
            low("wo", halves(wo, k), stage_o[:, k], 68 + c + 1)
        low_wkv(30, 128)
        for t in range(NT + 2):
            if 0 <= t - 1 < NT:
                power("q", t - 1, 4)
            if t + 1 < NT:
                power("f", t + 1, 0)
            if t < NT:
                power("k", t, 2)
            if 0 <= t - 2 < NT:
                ln_rstd(7, t - 2)
            if t == NT:
                low_wq(19, stage_o)

    @block.tensor
    def _(pe):
        mm, tr = nc.tensor.matmul, nc.tensor.transpose

        def wq_split(load, k):
            pe.wait_ge(ld["wq_lo" if k < 2 else "wq_lo_v"], load * 2 + (k % 2 + 1))

        def ln_transpose(ln, n, free):
            s = LNS[ln]
            pe.wait_ge(s["xn"], ln_at(ln, n + 1))
            free()
            for k in range(KT):
                i = tr(ln_bank(ln, n)[:, k * P:(k + 1) * P], xn[:, xn_slot(ln, n), k * P:(k + 1) * P], ident[:])
            i.then_inc(s["tr"], 1)

        def attention(a, next_ln):
            s, keys = A, a.keys

            def scores(u):
                pe.wait_ge(s["qT_lo"], u.c + 1)
                if a.kv_new(u):
                    pe.wait_ge(s["kT_lo"], a.kv_n(u) + 1)
                need(pe, s["exp"], u.c)
                n = u.res(NT)
                for b in range(2):
                    for hp in range(2):
                        at = ((b * 2 + hp) if a.index == 0 else (hp * 2 + b)) * keys
                        for i, (ql, kl) in enumerate(PASSES):
                            m = mm(psS[:, at:at + keys],
                                   qT[:, ql, b, 2 * hp:2 * hp + 2, :].rearrange("p h t -> p (h t)"),
                                   a.kT[:, u.res(a.ring), kl, b * keys:(b + 1) * keys], start=i == 0, stop=i == 2)
                m.then_inc(s["scores"], 1)

            def q_proj(st, first, last):
                n = st.res(NT)
                if first == 0:
                    need(pe, s["q_read"], st.c)
                for k in range(first, last):
                    if n == 0:
                        wq_split(st.div(NT) + a.wq0, k)
                    if st.static and k == 0:
                        if st.t < LAG:
                            pe.wait_ge(LNS[2 * a.index]["lo"], ln_at(2 * a.index, NT if st.t == LAG - 1 else n + 1))
                    for i, (xl, wl) in enumerate(PASSES):
                        m = mm(psQ[:], lat(xl, k, n), wq[:, wl, k, :],
                               start=k == 0 and i == 0, stop=k == KT - 1 and i == 2)
                    m.then_inc(s["wq_used"], 1)

            def kv_proj(st):
                if st.static and st.t == 0 and a.index == 1:
                    pe.wait_ge(setup["ctxT"], 8)
                need(pe, s["kT_lo"], a.kv_n(st))
                need(pe, s["v_lo"], a.kv_n(st))
                n = st.res(NT)
                if n == 0:
                    pe.wait_ge(ld["wkv_lo"], st.div(a.kv_period) * 2 + (a.wkv0 + 2))
                if st.static and a.index == 0 and st.t < LAG:
                    half = st.t // (LAG - 1)
                    pe.wait_ge(ld["ctx_lo"], half * 2 + 2)
                    pe.wait_ge(ld["ctx_lo_v"], half * 2 + 2)
                for b in range(2 if a.index == 0 else 1):
                    for k in range(KT):
                        for i, (xl, wl) in enumerate(PASSES):
                            lhsT = hidden(xl, k, n, b) if a.index == 0 else ctxT[:, xl, k, tok(n)]
                            m = mm(psKV[:, b * 256:(b + 1) * 256], lhsT, wkv_k(wl, k, 256),
                                   start=k == 0 and i == 0, stop=k == KT - 1 and i == 2)
                m.then_inc(s["kv"], 1)

            def q_transpose(st):
                pe.wait_ge(s["q_read"], st.c + 1)
                need(pe, s["qT_lo"], st.c)
                if st.static and st.t < LAG - 1:
                    pe.wait_ge(LNS[2 * a.index]["lo"], ln_at(2 * a.index, 2 * st.t + 3 if a.index == 0 else NT))
                if st.static and st.t - LN_SLOT >= 0:
                    pe.wait_ge(LNS[next_ln]["lo"], ln_at(next_ln, st.t - LN_SLOT + 1))
                for h in range(HQ):
                    i = tr(psT[:, h * P:(h + 1) * P], q_sb[:, h * P:(h + 1) * P], ident[:])
                i.then_inc(s["q_tr"], 1)

            def k_transpose(st):
                pe.wait_ge(s["k_read"], a.kv_n(st) + 1)
                pe.wait_ge(s["v_lo"], a.kv_n(st) + 1)
                for b in range(2 if a.index == 0 else 1):
                    i = tr(psKV[:, b * P:(b + 1) * P], k_sb[:, b * P:(b + 1) * P], ident[:])
                i.then_inc(s["k_tr"], 1)

            def p_transpose(u):
                pe.wait_ge(s["prob"], u.c + 1)
                need(pe, s["pT_lo"], u.c)
                for j in range(4 * keys // P):
                    i = tr(psP[:, j * P:(j + 1) * P], prob[:, j * P:(j + 1) * P], ident[:])
                i.then_inc(s["p_tr"], 1)

            def attend(u):
                pe.wait_ge(s["pT_lo"], u.c + 1)
                need(pe, s["oT_lo"], u.c)
                n = u.res(NT)
                for b in range(2):
                    for i, (vl, pl) in enumerate(PASSES):
                        if a.index == 0:
                            lhsT, rhs = a.v[:, n, vl, b * HD:(b + 1) * HD], pT[:, pl, b * 256:(b + 1) * 256]
                        else:
                            rows = slice(b * S, (b + 1) * S)
                            lhsT, rhs = a.v[rows, u.res(a.ring), vl, 0:HD], pT[rows, pl, 0:256]
                        m = mm(psO[:, b, 0:256], lhsT, rhs, start=i == 0, stop=i == 2)
                m.then_inc(s["pv"], 1)

            def out_proj(w, first, last):
                n = w.res(NT)
                if first == 0:
                    pe.wait_ge(s["oT_lo"], w.c + 1)
                    need(pe, s["x_add"], w.c)
                for h in range(first, last):
                    if n == 0:
                        pe.wait_ge(ld["wo_lo"], w.div(NT) * 4 + (a.wo0 + h + 1))
                    for i, (ol, wl) in enumerate(PASSES):
                        m = mm(psY[:], oT[:, ol, h, :], wo[:, wl, h, :],
                               start=h == 0 and i == 0, stop=h == HQ - 1 and i == 2)
                    m.then_inc(s["wo_used"], 1)

            for t in steps(pe, STEPS, a.unroll, LAG, a.done):
                t1, t2, t3 = t.back(1), t.back(2), t.back(3)
                if t.exists:
                    q_proj(t, 0, 2)
                if t2.exists:
                    p_transpose(t2)
                if t.exists:
                    q_proj(t, 2, 4)
                    if a.kv_new(t):
                        kv_proj(t)
                if t1.exists:
                    scores(t1)
                if a.index == 0 and t.static and t.t < LAG - 1:
                    for n in (2 * t.t + 2, 2 * t.t + 3):
                        def free():
                            pe.wait_ge(LNS[0]["lo"], ln_at(0, n - 1))
                            need(pe, s["qT_lo"], t.c)
                        ln_transpose(0, n, free)
                if t.static and t.t >= LN_SLOT:
                    n = t.t - LN_SLOT

                    def free():
                        pe.wait_ge(s["qT_lo"], min(t.c, a.done + STEPS))
                        need(pe, LNS[next_ln]["lo"], ln_at(next_ln, n))
                    ln_transpose(next_ln, n, free)
                if t2.exists:
                    attend(t2)
                if t3.exists:
                    out_proj(t3, 0, 4)
                if t.exists:
                    q_transpose(t)
                    if a.kv_new(t):
                        k_transpose(t)

        def ffn(f, next_ln):
            s, done = FS, f.done
            for t in range(NT + 3):
                if t < NT:
                    pe.wait_ge(LNS[f.ln]["lo"], ln_at(f.ln, t + 1))
                    need(pe, s["hid"], done + t)
                    if t == 0:
                        pe.wait_ge(ld["wkv_lo"], f.wkv_n)
                        if f.ln == 5:
                            pe.wait_ge(LNS[f.ln]["lo"], ln_at(f.ln, NT))
                    for k in range(KT):
                        for i, (xl, wl) in enumerate(PASSES):
                            m = mm(psQ[:, 0:f.width], lat(xl, k, t), wkv_k(wl, k, f.width),
                                   start=k == 0 and i == 0, stop=k == KT - 1 and i == 2)
                    m.then_inc(s["gate_a"], 1)
                    if f.dense:
                        need(pe, s["x_add"], done + t - 2)
                        for k in range(KT):
                            if t == 0:
                                wq_split(WQ_DENSE[f.index], k)
                            for i, (xl, wl) in enumerate(PASSES):
                                m = mm(ring3(t)[:], lat(xl, k, t), wq[:, wl, k, :],
                                       start=k == 0 and i == 0, stop=False)
                        m.then_inc(s["dense"], 1)
                if 0 <= t - 1 < NT:
                    u = t - 1
                    pe.wait_ge(s["hid"], done + u + 1)
                    need(pe, s["hidT_lo"], done + u)
                    for j in range(f.parts):
                        i = tr(psP[0:f.rows, j * P:(j + 1) * P], s_sb[:, j * f.rows:(j + 1) * f.rows], ident[:])
                    i.then_inc(s["hid_tr"], 1)
                if 0 <= t - 2 < NT:
                    u = t - 2
                    pe.wait_ge(s["hidT_lo"], done + u + 1)
                    if u == 0:
                        pe.wait_ge(ld["wo_lo"], f.wo_n)
                    if not f.dense:
                        need(pe, s["x_add"], done + u - 2)
                    for j in range(f.parts):
                        for i, (hl, wl) in enumerate(PASSES):
                            m = mm(ring3(u)[:], hidT[0:f.rows, hl, j, :], wo[0:f.rows, wl, j, :],
                                   start=not f.dense and j == 0 and i == 0, stop=j == f.parts - 1 and i == 2)
                    m.then_inc(s["experts"], 1)
                if 0 <= t - 3 < NT and next_ln != 4:
                    ln_transpose(next_ln, t - 3, lambda: need(pe, LNS[next_ln]["lo"], ln_at(next_ln, t - 3)))

        def linear_attention(next_ln):
            s = M
            for t in range(NT + 4):
                if 0 <= t - 2 < NT:
                    u = t - 2
                    pe.wait_ge(s["q2_lo"], u + 1)
                    pe.wait_ge(s["kvs_lo"], u + 1)
                    need(pe, s["x_add"], u)
                    for i, (kl, ql) in enumerate(PASSES):
                        m = mm(psY[:], kvs_r[:, u % 2, kl, :], q2[:, ql, :], start=i == 0, stop=i == 2)
                    m.then_inc(s["out"], 1)
                if 0 <= t - 1 < NT:
                    pe.wait_ge(s["eT_lo"], t)
                    need(pe, s["kvs"], t - 1)
                    for k in range(KT):
                        for i, (el, cl) in enumerate(PASSES):
                            m = mm(psKV[:, 0:P], eT[:, el, k, :], ctxT[:, cl, k, tok(t - 1)],
                                   start=k == 0 and i == 0, stop=k == KT - 1 and i == 2)
                    m.then_inc(s["kv"], 1)
                if t < NT:
                    ln_transpose(4, t, lambda: need(pe, s["q_shift"], t))
                    pe.wait_ge(s["e"], t + 1)
                    need(pe, s["eT_lo"], t)
                    if t == 0:
                        pe.wait_ge(FS["x_add"], 2 * NT)
                    for k in range(KT):
                        i = tr(psS[:, k * P:(k + 1) * P], stage_q[:, t % 4, k * P:(k + 1) * P], ident[:])
                    i.then_inc(s["e_tr"], 1)
                if 0 <= t - 1 < NT:
                    pe.wait_ge(s["q_soft"], t)
                    need(pe, s["q2_lo"], t - 1)
                    for k in range(KT):
                        i = tr(psP[:, k * P:(k + 1) * P], prob[:, k * P:(k + 1) * P], ident[:])
                    i.then_inc(s["q_tr"], 1)
                if 0 <= t - 3 < NT:
                    def free():
                        if t == 3:
                            pe.wait_ge(FS["hid"], 2 * NT)
                        need(pe, LNS[next_ln]["lo"], ln_at(next_ln, t - 3))
                    ln_transpose(next_ln, t - 3, free)

        def add_bias(bank, what):
            r = bias_row[what]
            for i in range(2):
                m = mm(bank, ones_r[r:r + 1, :], pT[r:r + 1, i, :], start=False, stop=i == 1)
            return m

        def cross_attention(next_ln):
            s = N3

            def f_transpose(n):
                pe.wait_ge(s["f"], n + 1)
                need(pe, s["fT_lo"], n)
                for k in range(KT):
                    i = tr(psS[:, k * P:(k + 1) * P], stage_q[:, n % 4, k * P:(k + 1) * P], ident[:])
                i.then_inc(s["f_tr"], 1)

            def similarity(n):
                pe.wait_ge(LNS[next_ln]["lo"], ln_at(next_ln, n + 1))
                if n == 0:
                    pe.wait_ge(ld["wkv_lo"], 32)
                need(pe, C3["exp"], n)
                for k in range(KT):
                    for i, (xl, wl) in enumerate(PASSES):
                        m = mm(psO[:, 1, P:P + 64], lat(xl, k, n), wkv_k(wl, k, 64),
                               start=k == 0 and i == 0, stop=k == KT - 1 and i == 2)
                m.then_inc(C3["sim"], 1)

            f_transpose(0)
            for t in range(NT + 4):
                u = t - 1
                if t < NT:
                    pe.wait_ge(s["fT_lo"], t + 1)
                    need(pe, s["kn"], t)
                    if t == 0:
                        pe.wait_ge(ld["wo_lo"], 72)
                        pe.wait_ge(ld["vec_lo"], 1)
                    for k in range(KT):
                        for i, (xl, wl) in enumerate(PASSES):
                            mm(psKV[:], fT[:, xl, k, :], wo[:, wl, k, :], start=k == 0 and i == 0, stop=False)
                    add_bias(psKV[:], "k").then_inc(s["k"], 1)
                if 0 <= u < NT:
                    pe.wait_ge(s["q_sb"], u + 1)
                    need(pe, LNS[6]["lo"], ln_at(6, NT))
                    need(pe, LNS[next_ln]["lo"], ln_at(next_ln, min(t - 3, NT)))
                    for k in range(KT):
                        i = tr(psT[:, k * P:(k + 1) * P], q_sb[:, k * P:(k + 1) * P], ident[:])
                    i.then_inc(s["q_tr"], 1)
                if 0 <= t - 2 < NT:
                    pe.wait_ge(s["pT_lo"], t - 1)
                    pe.wait_ge(s["f_lo"], t - 1)
                    need(pe, s["x_add"], t - 2)
                    for i, (pl, fl) in enumerate(PASSES):
                        m = mm(psY[:], pT3[:, pl, :], f_r[:, (t - 2) % 3, fl, :], start=i == 0, stop=i == 2)
                    m.then_inc(s["attend"], 1)
                if 0 <= t - 4 < NT:
                    similarity(t - 4)
                if 0 <= u < NT:
                    pe.wait_ge(s["qT_lo"], u + 1)
                    pe.wait_ge(s["kT_lo"], u + 1)
                    need(pe, s["exp"], u)
                    for k in range(KT):
                        for i, (ql, kl) in enumerate(PASSES):
                            m = mm(psO[:, 0, 0:P], qT3[:, ql, k, :], kT3[:, kl, k, :],
                                   start=k == 0 and i == 0, stop=k == KT - 1 and i == 2)
                    m.then_inc(s["scores"], 1)
                if t + 1 < NT:
                    f_transpose(t + 1)
                if 0 <= t - 3 < NT:
                    ln_transpose(next_ln, t - 3, lambda: pe.wait_ge(s["qT_lo"], min(t, NT)))
                if t < NT:
                    pe.wait_ge(LNS[6]["lo"], ln_at(6, t + 1))
                    need(pe, s["q_sq"], t)
                    for k in range(KT):
                        if t == 0:
                            wq_split(18, k)
                        for i, (xl, wl) in enumerate(PASSES):
                            mm(psQ[:], lat(xl, k, t), wq[:, wl, k, :], start=k == 0 and i == 0, stop=False)
                    add_bias(psQ[:], "q").then_inc(s["q"], 1)
                if 0 <= u < NT:
                    pe.wait_ge(s["prob"], u + 1)
                    need(pe, C3["exp"], t - 4 + 1)
                    tr(psO[:, 1, 0:P], s_sb[:, 0:P], ident[:]).then_inc(s["p_tr"], 1)
                if t < NT:
                    pe.wait_ge(s["kn"], t + 1)
                    need(pe, s["kw"], t)
                    for k in range(KT):
                        i = tr(psP[:, k * P:(k + 1) * P], k3[:, k * P:(k + 1) * P], ident[:])
                    i.then_inc(s["k_tr"], 1)
                if t > NT + 1 :
                    for n in range((t - NT - 2) * 2, (t - NT - 2) * 2 + 2):
                        dense(n)

        def dense(n):
            s = C3
            if n == 0:
                pe.wait_ge(N3["q_sq"], NT)
                pe.wait_ge(N3["kn"], NT)
                pe.wait_ge(N3["kw"], NT)
            need(pe, s["masked"], n - 3)
            for k in range(KT):
                if n == 0:
                    wq_split(19, k)
                for i, (xl, wl) in enumerate(PASSES):
                    mm(dense_bank(n)[:], lat(xl, k, n), wq[:, wl, k, :], start=k == 0 and i == 0, stop=False)
            add_bias(dense_bank(n)[:], "o").then_inc(s["dense"], 1)

        def clustered():
            s = C3
            pe.wait_ge(s["hits"], NT)
            pe.wait_ge(N3["exp"], NT)
            for n in range(NT):
                m = mm(psO[0:64, 0, 0:2], hit(n), ones_r[:, 0:2], start=n == 0, stop=n == NT - 1)
            m.then_inc(s["count"], 1)
            pe.wait_ge(s["sel"], 1)
            mm(psT[:], s_sb[0:64, 0:P], prob[0:64, :], start=True, stop=True).then_inc(s["rows"], 1)
            for n in range(4, NT):
                dense(n)

        pe.wait_ge(setup["const"], 3)
        for n in range(2):
            ln_transpose(0, n, lambda: None)
        attention(L0, 1)
        ffn(FF[0], 2)
        attention(L1, 3)
        ffn(FF[1], 4)
        linear_attention(5)
        ffn(FF[2], 6)
        cross_attention(7)
        clustered()

    @block.scalar
    def _(act):
        copy = lambda o, i: nc.scalar.activation(o, i, ACT.Copy)

        def ln_hi(ln, n):
            s = LNS[ln]
            act.wait_ge(s["tr"], ln_at(ln, n + 1))
            copy(lat_all(HI, n), slices(ln_bank(ln, n))).then_inc(s["hi"], 1)

        def high(what, dst, stage, in_count):
            act.wait_ge(ld[what + "_in"], in_count)
            copy(dst, stage).then_inc(ld[what + "_hi"], 1)

        def high_wq(load):
            for k in range(KT):
                high("wq", wq[:, HI, k], stage_q[:, k], (load + 1) * 16)

        def high_wo(load, n=KT):
            for k in range(n):
                high("wo", wo[:, HI, k], stage_o[:, k], (load + 1) * 16)

        def high_ctx(half):
            for k in range(KT):
                high("ctx", ctx_part(HI, k, half), stage_o[:, k].rearrange("p (n b t) -> p n b t", n=4, b=2),
                     (half + 1) * 16)

        def high_wkv(load, width=D):
            for k in range(2):
                high("wkv", wkv[:, HI, k, 0:width], stage_kv[:, k, 0:width], (load + 1) * 16)

        def attention(a, next_ln):
            s, keys = A, a.keys

            def squares(st):
                n = st.res(2)
                act.wait_ge(s["wq_used"], st.c * 4 + 4)
                for h in range(HQ):
                    i = nc.scalar.activation(junk_q[h], psQ[:, h * HD:(h + 1) * HD], ACT.Square,
                                             accum_out=ssq[:, n, h:h + 1])
                i.then_inc(s["squares"], 1)

            def exps(u):
                act.wait_ge(s["neg_max"], u.c + 1)
                need(act, s["p_tr"], u.c)
                need(act, s["rsums"], u.c)
                for j in range(4):
                    at = slice(j * keys, (j + 1) * keys)
                    if a.rms:
                        e = nc.scalar.activation(prob[:, at], s_sb[:, at], ACT.Exp,
                                                 bias=neg_mx[:, j:j + 1], scale=1.0, accum_out=sums[:, j:j + 1])
                    else:
                        e = nc.scalar.activation(prob[:, at], psS[:, at], ACT.Exp,
                                                 bias=neg_mx[:, j:j + 1], scale=a.scale,
                                                 accum_out=sums[:, j:j + 1])
                e.then_inc(s["exp"], 1)

            def q_read(st):
                act.wait_ge(s["wq_used"], st.c * 4 + 4)
                need(act, s["q_tr"], st.c)
                copy(q_sb[:], psQ[:]).then_inc(s["q_read"], 1)

            def qT_hi(st):
                act.wait_ge(s["q_tr"], st.c + 1)
                need(act, s["scores"], st.c)
                copy(qT[:, HI], heads(psT[:])).then_inc(s["qT_hi"], 1)

            def kT_hi(st):
                act.wait_ge(s["k_tr"], a.kv_n(st) + 1)
                src = k_sb[:, HD:2 * HD] if a.rms else psKV[:, 0:2 * keys]
                if a.rms:
                    act.wait_ge(s["k_scaled"], st.t + 1)
                copy(a.kT[:, st.res(a.ring), HI], src).then_inc(s["kT_hi"], 1)

            def kv_read(st):
                act.wait_ge(s["kv"], a.kv_n(st) + 1)
                need(act, s["k_tr"], a.kv_n(st))
                if a.rms:
                    need(act, s["ms"], st.t - 1)
                    nc.scalar.activation(junk_k, psKV[:, 0:HD], ACT.Square, accum_out=ssq[:, st.res(2), 4:5])
                    copy(a.v[:, st.res(a.ring), HI], psKV[:, HD:2 * HD]).then_inc(s["v_hi"], 1)
                    return
                kv = psKV[:].rearrange("p (b c) -> p b c", b=2)
                copy(k_sb[:].rearrange("p (b c) -> p b c", b=2), kv[:, :, 0:HD]).then_inc(s["k_read"], 1)
                copy(a.v[:, st.res(a.ring), HI].rearrange("p (b c) -> p b c", b=2), kv[:, :, HD:256]).then_inc(s["v_hi"], 1)

            def oT_hi(u):
                act.wait_ge(s["pv"], u.c + 1)
                need(act, s["wo_used"], u.c * 4)
                copy(oT[:, HI].rearrange("p h (b t) -> p b h t", b=2),
                     psO[:, :, 0:256].rearrange("p b (h t) -> p b h t", h=HQ)).then_inc(s["oT_hi"], 1)

            def pT_hi(u):
                act.wait_ge(s["p_tr"], u.c + 1)
                need(act, s["pv"], u.c)
                copy(pT[:, HI, 0:4 * keys], psP[:, 0:4 * keys]).then_inc(s["pT_hi"], 1)

            for t in steps(act, STEPS, a.unroll, LAG, a.done):
                t1, t2 = t.back(1), t.back(2)
                if t2.exists:
                    pT_hi(t2)
                if t.exists:
                    if a.rms:
                        squares(t)
                    else:
                        q_read(t)
                    if a.kv_new(t):
                        kv_read(t)
                    if t.res(8) == 7:
                        act.wait_ge(s["wq_used"], t.c * 4 + 4)
                        high_wq(t.div(8) + (10 if a.rms else 1))
                if a.index == 0 and t.static and t.t < LAG - 1:
                    for n in (2 * t.t + 2, 2 * t.t + 3):
                        ln_hi(0, n)
                if t.static and t.t >= LN_SLOT:
                    ln_hi(next_ln, t.t - LN_SLOT)
                if t1.exists:
                    exps(t1)
                if t2.exists:
                    oT_hi(t2)
                if a.rms and t.res(8) == 7 and t.exists:
                    act.wait_ge(s["kv"], a.kv_n(t) + 1)
                    if t.static and t.t == STEPS - 1:
                        high_wkv(13, 144)
                    else:
                        high_wkv(t.div(8) + 6)
                if not a.rms and t.res(16) == 12 and t.exists:
                    act.wait_ge(s["kv"], t.div(16) * 8 + 8)
                    if t.static and t.t == 60:
                        high_wkv(4, 504)
                    else:
                        high_wkv(t.div(16) + 1)
                if t.res(8) == 2 and not (t.static and t.t >= STEPS):
                    need(act, s["wo_used"], t.div(8) * 32 + a.done * 4)
                    high_wo(t.div(8) + (9 if a.rms else 0))
                if t.exists:
                    if a.kv_new(t):
                        kT_hi(t)
                    qT_hi(t)
                    if a.index == 0 and t.static and t.t == 0:
                        high_ctx(1)

        high_wq(0)
        ln_hi(0, 0)
        high_ctx(0)
        high_wkv(0)
        ln_hi(0, 1)
        attention(L0, 1)

        def high_b(f, load):
            for j in range(f.parts):
                high("wo", wo[0:f.rows, HI, j], stage_o[0:f.rows, j], (load + 1) * 16)

        def ffn(f, next_ln, after):
            s, done = FS, f.done
            for t in range(NT + 3):
                if t < NT:
                    act.wait_ge(s["shift"], done + t + 1)
                    if f.index == 1:
                        nc.scalar.activation(gate[:, 0:8], logits[:, 0:8], ACT.Exp, bias=small[:, 0:1], scale=1.0,
                                             accum_out=small[:, 1:2]).then_inc(s["exp"], 1)
                    else:
                        nc.scalar.activation(small[:, 1:2], small[:, 0:1], ACT.Exp).then_inc(s["exp"], 1)
                if 0 <= t - 1 < NT:
                    act.wait_ge(s["hid_tr"], done + t)
                    need(act, s["experts"], done + t - 1)
                    copy(hidT[0:f.rows, HI, 0:f.parts], psP[0:f.rows, 0:f.parts * P].rearrange(
                        "p (j t) -> p j t", t=P)).then_inc(s["hidT_hi"], 1)
                if 0 <= t - 3 < NT and next_ln != 4:
                    ln_hi(next_ln, t - 3)
                after(t)

        def after0(t):
            if t < 8:
                hl, k = t // 4, t % 4
                copy(ctxT[:, hl, k].rearrange("p (n b t) -> p n b t", n=NT, b=2),
                     hT[:, hl, k, :, 0:4:3, :].bitcast(f32)).then_inc(setup["ctxT"], 1)
            if t == 8:
                act.wait_ge(FS["gate_a"], NT)
                high_wkv(5)
                act.wait_ge(FS["dense"], NT)
                high_wq(9)

        def ctx_exp(n):
            act.wait_ge(M["k_max"], n + 1)
            nc.scalar.activation(stage_q[:, n % 4], stage_q[:, n % 4], ACT.Exp, bias=small[:, 8 + n % 2:9 + n % 2],
                                 scale=1.0, accum_out=small[:, 10 + n % 2:11 + n % 2]).then_inc(M["e"], 1)

        def f_squares(n):
            act.wait_ge(ld[f"c{n % 4}"], (n // 4 + 3) * 16)
            need(act, N3["ms_f"], n)
            nc.scalar.activation(junk_f3, stage_q[:, n % 4], ACT.Square,
                                 accum_out=small[:, 6:7]).then_inc(N3["f_sq"], 1)

        def after1(t):
            if t == 8:
                act.wait_ge(FS["gate_a"], 2 * NT)
                high_wkv(14, 136)
                ctx_exp(0)
            if t == NT + 2:
                act.wait_ge(FS["experts"], 2 * NT)
                high_b(FF[2], 18)
                act.wait_ge(ld["vec_in"], 48)
                for r in bias_row.values():
                    i = copy(pT[r:r + 1, HI], wide[r:r + 1])
                i.then_inc(ld["vec_hi"], 1)
                copy(ones_r[:], ones[:]).then_inc(setup["ones_r"], 1)

        def after2(t):
            if t == 8:
                f_squares(0)
                for k in (1, 2, 3):
                    high("wo", wo[:, HI, k], stage_o[:, k], 21 * 16)
                act.wait_ge(FS["gate_a"], 3 * NT)
                high_wkv(15, 128)
            if t == NT + 2:
                act.wait_ge(FS["experts"], 3 * NT)
                high("wo", wo[:, HI, 0], stage_o[:, 0], 21 * 16)

        def linear_attention(next_ln):
            s = M

            for t in range(NT + 4):
                if 0 <= t - 1 < NT:
                    act.wait_ge(s["kvs"], t)
                    need(act, s["out"], t - 2)
                    copy(kvs_r[:, (t - 1) % 2, HI], kvs).then_inc(s["kvs_hi"], 1)
                if t < NT:
                    act.wait_ge(s["e_tr"], t + 1)
                    need(act, s["kv"], t)
                    copy(eT[:, HI], slices(psS)).then_inc(s["eT_hi"], 1)
                if 0 <= t - 1 < NT:
                    act.wait_ge(s["q_tr"], t)
                    need(act, s["out"], t - 1)
                    copy(q2[:, HI], psP[:]).then_inc(s["q2_hi"], 1)
                if t < NT:
                    act.wait_ge(s["q_shift"], t + 1)
                    nc.scalar.activation(q_sb[:], q_sb[:], ACT.Exp).then_inc(s["q_exp"], 1)
                if 0 <= t - 3 < NT:
                    ln_hi(next_ln, t - 3)
                if t + 1 < NT:
                    ctx_exp(t + 1)
                if t == 4:
                    act.wait_ge(ld["wo_in"], 20 * 16)
                    for k in range(KT):
                        copy(wq[:, HI, k], stage_o[:, k]).then_inc(ld["wq_hi"], 1)

        def cross_attention(next_ln):
            s = N3

            def f_hi(n):
                act.wait_ge(s["f"], n + 1)
                need(act, s["attend"], n - 2)
                copy(f_r[:, n % 3, HI], stage_q[:, n % 4]).then_inc(s["f_hi"], 1)

            def fT_hi(n):
                act.wait_ge(s["f_tr"], n + 1)
                need(act, s["k"], n)
                copy(fT[:, HI], slices(psS)).then_inc(s["fT_hi"], 1)

            f_hi(0)
            fT_hi(0)
            for t in range(NT + 4):
                u = t - 1
                if 0 <= u < NT:
                    act.wait_ge(s["kw"], u + 1)
                    need(act, s["scores"], u)
                    copy(kT3[:, HI], slices(k3w)).then_inc(s["kT_hi"], 1)
                if t + 1 < NT:
                    f_squares(t + 1)
                if t < NT:
                    act.wait_ge(s["k"], t + 1)
                    need(act, s["ms_k"], t)
                    nc.scalar.activation(junk_k3, psKV[:], ACT.Square, accum_out=small[:, 7:8]).then_inc(s["k_sq"], 1)
                if 0 <= u < NT:
                    act.wait_ge(s["q_tr"], u + 1)
                    copy(qT3[:, HI], slices(psT)).then_inc(s["qT_hi"], 1)
                if t < NT:
                    act.wait_ge(s["pw_k"], t + 1)
                    need(act, s["kT_lo"], t)
                    nc.scalar.activation(k3[:], psKV[:], ACT.Copy, scale=small[:, 3:4]).then_inc(s["kn"], 1)
                if t + 1 < NT:
                    f_hi(t + 1)
                if 0 <= t - 4 < NT:
                    act.wait_ge(C3["neg_max"], t - 3)
                    nc.scalar.activation(hit_exp[:], psO[:, 1, P:P + 64], ACT.Exp, bias=small[:, 13:14],
                                         scale=1.0 / TEMPERATURE, accum_out=small[:, 14:15]).then_inc(C3["exp"], 1)
                if 0 <= u < NT:
                    act.wait_ge(s["neg_max"], u + 1)
                    need(act, s["p_tr"], u)
                    for b in range(2):
                        rows = slice(b * S, (b + 1) * S)
                        i = nc.scalar.activation(s_sb[rows, b * S:(b + 1) * S], psO[rows, 0, b * S:(b + 1) * S], ACT.Exp,
                                                 bias=small[rows, 10:11], scale=small[rows, 9:10],
                                                 accum_out=small[rows, 11:12])
                    i.then_inc(s["exp"], 1)
                if 0 <= t - 3 < NT:
                    ln_hi(next_ln, t - 3)
                if t + 1 < NT:
                    fT_hi(t + 1)
                if t < NT:
                    act.wait_ge(s["q"], t + 1)
                    need(act, s["q_tr"], t)
                    copy(q_sb[:], psQ[:]).then_inc(s["q_sb"], 1)
                    need(act, s["ms_q"], t)
                    nc.scalar.activation(junk_q3, psQ[:], ACT.Square, accum_out=small[:, 8:9]).then_inc(s["q_sq"], 1)
                if 0 <= u < NT:
                    act.wait_ge(s["p_tr"], u + 1)
                    need(act, s["attend"], u)
                    copy(pT3[:, HI], psO[:, 1, 0:P]).then_inc(s["pT_hi"], 1)
                if t == NT :
                    act.wait_ge(s["q"], NT)
                    act.wait_ge(ld["wo_in"], 22 * 16)
                    for k in range(KT):
                        copy(wq[:, HI, k], stage_o[:, k]).then_inc(ld["wq_hi"], 1)

        act.wait_ge(A["wo_used"], STEPS * 4)
        high_b(FF[0], 8)
        ffn(FF[0], 2, after0)
        attention(L1, 3)
        act.wait_ge(A["wo_used"], 2 * STEPS * 4)
        high_b(FF[1], 17)
        ffn(FF[1], 4, after1)
        linear_attention(5)
        ffn(FF[2], 6, after2)
        cross_attention(7)

    @block.vector
    def _(dve):
        V = nc.vector

        def sub_hi(dst_lo, src, dst_hi):
            return V.tensor_tensor(dst_lo, src, dst_hi.bitcast(f32), ALU.subtract)

        links = [0]

        def link(instruction):
            links[0] += 1
            instruction.then_inc(chain, 1)
            dve.wait_ge(chain, links[0])

        def low_wq(load, stage=stage_q):
            for k in range(2, KT):
                dve.wait_ge(ld["wq_hi"], load * 4 + (k + 1))
                sub_hi(wq[:, LO, k], stage[:, k], wq[:, HI, k]).then_inc(ld["wq_lo_v"], 1)

        def ln_stats(ln, n):
            s = LNS[ln]
            link(V.bn_stats(bn[:, n % 2], x[:, n]))
            link(V.bn_aggr(mv[:, n], bn[:, n % 2]))
            V.tensor_scalar(var_eps[:, n:n + 1], mv[:, n, 1:2], LN_EPS, None, ALU.add).then_inc(s["var"], 1)

        def x_stats(n):
            dve.wait_ge(ld[f"x{n}" if n < 2 else "x_rest"], 16)
            ln_stats(0, n)

        def low_ctx(half):
            for k in range(2, KT):
                dve.wait_ge(ld["ctx_hi"], half * 4 + k + 1)
                sub_hi(ctx_part(LO, k, half), stage_o[:, k].rearrange("p (n b t) -> p n b t", n=4, b=2),
                       ctx_part(HI, k, half)).then_inc(ld["ctx_lo_v"], 1)

        def ln_norm(ln, n):
            s = LNS[ln]
            dve.wait_ge(s["rstd"], ln_at(ln, n + 1))
            need(dve, s["tr"], ln_at(ln, n if ln in (4, 5) else n - 1))
            V.tensor_scalar(xn[:, xn_slot(ln, n)], x[:, n], mv[:, n, 0:1], rstd[:, n:n + 1], ALU.subtract,
                            ALU.mult).then_inc(s["xn"], 1)

        def ln_lo(ln, n):
            s = LNS[ln]
            dve.wait_ge(s["hi"], ln_at(ln, n + 1))
            sub_hi(lat_all(LO, n), slices(ln_bank(ln, n)), lat_all(HI, n)).then_inc(s["lo"], 1)

        def attention(a, next_ln):
            s, keys = A, a.keys

            def blocks(t):
                return t[:, 0:4 * keys].rearrange("p (j c) -> p j c", j=4)

            def row_max(u):
                dve.wait_ge(s["scores"], u.c + 1)
                need(dve, s["exp"], u.c)
                src = psS
                if a.rms:
                    src = s_sb
                    V.scalar_tensor_tensor(blocks(s_sb), blocks(psS), a.scale, mask[:].unsqueeze(1).to_broadcast(
                        [P, 4, keys]), ALU.mult, ALU.add).then_inc(s["masked"], 1)
                    dve.wait_ge(s["masked"], u.t + 1)
                V.tensor_reduce(mx[:], blocks(src), AX.X, ALU.max).then_inc(s["max"], 1)
                dve.wait_ge(s["max"], u.c + 1)
                V.tensor_scalar(neg_mx[:], mx[:], -1.0 if a.rms else -a.scale, None, ALU.mult).then_inc(s["neg_max"], 1)

            def normalise(u):
                dve.wait_ge(s["exp"], u.c + 1)
                V.reciprocal(rsums[:], sums[:]).then_inc(s["rsums"], 1)
                dve.wait_ge(s["rsums"], u.c + 1)
                V.tensor_tensor(blocks(prob), blocks(prob), rsums[:].unsqueeze(2).to_broadcast([P, 4, keys]),
                                ALU.mult).then_inc(s["prob"], 1)

            def mean_squares(st):
                n = st.res(2)
                dve.wait_ge(s["squares"], st.t + 1)
                need(dve, s["rms"], st.t - 1)
                V.tensor_scalar(ms_eps[:, n], ssq[:, n], 1.0 / HD, RMS_EPS, ALU.mult,
                                ALU.add).then_inc(s["ms"], 1)

            def qk_normalise(st):
                n = st.res(2)
                dve.wait_ge(s["rms"], st.t + 1)
                need(dve, s["q_tr"], st.c)
                four = lambda t: t[:].rearrange("p (h c) -> p h c", h=HQ)
                V.tensor_tensor(four(q_sb), four(psQ), rms[:, n, 0:HQ].unsqueeze(2).to_broadcast([P, HQ, HD]),
                                ALU.mult).then_inc(s["q_read"], 1)
                need(dve, s["k_tr"], a.kv_n(st))
                V.tensor_scalar(k_sb[:, 0:HD], psKV[:, 0:HD], rms[:, n, 4:5], None, ALU.mult).then_inc(s["k_read"], 1)

            def k_scale(st):
                dve.wait_ge(s["k_tr"], a.kv_n(st) + 1)
                V.tensor_scalar(k_sb[:, HD:2 * HD], psKV[:, 0:HD], wqk[:, 2:3], None, ALU.mult).then_inc(s["k_scaled"], 1)

            def qT_lo(st):
                dve.wait_ge(s["qT_hi"], st.c + 1)
                sub_hi(qT[:, LO], heads(psT[:]), qT[:, HI]).then_inc(s["qT_lo"], 1)

            def kT_lo(st):
                dve.wait_ge(s["kT_hi"], a.kv_n(st) + 1)
                src = k_sb[:, HD:2 * HD] if a.rms else psKV[:, 0:2 * keys]
                sub_hi(a.kT[:, st.res(a.ring), LO], src, a.kT[:, st.res(a.ring), HI]).then_inc(s["kT_lo"], 1)

            def v_lo(st):
                dve.wait_ge(s["v_hi"], a.kv_n(st) + 1)
                if a.rms:
                    sub_hi(a.v[:, st.res(a.ring), LO], psKV[:, HD:2 * HD], a.v[:, st.res(a.ring), HI]).then_inc(s["v_lo"], 1)
                    return
                two = lambda ap: ap.rearrange("p (b c) -> p b c", b=2)
                sub_hi(two(a.v[:, st.res(a.ring), LO]), two(psKV[:])[:, :, HD:256],
                       two(a.v[:, st.res(a.ring), HI])).then_inc(s["v_lo"], 1)

            def x_add(w):
                n = w.res(NT)
                dve.wait_ge(s["wo_used"], w.c * 4 + 4)
                last = w.static and w.t >= STEPS - NT
                i = V.tensor_tensor(x[:, n], x[:, n], psY[:], ALU.add).then_inc(s["x_add"], 1)
                if last:
                    dve.wait_ge(s["x_add"], w.c + 1)
                    ln_stats(next_ln, n)

            def oT_lo(u):
                dve.wait_ge(s["oT_hi"], u.c + 1)
                out = oT[:, LO].rearrange("p h (b t) -> p b h t", b=2)
                hi = oT[:, HI].rearrange("p h (b t) -> p b h t", b=2)
                sub_hi(out, psO[:, :, 0:256].rearrange("p b (h t) -> p b h t", h=HQ), hi).then_inc(s["oT_lo"], 1)

            def pT_lo(u):
                dve.wait_ge(s["pT_hi"], u.c + 1)
                sub_hi(pT[:, LO, 0:4 * keys], psP[:, 0:4 * keys], pT[:, HI, 0:4 * keys]).then_inc(s["pT_lo"], 1)

            for t in steps(dve, STEPS, a.unroll, LAG, a.done):
                t1, t2, t3 = t.back(1), t.back(2), t.back(3)
                tail = t.static and t.t >= LN_SLOT
                first = a.index == 0 and t.static and t.t < LAG - 1
                if first:
                    ln_norm(0, 2 * t.t + 2)
                    ln_norm(0, 2 * t.t + 3)
                if t2.exists:
                    pT_lo(t2)
                if t.exists and a.kv_new(t):
                    v_lo(t)
                if first:
                    ln_lo(0, 2 * t.t + 2)
                    ln_lo(0, 2 * t.t + 3)
                if t.exists and a.rms:
                    mean_squares(t)
                if tail:
                    ln_norm(next_ln, t.t - LN_SLOT)
                if t1.exists:
                    row_max(t1)
                if tail:
                    ln_lo(next_ln, t.t - LN_SLOT)
                if t.exists and a.rms:
                    qk_normalise(t)
                if t.exists and t.res(8) == 7:
                    low_wq(t.div(8) + (10 if a.rms else 1))
                if t1.exists:
                    normalise(t1)
                if t3.exists:
                    x_add(t3)
                if t2.exists:
                    oT_lo(t2)
                if t.exists:
                    if a.kv_new(t):
                        if a.rms:
                            k_scale(t)
                        kT_lo(t)
                    qT_lo(t)
                if first:
                    if t.t == 0:
                        low_ctx(1)
                        dve.wait_ge(ld["small"], 96)
                        V.tensor_tensor(wqk[:, 2:3], wqk[:, 0:1], wqk[:, 1:2], ALU.mult)
                        link(V.tensor_tensor(wqk3[:, 2], wqk3[:, 0], wqk3[:, 1], ALU.mult))
                    if t.t < LAG - 2:
                        x_stats(2 * t.t + 4)
                        x_stats(2 * t.t + 5)

        col = lambda c: small[:, c:c + 1]

        def mean_square(what, n, src, dst):
            dve.wait_ge(N3[what + "_sq"], n + 1)
            V.tensor_scalar(col(dst), col(src), 1.0 / D, RMS_EPS3, ALU.mult, ALU.add).then_inc(N3["ms_" + what], 1)

        def features(n):
            if n == 0:
                dve.wait_ge(ld["fn_in"], 16)
            dve.wait_ge(N3["pw_f"], n + 1)
            V.scalar_tensor_tensor(stage_q[:, n % 4], stage_q[:, n % 4], col(1), wide[:], ALU.mult,
                                   ALU.mult).then_inc(N3["f"], 1)

        def ffn(f, next_ln):
            s, done, E, R = FS, f.done, f.E, f.R

            def gates(t):
                dve.wait_ge(s["gate_a"], done + t + 1)
                link(V.tensor_copy(logits[:, 0:E], psQ[:, 0:E]))
                if f.index == 1:
                    link(V.max(top[:], logits[:, 0:E]))
                    V.tensor_scalar(small[:, 0:1], top[:, 0:1], -1.0, None, ALU.mult).then_inc(s["shift"], 1)
                    dve.wait_ge(s["exp"], done + t + 1)
                    link(V.reciprocal(small[:, 2:3], small[:, 1:2]))
                    link(V.tensor_scalar(logits[:, 0:E], gate[:, 0:E], small[:, 2:3], None, ALU.mult))
                wide_e = max(E, 8)
                link(V.max(top[:], logits[:, 0:wide_e]))
                if f.index != 1:
                    V.tensor_tensor(small[:, 0:1], top[:, 1:2], top[:, 0:1], ALU.subtract).then_inc(s["shift"], 1)
                link(V.max_index(top_at[:], top[:], logits[:, 0:wide_e]))
                link(V.tensor_copy(top_f[:], top_at[:, 0:2]))
                if f.index == 1:
                    first, second = top[:, 0:1], top[:, 1:2]
                    link(V.tensor_tensor(small[:, 2:3], first, second, ALU.add))
                else:
                    first, second = ones[:, 0:1], small[:, 1:2]
                    dve.wait_ge(s["exp"], done + t + 1)
                    link(V.tensor_scalar(small[:, 2:3], second, 1.0, None, ALU.add))
                link(V.reciprocal(small[:, 3:4], small[:, 2:3]))
                for c, share in enumerate((first, second)):
                    link(V.tensor_tensor(small[:, 4 + c:5 + c], share, small[:, 3:4], ALU.mult))
                for c in range(2):
                    link(V.tensor_scalar(pick[:, c, 0:E], iota[:, 0:E], top_f[:, c:c + 1], small[:, 4 + c:5 + c],
                                         ALU.is_equal, ALU.mult))
                link(V.tensor_tensor(gate[:, 0:E], pick[:, 0, 0:E], pick[:, 1, 0:E], ALU.add))

            def hid(t):
                need(dve, s["hid_tr"], done + t)
                by_expert = lambda ap: ap.rearrange("p (e r) -> p e r", e=E)
                V.scalar_tensor_tensor(by_expert(s_sb[:, 0:E * R]), by_expert(psQ[:, E:f.width]), f.scale,
                                       gate[:, 0:E].unsqueeze(2).to_broadcast([P, E, R]), ALU.mult,
                                       ALU.mult).then_inc(s["hid"], 1)

            if f.index == 0:
                dve.wait_ge(setup["iota"], 2)
                dve.wait_ge(setup["ones"], 1)
            if E < 8:
                link(V.memset(logits[:, E:8], -3e38))
            for t in range(NT + 3):
                if 0 <= t - 3 < NT and next_ln != 4:
                    ln_norm(next_ln, t - 3)
                if t < NT:
                    gates(t)
                    hid(t)
                if 0 <= t - 1 < NT:
                    dve.wait_ge(s["hidT_hi"], done + t)
                    sub_hi(hidT[0:f.rows, LO, 0:f.parts],
                           psP[0:f.rows, 0:f.parts * P].rearrange("p (j t) -> p j t", t=P),
                           hidT[0:f.rows, HI, 0:f.parts]).then_inc(s["hidT_lo"], 1)
                if 0 <= t - 2 < NT:
                    u = t - 2
                    dve.wait_ge(s["experts"], done + u + 1)
                    V.tensor_tensor(x[:, u], x[:, u], ring3(u)[:], ALU.add).then_inc(s["x_add"], 1)
                    dve.wait_ge(s["x_add"], done + u + 1)
                    ln_stats(next_ln, u)
                if 0 <= t - 3 < NT and next_ln != 4:
                    ln_lo(next_ln, t - 3)
                if f.index == 0 and t == 8:
                    low_wq(9)
                if f.index == 1 and t == 8:
                    ctx_max(0)
                    ln_norm(4, 0)
                if f.index == 1 and t == NT + 2:
                    dve.wait_ge(ld["vec_hi"], 1)
                    for r in bias_row.values():
                        i = sub_hi(pT[r:r + 1, LO], wide[r:r + 1], pT[r:r + 1, HI])
                    i.then_inc(ld["vec_lo"], 1)
                if f.index == 2 and t == 8 :
                    mean_square("f", 0, 6, 0)
                    features(0)

        def ctx_max(n):
            dve.wait_ge(ld[f"c{n % 4}"], (n // 4 + 1) * 16)
            link(V.tensor_reduce(mx[:, 0:1], stage_q[:, n % 4], AX.X, ALU.max))
            V.tensor_scalar(small[:, 8 + n % 2:9 + n % 2], mx[:, 0:1], -1.0, None, ALU.mult).then_inc(M["k_max"], 1)

        def linear_attention(next_ln):
            s = M
            by8 = lambda ap: ap.rearrange("p (g e) -> p g e", e=8)
            group = k_sb[:, 0:S]

            dve.wait_ge(setup["b8"], 3)
            for t in range(NT + 4):
                u = t - 2
                if 0 <= t - 3 < NT:
                    ln_norm(next_ln, t - 3)
                if 0 <= u < NT:
                    dve.wait_ge(s["out"], u + 1)
                    V.tensor_tensor(x[:, u], x[:, u], psY[:], ALU.add).then_inc(s["x_add"], 1)
                if 0 <= t - 1 < NT:
                    dve.wait_ge(s["kv"], t)
                    link(V.reciprocal(small[:, 12:13], small[:, 10 + (t - 1) % 2:11 + (t - 1) % 2]))
                    V.scalar_tensor_tensor(kvs, psKV[:, 0:P], small[:, 12:13], block8[:], ALU.mult,
                                           ALU.mult).then_inc(s["kvs"], 1)
                if 0 <= u < NT:
                    dve.wait_ge(s["x_add"], u + 1)
                    ln_stats(next_ln, u)
                if t < NT:
                    dve.wait_ge(LNS[4]["tr"], ln_at(4, t + 1))
                    link(V.tensor_reduce(group, by8(psT[:]), AX.X, ALU.max))
                    V.tensor_tensor(by8(q_sb[:]), by8(psT[:]), group.unsqueeze(2).to_broadcast([P, S, 8]),
                                    ALU.subtract).then_inc(s["q_shift"], 1)
                if 0 <= t - 1 < NT:
                    dve.wait_ge(s["kvs_hi"], t)
                    sub_hi(kvs_r[:, (t - 1) % 2, LO], kvs, kvs_r[:, (t - 1) % 2, HI]).then_inc(s["kvs_lo"], 1)
                if t < NT:
                    dve.wait_ge(s["eT_hi"], t + 1)
                    sub_hi(eT[:, LO], slices(psS), eT[:, HI]).then_inc(s["eT_lo"], 1)
                if 0 <= t - 1 < NT:
                    dve.wait_ge(s["q2_hi"], t)
                    sub_hi(q2[:, LO], psP[:], q2[:, HI]).then_inc(s["q2_lo"], 1)
                if t < NT:
                    dve.wait_ge(s["q_exp"], t + 1)
                    link(V.tensor_reduce(group, by8(q_sb[:]), AX.X, ALU.add))
                    link(V.reciprocal(group, group))
                    need(dve, s["q_tr"], t)
                    V.tensor_tensor(by8(prob[:]), by8(q_sb[:]), group.unsqueeze(2).to_broadcast([P, S, 8]),
                                    ALU.mult).then_inc(s["q_soft"], 1)
                if t + 1 < NT:
                    ctx_max(t + 1)
                    ln_norm(4, t + 1)
                if 0 <= t - 3 < NT:
                    ln_lo(next_ln, t - 3)
                if t == 4:
                    low_wq(18, stage_o)

        def cross_attention(next_ln):
            s = N3
            def f_lo(n):
                dve.wait_ge(s["f_hi"], n + 1)
                sub_hi(f_r[:, n % 3, LO], stage_q[:, n % 4], f_r[:, n % 3, HI]).then_inc(s["f_lo"], 1)

            def fT_lo(n):
                dve.wait_ge(s["fT_hi"], n + 1)
                sub_hi(fT[:, LO], slices(psS), fT[:, HI]).then_inc(s["fT_lo"], 1)

            link(V.memset(s_sb[:, 0:P], 0.0))
            f_lo(0)
            fT_lo(0)
            for t in range(NT + 4):
                u = t - 1
                if 0 <= u < NT:
                    mean_square("q", u, 8, 4)
                    dve.wait_ge(s["kT_hi"], u + 1)
                    sub_hi(kT3[:, LO], slices(k3w), kT3[:, HI]).then_inc(s["kT_lo"], 1)
                if t + 1 < NT:
                    mean_square("f", t + 1, 6, 0)
                if 0 <= u < NT:
                    dve.wait_ge(s["pw_q"], u + 1)
                    link(V.tensor_scalar(col(9), col(5), D ** -0.5, None, ALU.mult))
                if 0 <= t - 3 < NT:
                    ln_norm(next_ln, t - 3)
                if t + 1 < NT:
                    features(t + 1)
                if t < NT:
                    mean_square("k", t, 7, 2)
                if 0 <= u < NT:
                    dve.wait_ge(s["qT_hi"], u + 1)
                    sub_hi(qT3[:, LO], slices(psT), qT3[:, HI]).then_inc(s["qT_lo"], 1)
                if 0 <= t - 2 < NT:
                    dve.wait_ge(s["attend"], t - 1)
                    V.tensor_tensor(x[:, t - 2], x[:, t - 2], psY[:], ALU.add).then_inc(s["x_add"], 1)
                    dve.wait_ge(s["x_add"], t - 1)
                    ln_stats(next_ln, t - 2)
                if 0 <= t - 4 < NT:
                    hits_of(t - 4)
                if 0 <= u < NT:
                    dve.wait_ge(s["scores"], u + 1)
                    for b in range(2):
                        rows = slice(b * S, (b + 1) * S)
                        i = V.tensor_reduce(mx[rows, 0:1], psO[rows, 0, rows], AX.X, ALU.max)
                    link(i)
                    V.tensor_scalar(col(10), mx[:, 0:1], col(9), -1.0, ALU.mult, ALU.mult).then_inc(s["neg_max"], 1)
                if t + 1 < NT:
                    f_lo(t + 1)
                if 0 <= u < NT:
                    dve.wait_ge(s["exp"], u + 1)
                    link(V.reciprocal(col(12), col(11)))
                    V.tensor_scalar(s_sb[:, 0:P], s_sb[:, 0:P], col(12), None, ALU.mult).then_inc(s["prob"], 1)
                if 0 <= t - 3 < NT:
                    ln_lo(next_ln, t - 3)
                if t + 1 < NT:
                    fT_lo(t + 1)
                if 0 <= u < NT:
                    dve.wait_ge(s["pT_hi"], u + 1)
                    sub_hi(pT3[:, LO], psO[:, 1, 0:P], pT3[:, HI]).then_inc(s["pT_lo"], 1)
                if t < NT:
                    dve.wait_ge(s["k_tr"], t + 1)
                    V.tensor_tensor(slices(k3w), slices(psP), wqk3[:, 2].unsqueeze(2).to_broadcast([P, KT, P]),
                                    ALU.mult).then_inc(s["kw"], 1)
                if t == NT:
                    low_wq(19, stage_o)

        def hits_of(n):
            s = C3
            dve.wait_ge(s["sim"], n + 1)
            link(V.tensor_reduce(mx[:, 1:2], psO[:, 1, P:P + 64], AX.X, ALU.max))
            V.tensor_scalar(small[:, 13:14], mx[:, 1:2], -1.0 / TEMPERATURE, None, ALU.mult).then_inc(s["neg_max"], 1)
            dve.wait_ge(s["exp"], n + 1)
            link(V.reciprocal(small[:, 15:16], small[:, 14:15]))
            V.tensor_scalar(hit(n), hit_exp[:], small[:, 15:16], THRESHOLD, ALU.mult, ALU.is_gt).then_inc(s["hits"], 1)
            dve.wait_ge(s["hits"], n + 1)
            link(V.tensor_reduce(q_any[:, n:n + 1], hit(n).bitcast(f32), AX.X, ALU.max))

        def clustered():
            s = C3
            dve.wait_ge(ld["asg_in"], 16)
            V.tensor_scalar(prob[0:64], q_sb[0:64].bitcast(i32), row_id[0:64], None, ALU.is_equal)
            dve.wait_ge(s["count"], 1)
            link(V.tensor_scalar(small[0:64, 0:1], psO[0:64, 0, 0:1], 0.5, None, ALU.is_ge))
            V.tensor_scalar(s_sb[0:64, 0:P], ones[0:64, :], small[0:64, 0:1], None, ALU.mult).then_inc(s["sel"], 1)
            dve.wait_ge(s["rows"], 1)
            link(V.tensor_copy(wide[:], psT[:]))
            for t in range(NT):
                dve.wait_ge(s["dense"], t + 1)
                need(dve, s["out"], t - 1)
                kept = (xn[:, 1], prob[:])[t % 2]
                V.scalar_tensor_tensor(kept, dense_bank(t)[:], q_any[:, t:t + 1], wide[:], ALU.mult,
                                       ALU.mult).then_inc(s["masked"], 1)
                dve.wait_ge(s["masked"], t + 1)
                V.tensor_tensor(x[:, t], x[:, t], kept, ALU.add).then_inc(s["out"], 1)

        x_stats(0)
        x_stats(1)
        ln_norm(0, 0)
        ln_norm(0, 1)
        low_wq(0)
        ln_lo(0, 0)
        low_ctx(0)
        ln_lo(0, 1)
        x_stats(2)
        x_stats(3)
        attention(L0, 1)
        ffn(FF[0], 2)
        attention(L1, 3)
        ffn(FF[1], 4)
        linear_attention(5)
        ffn(FF[2], 6)
        cross_attention(7)
        clustered()

    block_cm.__exit__(None, None, None)


def arrays_of(inputs):
    import numpy as np
    f = {k: np.asarray(a) for k, a in inputs.items()}
    c = np.ascontiguousarray

    def by_slice(w):
        return c(w.reshape(KT, P, -1).transpose(1, 0, 2))

    def head_groups(w):
        return c(w.reshape(KT, P, NHG, D).transpose(2, 1, 0, 3))

    def out_groups(w):
        return c(w.reshape(NHG, HQ, P, D).transpose(0, 2, 1, 3))

    def kv_groups(wk, wv, n):
        both = np.concatenate([wk.reshape(KT, P, n, HD), wv.reshape(KT, P, n, HD)], axis=3)
        return c(both.transpose(2, 1, 0, 3).reshape(n, P, 2, 512))

    a = {}
    a["x"] = c(f["x"].reshape(NT, P, D).transpose(1, 0, 2))
    a["ctxT"] = c(f["ctx_4096"].reshape(2, 512, KT, P).transpose(0, 3, 2, 1))
    a["wq0"] = head_groups(f["L0_xattn_Wq"])
    a["wo0"] = out_groups(f["L0_xattn_Wo"])
    a["wkv0"] = kv_groups(f["L0_xattn_Wk"], f["L0_xattn_Wv"], 4)
    a["wq1"] = head_groups(f["L1_xattn_Wq"].T)
    a["wo1"] = out_groups(f["L1_xattn_Wo"].T)
    a["wkv1"] = kv_groups(f["L1_xattn_Wk"].T, f["L1_xattn_Wv"].T, NHG)
    a["mask"] = c(f["mask_1x1xSxS2_ff0"].reshape(S, S))

    def two_slices(w):
        return c(w.reshape(2, 2, P, -1).transpose(2, 0, 1, 3).reshape(P, 2, -1))

    def gate_a(gate, lora_a):
        return two_slices(np.concatenate([gate, lora_a.reshape(-1, D)]).T)

    def ranks(lora_b):
        return lora_b.transpose(0, 2, 1).reshape(-1, D)

    a["ga0"] = gate_a(f["L0_ffn_gate_W"], f["L0_ffn_lora_A"])
    a["ga1"] = gate_a(f["L1_ffn_gate_W"], f["L1_ffn_A"])
    a["ga2"] = gate_a(f["L2_ffn_router_w"], f["L2_ffn_A"])
    a["cent"] = two_slices(f["L3_ffn_centroids"].T)
    a["base0"], a["base1"] = by_slice(f["L0_ffn_base_W"].T), by_slice(f["L1_ffn_W_base"].T)
    a["wq3"], a["wk3"] = by_slice(f["L3_xattn_Wq_w"].T), by_slice(f["L3_xattn_Wk_w"].T)
    a["w3"] = by_slice(f["L3_ffn_weight"].T)
    a["b0"] = c(ranks(f["L0_ffn_lora_B"]).reshape(2, 112, D).transpose(1, 0, 2))
    a["b1"], a["b2"] = (c(ranks(f[n])[:, None]) for n in ("L1_ffn_B", "L2_ffn_B"))
    a["ctx"] = c(f["ctx_4096"].reshape(NT, P, D).transpose(1, 0, 2))
    a["qn1"], a["kn1"] = f["L1_xattn_q_norm_w"].reshape(P, 1), f["L1_xattn_k_norm_w"].reshape(P, 1)
    a["qn3"], a["kn3"] = (c(f[n].reshape(KT, P).T) for n in ("L3_xattn_qn_w", "L3_xattn_kn_w"))
    for name, n in (("bq3", "L3_xattn_Wq_b"), ("bk3", "L3_xattn_Wk_b"), ("bias3", "L3_ffn_bias"),
                    ("fn_w", "L3_xattn_fn_w"), ("asg", "L3_ffn_assignments")):
        a[name] = f[n].reshape(1, D)
    return a


def kernel(**inputs):
    import concourse.bacc as bacc
    from concourse.bass_utils import run_bass_kernel_spmd

    nc = bacc.Bacc("TRN2", target_bir_lowering=False, num_devices=1)
    arrays, io = {}, {}
    for name, a in arrays_of(inputs).items():
        arrays["in_" + name] = a
        io[name] = nc.dram_tensor("in_" + name, a.shape, mybir.dt.from_np(a.dtype), kind="ExternalInput").ap()
    io["out"] = nc.dram_tensor("out", (P, NT, D), mybir.dt.float32, kind="ExternalOutput").ap()
    build(nc, io)
    got = run_bass_kernel_spmd(nc, [arrays], core_ids=[0]).results[0]["out"]
    return got.transpose(1, 0, 2).reshape(B, S, D)
```

```python
import concourse.bass as bass
from concourse import mybir


P = 128
B, S, D = 16, 64, 512
TOK = B * S
NT = TOK // P
KT = D // P
HD = 128
HQ = 4
NHG = 32 // HQ
STEPS = NHG * NT
TEMPERATURE, THRESHOLD = 0.1, 0.01
LN_SLOT = STEPS - 4
LN_EPS = 1e-5
RMS_EPS, RMS_EPS3 = 1e-5, 1e-6
HI, LO = 0, 1
PASSES = ((HI, HI), (HI, LO), (LO, HI))


class Step:

    def __init__(self, base, n, i=None, unroll=0, done=0):
        self.base, self.n, self.i, self.unroll = base, n, i, unroll
        self.done = done

    @property
    def c(self):
        at = self.base + self.done
        return at if self.i is None else self.i * self.unroll + at

    @property
    def t(self):
        return self.base if self.i is None else self.i * self.unroll + self.base

    @property
    def exists(self):
        return self.i is not None or 0 <= self.base < self.n

    @property
    def static(self):
        return self.i is None

    def back(self, k):
        return Step(self.base - k, self.n, self.i, self.unroll, self.done)

    def res(self, m):
        return self.base % m

    def div(self, m):
        q = self.base // m
        return q if self.i is None else self.i * (self.unroll // m) + q


def steps(eng, n, unroll, lead, done):
    loops = (n - lead - NT) // unroll
    for t in range(lead):
        yield Step(t, n, done=done)
    with eng.Fori(0, loops) as i:
        for t in range(lead, lead + unroll):
            yield Step(t, n, i, unroll, done)
    for t in range(lead + loops * unroll, n + 1):
        yield Step(t, n, done=done)


def need(eng, sem, value):
    if isinstance(value, int) and value <= 0:
        return
    eng.wait_ge(sem, value)


class Sems:

    def __init__(self, nc, layer):
        self._nc, self._layer, self._of = nc, layer, {}

    def __getitem__(self, what):
        if what not in self._of:
            self._of[what] = self._nc.alloc_semaphore(f"{self._layer}_{what}")
        return self._of[what]


def build(nc, io):
    f32, f32r, i32, u32 = mybir.dt.float32, mybir.dt.float32r, mybir.dt.int32, mybir.dt.uint32
    ALU, ACT, AX = mybir.AluOpType, mybir.ActivationFunctionType, mybir.AxisListType
    sb = lambda name, shape, dt=f32: nc.alloc_sbuf_tensor(name, [P, *shape], dt)
    ps = lambda name, shape: nc.alloc_psum_tensor(name, [P, *shape], f32)

    x = sb("x_res", [NT, D])
    hT = sb("hT", [2, KT, NT, 4, S], f32r)
    wq = sb("wq", [2, KT, D], f32r)
    wo = sb("wo", [2, KT, D], f32r)
    wkv = sb("wkv", [2, 2, D], f32r)
    stage_q = sb("stage_q", [KT, D])
    stage_o = sb("stage_o", [KT, D])
    stage_kv = sb("stage_kv", [2, D])
    arena = sb("arena", [8192], f32r)
    half = lambda n: arena[:, n * 4096:(n + 1) * 4096].rearrange("p (n h c) -> p n h c", n=NT, h=2)
    kT0, v0 = half(0), half(1)
    ctxT = arena[:].rearrange("p (h k t) -> p h k t", h=2, k=KT)
    kT1 = sb("kT1", [4, 2, HD], f32r)
    v1 = sb("v1", [4, 2, HD], f32r)
    q_sb = sb("q_sb", [D])
    k_sb = sb("k_sb", [2 * HD])
    qT = sb("qT", [2, 2, HQ, S], f32r)
    pair = lambda t, dims: t[:].rearrange(f"p {dims} -> p ({dims})").rearrange(
        "p (l n b h t) -> p l n b h t", l=2, n=2, b=2, h=2)
    q01, q23 = (pair(kT1, "a l c"), pair(v1, "a l c")), pair(qT, "l b h t")
    s_sb = sb("s_sb", [2 * P])
    prob = sb("prob", [D])
    pT = sb("pT", [2, D], f32r)
    oT = sb("oT", [2, HQ, P], f32r)
    xn = sb("xn", [2, D])
    ident = sb("ident", [P])
    minus_half = sb("minus_half", [8])
    bn = sb("bn", [2, 6])
    mv = sb("mv", [NT, 2])
    var_eps = sb("var_eps", [NT])
    rstd = sb("rstd", [NT])
    mx = sb("mx", [4])
    neg_mx = sb("neg_mx", [4])
    sums = sb("sums", [4])
    rsums = sb("rsums", [4])
    ssq = sb("ssq", [2, 5])
    ms_eps = sb("ms_eps", [2, 5])
    rms = sb("rms", [2, 5])
    mask = sb("mask", [S])
    wqk = sb("wqk", [3])
    wqk3 = sb("wqk3", [3, KT])
    wide = sb("wide", [D])
    ones = sb("ones", [P])
    ones_r = sb("ones_r", [P], f32r)
    iota = sb("iota", [32])
    row_id = sb("row_id", [1])
    block8 = sb("block8", [P])
    logits = sb("logits", [32])
    top = sb("top", [8])
    top_at = sb("top_at", [8], u32)
    top_f = sb("top_f", [2])
    pick = sb("pick", [2, 32])
    gate = sb("gate", [32])
    small = sb("small", [16])
    q_any = sb("q_any", [NT])

    psQ, psKV, psT, psP, psY = (ps(n, [D]) for n in ("psQ", "psKV", "psT", "psP", "psY"))
    psSO = ps("psSO", [3, D])
    psS, psO, psS0, psO0 = psSO[:, 0], psSO[:, 1:3], psSO[:, 0:2], psSO[:, 2]

    setup = Sems(nc, "setup")
    ld = Sems(nc, "ld")
    A = Sems(nc, "attn")
    ln_even, ln_odd = Sems(nc, "ln_even"), Sems(nc, "ln_odd")
    LNS = [ln_even, ln_odd, ln_even, ln_odd, Sems(nc, "ln_l2"), ln_odd, ln_even, ln_odd]
    out_done = nc.alloc_semaphore("out_done")

    FS = Sems(nc, "ffn")
    M, N3, C3 = Sems(nc, "m2"), Sems(nc, "a3"), Sems(nc, "c3")
    chain = nc.alloc_semaphore("dve_chain")

    def ln_at(ln, n):
        return sum(other is LNS[ln] for other in LNS[:ln]) * NT + n

    class Ffn:

        def __init__(self, index, ln, E, R, dense, scale, wkv_n, wo_n):
            self.index, self.ln, self.E, self.R = index, ln, E, R
            self.done = index * NT
            self.dense, self.scale = dense, scale
            self.width = E + E * R
            self.parts = 2 if E * R > P else 1
            self.rows = E * R // self.parts
            self.wkv_n, self.wo_n = wkv_n, wo_n

    FF = [Ffn(0, 1, 28, 8, True, 2.0, 10, 34), Ffn(1, 3, 8, 8, True, 2.0, 28, 67), Ffn(2, 5, 4, 16, False, 4.0, 30, 68)]
    WQ_DENSE = [8, 17]

    class Attn:
        def __init__(self, index):
            self.index = index
            self.done, self.kv_done = (0, 0) if index == 0 else (STEPS, STEPS // 2)
            self.rms = index == 1
            self.lead = NT if index == 0 else NT // 2
            self.keys = 2 * S if index == 0 else S
            self.unroll = 2 * NT if index == 0 else NT
            self.kv_period = self.unroll
            self.kT, self.v, self.ring = (kT0, v0, NT) if index == 0 else (kT1, v1, 4)
            self.wq0, self.wo0, self.wkv0 = (0, 0, 0) if index == 0 else (9, 34, 10)

        def norm_slot(self, st):
            if not (st.static and st.t >= LN_SLOT):
                return None
            return "last" if st.t >= STEPS - (not self.rms) else "between"

        def kv_new(self, st):
            return st.exists and st.res(self.kv_period) < NT

        def kv_n(self, st):
            return st.div(self.kv_period) * NT + (st.res(NT) + self.kv_done)

        scale = HD ** -0.5

    L0, L1 = Attn(0), Attn(1)

    def heads(ap):
        return ap.rearrange("p (h b t) -> p b h t", h=HQ, b=2)

    def tok(n):
        return slice(n * P, (n + 1) * P)

    def lat(hl, k, n):
        return hT[:, hl, k, n, 1:3].rearrange("p b t -> p (b t)")

    def lat_pair(hl, k, pair):
        return hT[:, hl, k, 2 * pair:2 * pair + 2, 1:3].rearrange("p n b t -> p n (b t)")

    def lat_all(hl, n):
        return hT[:, hl, :, n, 1:3].rearrange("p k b t -> p k (b t)")

    def o_banks(a):
        if a.index == 0:
            return psO0.rearrange("p (b h t) -> p b h t", b=2, h=HQ)
        return psO[:, :, 0:256].rearrange("p b (h t) -> p b h t", h=HQ)

    def two_by_two(t):
        return t[:].rearrange("p (b j c) -> p b j c", b=2, j=2)

    def score_parts(hl):
        return psS0.rearrange("p b (j h c) -> p h b j c", j=2, h=2)[:, hl]

    def slices(bank):
        return bank[:].rearrange("p (k t) -> p k t", k=KT)

    def hidden(hl, k, n, b):
        return hT[:, hl, k, n, 2 * b:2 * b + 2].rearrange("p b t -> p (b t)")

    def ctx_part(hl, k, half):
        return hT[:, hl, k, half * 4:half * 4 + 4, 0:4:3, :]

    def unit_bank(k):
        return (psQ, psT)[k.res(2)]

    def unit_buffer(k):
        return q23 if k.res(2) else q01[k.res(4) // 2]

    def unit_in(hl, k):
        return unit_buffer(k)[:, hl].rearrange("p n b h t -> p h (n b) t")

    def unit_out(k):
        return unit_bank(k)[:].rearrange("p (h x t) -> p h x t", h=2, t=S)

    def units_of(st):
        first = [st] if st.static and st.t == 0 else []
        return first + [st.back(-1)] * st.back(-1).exists

    def first_norms(t):
        return range(2 * t + 2, 2 * t + 4) if t < 2 else range(t + 4, min(t + 5, NT))

    def xn_slot(ln, n):
        return {4: 0, 5: 1}.get(ln, n % 2)

    def ln_bank(ln, n):
        if ln == 0 and n in (0, 3, 5):
            return psY
        if ln in (1, 3):
            return psT if n == NT - 1 else psP
        return {0: psP, 5: psQ}.get(ln, psT)

    def gate_bank(f, n):
        return psSO[:, 1] if f.index == 2 and n % 2 else psQ

    def ring3(n):
        return (psS, psKV, psY)[n % 3]

    eT, q2, kvs_r = (kT1[:].rearrange("p a h c -> p (a h c)").rearrange("p (h k c) -> p h k c", h=2, k=KT),
                     qT[:].rearrange("p h b g t -> p h (b g t)"),
                     v1[:].rearrange("p a h c -> p (a h c)").rearrange("p (a h c) -> p a h c", a=4, h=2))
    hidT = oT
    def cut(at, *shape):
        size, names = 1, "abc"[:len(shape)]
        for x_ in shape:
            size *= x_
        v_ = arena[:, at:at + size]
        return v_.rearrange(f"p ({' '.join(names)}) -> p {' '.join(names)}", **dict(zip(names, shape)))
    f_r, fT, kT3, qT3, pT3 = cut(0, 3, 2, D), cut(3072, 2, KT, P), cut(4096, 2, KT, P), cut(5120, 2, KT, P), cut(6144, 2, P)
    k3, k3w = prob, prob
    kvs = k_sb[:, HD:2 * HD]
    junk_k = prob[:, 3 * HD:4 * HD]
    junk_q = [pT[:, h // 2, (2 + h % 2) * HD:(3 + h % 2) * HD] for h in range(HQ)]
    junk_f3, junk_k3, junk_q3 = (t[:, a:a + 2].rearrange("p a h c -> p (a h c)") for t, a in ((kT1, 0), (kT1, 2), (v1, 0)))
    hit_exp = mask
    hits = v1[:, 2:4].rearrange("p a h c -> p (a h c)")

    def hit(n):
        return hits[:, n * 64:(n + 1) * 64]

    def dense_bank(n):
        return (psQ, psKV, psS, psP, psY)[n % 5]

    bias_row = {"q": 0, "k": 32, "o": 64}

    def wkv_k(hl, k, width):
        return wkv[:, hl, k // 2, (k % 2) * width:(k % 2 + 1) * width]

    block_cm = nc.Block()
    block = block_cm.__enter__()

    @block.sync
    def _(sp):
        def load(what, stage, src, split_before):
            sp.wait_ge(ld[what + "_lo"], split_before)
            sp.dma_start(stage, src).then_inc(ld[what + "_in"], 16)

        def load_wq(src, loads_before):
            need(sp, ld["wq_lo"], loads_before * 2)
            need(sp, ld["wq_lo_v"], loads_before * 2)
            sp.dma_start(stage_q[:], src).then_inc(ld["wq_in"], 16)

        for n in range(2):
            sp.dma_start(x[:, n], io["x"][:, n]).then_inc(ld[f"x{n}"], 16)
        load_wq(io["wq0"][0], 0)
        sp.dma_start(stage_o[:], io["ctxT"][0]).then_inc(ld["ctx_in"], 16)
        sp.dma_start(stage_kv[:], io["wkv0"][0]).then_inc(ld["wkv_in"], 16)
        sp.dma_start(x[:, 2:NT], io["x"][:, 2:NT]).then_inc(ld["x_rest"], 16)
        for b in range(2):
            sp.dma_start(mask[b * S:(b + 1) * S], io["mask"]).then_inc(ld["small"], 16)
        for c, what in enumerate(("qn1", "kn1")):
            sp.dma_start(wqk[:, c:c + 1], io[what]).then_inc(ld["small"], 16)
        for c, what in enumerate(("qn3", "kn3")):
            sp.dma_start(wqk3[:, c], io[what]).then_inc(ld["small"], 16)

        for half in range(2):
            sp.wait_ge(ld["ctx_lo"], half * 2 + 2)
            sp.wait_ge(ld["ctx_lo_v"], half * 2 + 2)
            if half == 0:
                sp.dma_start(stage_o[:], io["ctxT"][1]).then_inc(ld["ctx_in"], 16)
        sp.dma_start(stage_o[:], io["wo0"][0]).then_inc(ld["wo_in"], 16)
        with sp.Fori(0, 3) as kv:
            load_wq(io["wq0"][kv * 2 + 1], kv * 2 + 1)
            load("wkv", stage_kv[:], io["wkv0"][kv + 1], kv * 2 + 2)
            load("wo", stage_o[:], io["wo0"][kv * 2 + 1], kv * 8 + 4)
            load_wq(io["wq0"][kv * 2 + 2], kv * 2 + 2)
            load("wo", stage_o[:], io["wo0"][kv * 2 + 2], kv * 8 + 8)
        load_wq(io["wq0"][7], 7)
        load("wo", stage_o[:], io["wo0"][7], 28)
        load("wkv", stage_kv[:, :, 0:504], io["ga0"], 8)
        load_wq(io["base0"], 8)
        load("wo", stage_o[0:112, 0:2], io["b0"], 32)
        load("wkv", stage_kv[:], io["wkv1"][0], 10)
        load_wq(io["wq1"][0], 9)
        load("wo", stage_o[:], io["wo1"][0], 34)
        with sp.Fori(1, NHG) as hg:
            load("wkv", stage_kv[:], io["wkv1"][hg], hg * 2 + 10)
            load_wq(io["wq1"][hg], hg + 9)
            load("wo", stage_o[:], io["wo1"][hg], hg * 4 + 34)
        load("wkv", stage_kv[:, :, 0:144], io["ga1"], 26)
        load_wq(io["base1"], 17)
        load("wo", stage_o[0:64, 0:1], io["b1"], 66)
        sp.wait_ge(A["exp"], STEPS)
        for c, what in enumerate(("bq3", "bk3", "bias3")):
            sp.dma_start(wide[32 * c:32 * c + 1], io[what]).then_inc(ld["vec_in"], 16)
        sp.wait_ge(ld["wq_lo"], 36)
        sp.wait_ge(ld["wq_lo_v"], 36)
        for n in range(2 * NT):
            if n == 4:
                load("wkv", stage_kv[:, :, 0:136], io["ga2"], 28)
                load("wo", stage_o[0:64, 0:1], io["b2"], 67)
                load("wo", stage_o[:], io["wq3"], 68)
            if n == NT:
                sp.wait_ge(ld["wq_lo"], 38)
                sp.wait_ge(ld["wq_lo_v"], 38)
                sp.dma_start(stage_o[:], io["wk3"]).then_inc(ld["wo_in"], 16)
                load("wkv", stage_kv[:, :, 0:128], io["cent"], 30)
                sp.wait_ge(ld["vec_lo"], 1)
                sp.dma_start(wide[:], io["fn_w"].to_broadcast([P, D])).then_inc(ld["fn_in"], 16)
            if n >= 4:
                if n - 4 < NT:
                    sp.wait_ge(M["e_tr"], n - 3)
                else:
                    sp.wait_ge(N3["f_lo"], n - 4 - NT + 1)
                    sp.wait_ge(N3["f_tr"], n - 4 - NT + 1)
            sp.dma_start(stage_q[:, n % 4], io["ctx"][:, n % NT]).then_inc(ld[f"c{n % 4}"], 16)
        load("wo", stage_o[:], io["w3"], 72)
        sp.wait_ge(N3["q_tr"], NT)
        sp.dma_start(q_sb[0:64].bitcast(i32), io["asg"].to_broadcast([64, D])).then_inc(ld["asg_in"], 16)
        for n in range(NT):
            sp.wait_ge(C3["out"], n + 1)
            sp.dma_start(io["out"][:, n], x[:, n]).then_inc(out_done, 16)
        sp.wait_ge(out_done, 16 * NT)
    @block.gpsimd
    def _(pool):
        g = nc.gpsimd
        g.memset(minus_half[:], -0.5).then_inc(setup["const"], 1)
        g.memset(ident[:], 0.0).then_inc(setup["const"], 1)
        pool.wait_ge(setup["const"], 2)
        g.affine_select(out=ident[:], in_=ident[:], compare_op=ALU.not_equal, fill=1.0, base=0,
                        pattern=[[-1, P]], channel_multiplier=1).then_inc(setup["const"], 1)

        def low(what, dst, stage, hi_count):
            pool.wait_ge(ld[what + "_hi"], hi_count)
            g.tensor_tensor(dst[LO], stage, dst[HI].bitcast(f32), ALU.subtract).then_inc(ld[what + "_lo"], 1)

        def low_ctx(half):
            for k in range(2):
                low("ctx", (ctx_part(HI, k, half), ctx_part(LO, k, half)),
                    stage_o[:, k].rearrange("p (n b t) -> p n b t", n=4, b=2), half * 4 + k + 1)

        def halves(t, *at):
            return t[(slice(None), HI, *at)], t[(slice(None), LO, *at)]

        def ln_rstd(ln, n):
            pool.wait_ge(LNS[ln]["var"], ln_at(ln, n + 1))
            g.tensor_tensor(rstd[:, n:n + 1], var_eps[:, n:n + 1], minus_half[:, 0:1],
                            ALU.pow).then_inc(LNS[ln]["rstd"], 1)

        def ln_norm(ln, n):
            s = LNS[ln]
            pool.wait_ge(s["rstd"], ln_at(ln, n + 1))
            need(pool, s["tr"], ln_at(ln, n))
            g.tensor_scalar(xn[:, xn_slot(ln, n)], x[:, n], mv[:, n, 0:1], rstd[:, n:n + 1], ALU.subtract,
                            ALU.mult).then_inc(s["xn"], 1)

        g.memset(ones[:], 1.0).then_inc(setup["ones"], 1)
        g.iota(iota[:], [[1, 32]], base=0, channel_multiplier=0,
               allow_small_or_imprecise_dtypes=True).then_inc(setup["iota"], 1)
        g.iota(row_id[:], [[0, 1]], base=0, channel_multiplier=1,
               allow_small_or_imprecise_dtypes=True).then_inc(setup["iota"], 1)
        g.memset(block8[:], 1.0).then_inc(setup["b8"], 1)
        groups = block8[:].rearrange("p (g e) -> p g e", e=8)
        pool.wait_ge(setup["b8"], 1)
        g.affine_select(out=groups, in_=groups, compare_op=ALU.is_ge, fill=0.0, base=0,
                        pattern=[[-8, 16], [0, 8]], channel_multiplier=1).then_inc(setup["b8"], 1)
        pool.wait_ge(setup["b8"], 2)
        g.affine_select(out=groups, in_=groups, compare_op=ALU.is_ge, fill=0.0, base=7,
                        pattern=[[8, 16], [0, 8]], channel_multiplier=-1).then_inc(setup["b8"], 1)


        def low_wq(load, stage=stage_q):
            for k in range(2):
                low("wq", halves(wq, k), stage[:, k], load * 4 + (k + 1))

        def low_wo(count, n=KT):
            for k in range(n):
                low("wo", halves(wo, k), stage_o[:, k], count + k + 1)

        def low_wkv(count, width=D):
            for k in range(2):
                low("wkv", halves(wkv, k, slice(0, width)), stage_kv[:, k, 0:width], count + k + 1)

        ln_rstd(0, 0)
        ln_rstd(0, 1)
        low_wq(0)
        low_ctx(0)
        low_wkv(0)
        for n in range(2, NT):
            ln_rstd(0, n)
            if n == 5:
                low_ctx(1)
            if n == 6:
                low_wo(0)
        with pool.Fori(0, 3) as kv:
            low_wq(kv * 2 + 1)
            low_wo(kv * 8 + 4)
            low_wkv(kv * 2 + 2)
            low_wq(kv * 2 + 2)
            low_wo(kv * 8 + 8)
        low_wq(7)
        low_wo(28)
        for n in range(NT):
            ln_rstd(1, n)
            if n == 0:
                low_wkv(8, 504)
            if n == 3:
                low_wq(8)

        def power(what, n, col):
            pool.wait_ge(N3["ms_" + what], n + 1)
            g.tensor_tensor(small[:, col + 1:col + 2], small[:, col:col + 1], minus_half[:, 0:1],
                            ALU.pow).then_inc(N3["pw_" + what], 1)

        def low_b(f, count):
            for j in range(f.parts):
                low("wo", (wo[0:f.rows, HI, j], wo[0:f.rows, LO, j]), stage_o[0:f.rows, j], count + j + 1)

        low_b(FF[0], 32)
        for n in range(NT):
            ln_rstd(2, n)
            if n == 6:
                low_wq(9)
                low_wkv(10)
        s = A
        for t in steps(pool, STEPS, L1.unroll, L1.lead, L1.done):
            if t.static and 0 <= t.t - LN_SLOT < NT:
                ln_rstd(3, t.t - LN_SLOT)
            if t.exists:
                pool.wait_ge(s["ms"], t.t + 1)
                need(pool, s["k_read"], t.t + L1.kv_done - 1)
                g.tensor_tensor(rms[:, t.res(2)], ms_eps[:, t.res(2)], minus_half[:, 0:5],
                                ALU.pow).then_inc(s["rms"], 1)
            if t.res(8) == 7 and t.exists:
                low_wq(t.div(8) + 10)
                if t.static and t.t == STEPS - 1:
                    low_wkv(26, 144)
                else:
                    low_wkv(t.div(8) * 2 + 12)
            if t.res(8) == 2 and not (t.static and t.t >= 64):
                low_wo(t.div(8) * 4 + 34)
        for n in range(5, NT):
            ln_rstd(3, n)
        low_b(FF[1], 66)
        for n in range(NT):
            ln_rstd(4, n)
        low_wkv(28, 136)
        low_b(FF[2], 67)
        for t in range(NT + 3):
            if 0 <= t - 3:
                ln_rstd(5, t - 3)
                ln_norm(5, t - 3)
            if t + 1 < NT:
                ln_norm(4, t + 1)
            if t == 5:
                low_wq(18, stage_o)
        for n in range(NT):
            if n == NT - 2:
                power("f", 0, 0)
            ln_rstd(6, n)
        for c, k in enumerate((1, 2, 3, 0)):
            low("wo", halves(wo, k), stage_o[:, k], 68 + c + 1)
        low_wkv(30, 128)
        for t in range(NT + 2):
            if 0 <= t - 1 < NT:
                power("q", t - 1, 4)
            if t + 1 < NT:
                power("f", t + 1, 0)
            if t < NT:
                power("k", t, 2)
            if 0 <= t - 2 < NT:
                ln_rstd(7, t - 2)
            if t == NT:
                low_wq(19, stage_o)

    @block.tensor
    def _(pe):
        mm, tr = nc.tensor.matmul, nc.tensor.transpose

        def wq_split(load, k):
            pe.wait_ge(ld["wq_lo" if k < 2 else "wq_lo_v"], load * 2 + (k % 2 + 1))

        def ln_transpose(ln, n, free):
            s = LNS[ln]
            pe.wait_ge(s["xn"], ln_at(ln, n + 1))
            free()
            for k in range(KT):
                i = tr(ln_bank(ln, n)[:, k * P:(k + 1) * P], xn[:, xn_slot(ln, n), k * P:(k + 1) * P], ident[:])
            i.then_inc(s["tr"], 1)

        def gate_product(f, t):
            s, done = FS, f.done
            pe.wait_ge(LNS[f.ln]["lo"], ln_at(f.ln, t + 1))
            need(pe, s["hid"], done + t - (f.index == 2))
            if t == 0:
                pe.wait_ge(ld["wkv_lo"], f.wkv_n)
                if f.ln == 5:
                    pe.wait_ge(LNS[f.ln]["lo"], ln_at(f.ln, NT))
            for k in range(KT):
                for i, (xl, wl) in enumerate(PASSES):
                    m = mm(gate_bank(f, t)[:, 0:f.width], lat(xl, k, t), wkv_k(wl, k, f.width),
                           start=k == 0 and i == 0, stop=k == KT - 1 and i == 2)
            m.then_inc(s["gate_a"], 1)

        def dense_product(f, t):
            s, done = FS, f.done
            pe.wait_ge(LNS[f.ln]["lo"], ln_at(f.ln, t + 1))
            need(pe, s["x_add"], done + t - 2)
            for k in range(KT):
                if t == 0:
                    wq_split(WQ_DENSE[f.index], k)
                for i, (xl, wl) in enumerate(PASSES):
                    m = mm(ring3(t)[:], lat(xl, k, t), wq[:, wl, k, :], start=k == 0 and i == 0, stop=False)
            m.then_inc(s["dense"], 1)

        def attention(a, next_ln):
            s, keys = A, a.keys

            def scores(u):
                pe.wait_ge(s["qT_lo"], u.c + (1 if a.rms else 2 - u.res(2)))
                if a.kv_new(u):
                    pe.wait_ge(s["kT_lo"], a.kv_n(u) + 1)
                if a.index == 0:
                    need(pe, s["added"], u.t)
                else:
                    need(pe, s["exp"], u.c)
                n = u.res(NT)
                for b in range(2):
                    for hp in range(2):
                        def q_of(hl):
                            of = (qT[:, hl, b, 2 * hp:2 * hp + 2, :] if a.rms else
                                  (q01[u.res(4) // 2], q23)[hp][:, hl, u.res(2), b])
                            return of.rearrange("p h t -> p (h t)")
                        k_of = lambda hl: a.kT[:, u.res(a.ring), hl, b * keys:(b + 1) * keys]
                        bank, at = (psS0[:, b], hp * 2 * keys) if a.index == 0 else (psS, (hp * 2 + b) * 2 * keys)
                        mm(bank[:, at:at + 2 * keys], q_of(HI), k_of(slice(0, 2)), start=True, stop=False)
                        m = mm(bank[:, at:at + keys], q_of(LO), k_of(HI), start=False, stop=True)
                m.then_inc(s["scores"], 1)

            def q_unit(k):
                need(pe, s["qT_lo"], k.t - 1)
                if k.static and k.t < NT:
                    pe.wait_ge(LNS[0]["lo"], ln_at(0, k.t // 2 * 2 + 2))
                for h in range(2):
                    head = slice((k.res(2) * 2 + h) * HD, (k.res(2) * 2 + h + 1) * HD)
                    out = unit_bank(k)[:, h * 256:(h + 1) * 256].rearrange("p (n t) -> p n t", n=2)
                    for c in range(KT):
                        if k.res(NT) == 0 and h == 0:
                            wq_split(k.div(NT) + a.wq0, c)
                        for i, (xl, wl) in enumerate(PASSES):
                            m = mm(out, wq[:, wl, c, head], lat_pair(xl, c, k.res(NT) // 2),
                                   start=c == 0 and i == 0, stop=c == KT - 1 and i == 2)
                m.then_inc(s["q_units"], 1)

            def q_proj(st, first, last):
                n = st.res(NT)
                if first == 0:
                    need(pe, s["q_read"], st.t)
                for k in range(first, last):
                    if n == 0:
                        wq_split(st.div(NT) + a.wq0, k)
                    if st.static and k == 0:
                        if st.t < a.lead:
                            pe.wait_ge(LNS[2]["lo"], ln_at(2, NT if st.t == a.lead - 1 else n + 1))
                    for i, (xl, wl) in enumerate(PASSES):
                        m = mm(psQ[:], lat(xl, k, n), wq[:, wl, k, :],
                               start=k == 0 and i == 0, stop=k == KT - 1 and i == 2)
                    m.then_inc(s["wq_used"], 1)

            def kv_proj(st):
                if st.static and st.t == 0 and a.index == 1:
                    pe.wait_ge(setup["ctxT"], 8)
                need(pe, s["kT_lo"], a.kv_n(st))
                need(pe, s["v_lo"], a.kv_n(st))
                n = st.res(NT)
                if n == 0:
                    pe.wait_ge(ld["wkv_lo"], st.div(a.kv_period) * 2 + (a.wkv0 + 2))
                if st.static and a.index == 0 and st.t < NT:
                    half = st.t // 4
                    pe.wait_ge(ld["ctx_lo"], half * 2 + 2)
                    pe.wait_ge(ld["ctx_lo_v"], half * 2 + 2)
                for b in range(2 if a.index == 0 else 1):
                    for k in range(KT):
                        for i, (xl, wl) in enumerate(PASSES):
                            lhsT = hidden(xl, k, n, b) if a.index == 0 else ctxT[:, xl, k, tok(n)]
                            m = mm(psKV[:, b * 256:(b + 1) * 256], lhsT, wkv_k(wl, k, 256),
                                   start=k == 0 and i == 0, stop=k == KT - 1 and i == 2)
                m.then_inc(s["kv"], 1)

            def q_transpose(st):
                pe.wait_ge(s["q_read"], st.t + 1)
                need(pe, s["qT_lo"], st.c)
                if st.static and st.t == 0:
                    pe.wait_ge(LNS[2]["lo"], ln_at(2, NT))
                for h in range(HQ):
                    i = tr(psT[:, h * P:(h + 1) * P], q_sb[:, h * P:(h + 1) * P], ident[:])
                i.then_inc(s["q_tr"], 1)

            def k_transpose(st):
                pe.wait_ge(s["k_read"], a.kv_n(st) + 1)
                pe.wait_ge(s["v_lo"], a.kv_n(st) + 1)
                for b in range(2 if a.index == 0 else 1):
                    i = tr(psKV[:, b * P:(b + 1) * P], k_sb[:, b * P:(b + 1) * P], ident[:])
                i.then_inc(s["k_tr"], 1)

            def p_transpose(u):
                pe.wait_ge(s["prob"], u.c + 1)
                need(pe, s["pT_lo"], u.c)
                if a.index == 0 and u.static and u.t < 3:
                    pe.wait_ge(LNS[0]["lo"], ln_at(0, first_norms(u.t + 1)[-1] + 1))
                if u.static and u.t + 2 > LN_SLOT:
                    pe.wait_ge(LNS[next_ln]["lo"], ln_at(next_ln, u.t + 2 - LN_SLOT))
                for j in range(4 * keys // P):
                    i = tr(psP[:, j * P:(j + 1) * P], prob[:, j * P:(j + 1) * P], ident[:])
                i.then_inc(s["p_tr"], 1)

            def attend(u):
                pe.wait_ge(s["pT_lo"], u.c + 1)
                need(pe, s["oT_lo"], u.c)
                n = u.res(NT)
                for b in range(2):
                    for i, (vl, pl) in enumerate(PASSES):
                        if a.index == 0:
                            lhsT, rhs = a.v[:, n, vl, b * HD:(b + 1) * HD], pT[:, pl, b * 256:(b + 1) * 256]
                        else:
                            rows = slice(b * S, (b + 1) * S)
                            lhsT, rhs = a.v[rows, u.res(a.ring), vl, 0:HD], pT[rows, pl, 0:256]
                        out = psO0[:, b * 256:(b + 1) * 256] if a.index == 0 else psO[:, b, 0:256]
                        m = mm(out, lhsT, rhs, start=i == 0, stop=i == 2)
                m.then_inc(s["pv"], 1)

            def out_proj(w, first, last):
                n = w.res(NT)
                if first == 0:
                    pe.wait_ge(s["oT_lo"], w.c + 1)
                    need(pe, s["x_add"], w.c)
                for h in range(first, last):
                    if n == 0:
                        pe.wait_ge(ld["wo_lo"], w.div(NT) * 4 + (a.wo0 + h + 1))
                    for i, (ol, wl) in enumerate(PASSES):
                        m = mm(psY[:], oT[:, ol, h, :], wo[:, wl, h, :],
                               start=h == 0 and i == 0, stop=h == HQ - 1 and i == 2)
                    m.then_inc(s["wo_used"], 1)

            def ln_bank_free(ln, n, u):
                need(pe, LNS[ln]["lo"], ln_at(ln, {3: 1, 5: 4}.get(n, n) if ln == 0 else n))
                if u.exists:
                    pe.wait_ge(s["pT_lo"], u.c + 1)

            f = FF[a.index]
            for t in steps(pe, STEPS, a.unroll, a.lead, a.done):
                t1, t2, t3 = t.back(1), t.back(2), t.back(3)
                if a.rms:
                    if t.exists:
                        q_proj(t, 0, 2)
                    if t2.exists:
                        p_transpose(t2)
                    if t.exists:
                        q_proj(t, 2, 4)
                        kv_proj(t)
                    if t1.exists and t.exists:
                        scores(t1)
                else:
                    units = units_of(t)
                    if t.static and t.t == 0:
                        q_unit(t)
                        for n in first_norms(0):
                            ln_transpose(0, n, lambda: ln_bank_free(0, n, t2))
                    for k in units[-1:]:
                        q_unit(k)
                    if t1.exists and not units:
                        scores(t1)
                        if not t.exists:
                            gate_product(f, 0)
                    if t2.exists:
                        p_transpose(t2)
                    if a.kv_new(t):
                        kv_proj(t)
                    if t1.exists and units:
                        scores(t1)
                    for n in first_norms(t.t) if t.static and t.t > 0 else ():
                        ln_transpose(0, n, lambda: ln_bank_free(0, n, t2))
                if a.norm_slot(t) == "between":
                    ln_transpose(next_ln, t.t - LN_SLOT, lambda: ln_bank_free(next_ln, t.t - LN_SLOT, t2))
                if a.rms and t2.exists and t.exists:
                    attend(t2)
                if t3.exists:
                    out_proj(t3, 0, 4)
                if a.rms and not t.exists:
                    scores(t1)
                    attend(t2)
                if not a.rms:
                    if a.kv_new(t):
                        k_transpose(t)
                    if t2.exists:
                        attend(t2)
                if a.norm_slot(t) == "last":
                    ln_transpose(next_ln, t.t - LN_SLOT, lambda: ln_bank_free(next_ln, t.t - LN_SLOT, t2))
                if a.index == 1 and t.static and t.t == 0:
                    ln_transpose(2, NT - 1, lambda: pe.wait_ge(LNS[2]["lo"], ln_at(2, NT - 1)))
                if t.exists and a.rms:
                    q_transpose(t)
                    k_transpose(t)
            last, before = Step(STEPS - 1, STEPS, done=a.done), Step(STEPS - 2, STEPS, done=a.done)
            if a.rms:
                gate_product(f, 0)
            pe.wait_ge(s["max"], last.c + 1)
            dense_product(f, 0)
            p_transpose(last)
            out_proj(before, 0, 4)
            attend(last)
            ln_transpose(next_ln, 5, lambda: ln_bank_free(next_ln, 5, last))
            dense_product(f, 1)
            out_proj(last, 0, 4)
            ln_transpose(next_ln, 6, lambda: ln_bank_free(next_ln, 6, last))

        def ffn(f, next_ln):
            s, done = FS, f.done
            for t in range(NT + 3):
                u, v = t - 1, t - 3
                if t < NT and (t == 1 or not f.dense):
                    gate_product(f, t)
                if 0 <= u < NT:
                    pe.wait_ge(s["hid"], done + u + 1)
                    need(pe, s["hidT_lo"], done + u)
                    if u == 0 and f.dense:
                        pe.wait_ge(LNS[f.ln]["lo"], ln_at(f.ln, NT - 1))
                    for j in range(f.parts):
                        i = tr(psP[0:f.rows, j * P:(j + 1) * P], s_sb[:, j * f.rows:(j + 1) * f.rows], ident[:])
                    i.then_inc(s["hid_tr"], 1)
                if 0 <= v < NT - (f.index == 0) and next_ln != 4:
                    if v == 0:
                        pe.wait_ge(LNS[f.ln]["lo"], ln_at(f.ln, NT))
                    ln_transpose(next_ln, v, lambda: need(pe, LNS[next_ln]["lo"], ln_at(next_ln, v)))
                if t < NT and f.dense:
                    if t > 1:
                        gate_product(f, t)
                    if t == 1:
                        pe.wait_ge(A["x_add"], (f.index + 1) * STEPS)
                        dense_product(f, 2)
                        ln_transpose(f.ln, NT - 1, lambda: None)
                    if t > 2:
                        dense_product(f, t)
                if 0 <= u < NT:
                    pe.wait_ge(s["hidT_lo"], done + u + 1)
                    if u == 0:
                        pe.wait_ge(ld["wo_lo"], f.wo_n)
                    if not f.dense:
                        need(pe, s["x_add"], done + u - 2)
                    for j in range(f.parts):
                        for i, (hl, wl) in enumerate(PASSES):
                            m = mm(ring3(u)[:], hidT[0:f.rows, hl, j, :], wo[0:f.rows, wl, j, :],
                                   start=not f.dense and j == 0 and i == 0, stop=j == f.parts - 1 and i == 2)
                    m.then_inc(s["experts"], 1)

        def linear_attention(next_ln):
            s = M
            for t in range(NT + 4):
                if 0 <= t - 2 < NT:
                    u = t - 2
                    pe.wait_ge(s["q2_lo"], u + 1)
                    pe.wait_ge(s["kvs_lo"], u + 1)
                    need(pe, s["x_add"], u)
                    for i, (kl, ql) in enumerate(PASSES):
                        m = mm(psY[:], kvs_r[:, u % 2, kl, :], q2[:, ql, :], start=i == 0, stop=i == 2)
                    m.then_inc(s["out"], 1)
                if 0 <= t - 1 < NT:
                    pe.wait_ge(s["eT_lo"], t)
                    need(pe, s["kvs"], t - 1)
                    if t == 1:
                        pe.wait_ge(FS["x_add"], 2 * NT)
                    for k in range(KT):
                        for i, (el, cl) in enumerate(PASSES):
                            m = mm(psKV[:, 0:P], eT[:, el, k, :], ctxT[:, cl, k, tok(t - 1)],
                                   start=k == 0 and i == 0, stop=k == KT - 1 and i == 2)
                    m.then_inc(s["kv"], 1)
                if t < NT:
                    ln_transpose(4, t, lambda: need(pe, s["q_shift"], t))
                    pe.wait_ge(s["e"], t + 1)
                    need(pe, s["eT_lo"], t)
                    if t == 0:
                        pe.wait_ge(FS["x_add"], 2 * NT - 1)
                    for k in range(KT):
                        i = tr(psS[:, k * P:(k + 1) * P], stage_q[:, t % 4, k * P:(k + 1) * P], ident[:])
                    i.then_inc(s["e_tr"], 1)
                if 0 <= t - 1 < NT:
                    pe.wait_ge(s["q_soft"], t)
                    need(pe, s["q2_lo"], t - 1)
                    for k in range(KT):
                        i = tr(psP[:, k * P:(k + 1) * P], prob[:, k * P:(k + 1) * P], ident[:])
                    i.then_inc(s["q_tr"], 1)
                if 0 <= t - 3 < NT:
                    def free():
                        if t == 3:
                            pe.wait_ge(FS["hid"], 2 * NT)
                        need(pe, LNS[next_ln]["lo"], ln_at(next_ln, t - 3))
                    ln_transpose(next_ln, t - 3, free)

        def add_bias(bank, what):
            r = bias_row[what]
            for i in range(2):
                m = mm(bank, ones_r[r:r + 1, :], pT[r:r + 1, i, :], start=False, stop=i == 1)
            return m

        def cross_attention(next_ln):
            s = N3

            def f_transpose(n):
                pe.wait_ge(s["f"], n + 1)
                need(pe, s["fT_lo"], n)
                for k in range(KT):
                    i = tr(psS[:, k * P:(k + 1) * P], stage_q[:, n % 4, k * P:(k + 1) * P], ident[:])
                i.then_inc(s["f_tr"], 1)

            def similarity(n):
                pe.wait_ge(LNS[next_ln]["lo"], ln_at(next_ln, n + 1))
                if n == 0:
                    pe.wait_ge(ld["wkv_lo"], 32)
                need(pe, C3["exp"], n)
                for k in range(KT):
                    for i, (xl, wl) in enumerate(PASSES):
                        m = mm(psO[:, 1, P:P + 64], lat(xl, k, n), wkv_k(wl, k, 64),
                               start=k == 0 and i == 0, stop=k == KT - 1 and i == 2)
                m.then_inc(C3["sim"], 1)

            f_transpose(0)
            for t in range(NT + 4):
                u = t - 1
                if t < NT:
                    pe.wait_ge(s["fT_lo"], t + 1)
                    need(pe, s["kn"], t)
                    if t == 0:
                        pe.wait_ge(ld["wo_lo"], 72)
                        pe.wait_ge(ld["vec_lo"], 1)
                    for k in range(KT):
                        for i, (xl, wl) in enumerate(PASSES):
                            mm(psKV[:], fT[:, xl, k, :], wo[:, wl, k, :], start=k == 0 and i == 0, stop=False)
                    add_bias(psKV[:], "k").then_inc(s["k"], 1)
                if 0 <= u < NT:
                    pe.wait_ge(s["q_sb"], u + 1)
                    need(pe, LNS[6]["lo"], ln_at(6, NT))
                    need(pe, LNS[next_ln]["lo"], ln_at(next_ln, min(t - 3, NT)))
                    for k in range(KT):
                        i = tr(psT[:, k * P:(k + 1) * P], q_sb[:, k * P:(k + 1) * P], ident[:])
                    i.then_inc(s["q_tr"], 1)
                if 0 <= t - 2 < NT:
                    pe.wait_ge(s["pT_lo"], t - 1)
                    pe.wait_ge(s["f_lo"], t - 1)
                    need(pe, s["x_add"], t - 2)
                    for i, (pl, fl) in enumerate(PASSES):
                        m = mm(psY[:], pT3[:, pl, :], f_r[:, (t - 2) % 3, fl, :], start=i == 0, stop=i == 2)
                    m.then_inc(s["attend"], 1)
                if 0 <= t - 4 < NT:
                    similarity(t - 4)
                if 0 <= u < NT:
                    pe.wait_ge(s["qT_lo"], u + 1)
                    pe.wait_ge(s["kT_lo"], u + 1)
                    need(pe, s["exp"], u)
                    for k in range(KT):
                        for i, (ql, kl) in enumerate(PASSES):
                            m = mm(psO[:, 0, 0:P], qT3[:, ql, k, :], kT3[:, kl, k, :],
                                   start=k == 0 and i == 0, stop=k == KT - 1 and i == 2)
                    m.then_inc(s["scores"], 1)
                if t + 1 < NT:
                    f_transpose(t + 1)
                if 0 <= t - 3 < NT:
                    ln_transpose(next_ln, t - 3, lambda: pe.wait_ge(s["qT_lo"], min(t, NT)))
                if t < NT:
                    pe.wait_ge(LNS[6]["lo"], ln_at(6, t + 1))
                    need(pe, s["q_sq"], t)
                    for k in range(KT):
                        if t == 0:
                            wq_split(18, k)
                        for i, (xl, wl) in enumerate(PASSES):
                            mm(psQ[:], lat(xl, k, t), wq[:, wl, k, :], start=k == 0 and i == 0, stop=False)
                    add_bias(psQ[:], "q").then_inc(s["q"], 1)
                if 0 <= u < NT:
                    pe.wait_ge(s["prob"], u + 1)
                    need(pe, C3["exp"], t - 4 + 1)
                    tr(psO[:, 1, 0:P], s_sb[:, 0:P], ident[:]).then_inc(s["p_tr"], 1)
                if t < NT:
                    pe.wait_ge(s["kn"], t + 1)
                    need(pe, s["kw"], t)
                    for k in range(KT):
                        i = tr(psP[:, k * P:(k + 1) * P], k3[:, k * P:(k + 1) * P], ident[:])
                    i.then_inc(s["k_tr"], 1)
                if t > NT + 1 :
                    dense(t - NT - 2)

        def dense(n):
            s = C3
            if n == 0:
                pe.wait_ge(N3["q_sq"], NT)
                pe.wait_ge(N3["kn"], NT)
                pe.wait_ge(N3["kw"], NT)
            if n == 4:
                pe.wait_ge(N3["x_add"], NT)
            need(pe, s["masked"], n - 4)
            for k in range(KT):
                if n == 0:
                    wq_split(19, k)
                for i, (xl, wl) in enumerate(PASSES):
                    mm(dense_bank(n)[:], lat(xl, k, n), wq[:, wl, k, :], start=k == 0 and i == 0, stop=False)
            add_bias(dense_bank(n)[:], "o").then_inc(s["dense"], 1)

        def clustered():
            s = C3
            pe.wait_ge(s["hits"], NT)
            pe.wait_ge(N3["exp"], NT)
            for n in range(NT):
                m = mm(psO[0:64, 0, 0:2], hit(n), ones_r[:, 0:2], start=n == 0, stop=n == NT - 1)
            m.then_inc(s["count"], 1)
            dense(2)
            pe.wait_ge(s["sel"], 1)
            mm(psT[:], s_sb[0:64, 0:P], prob[0:64, :], start=True, stop=True).then_inc(s["rows"], 1)
            for n in range(3, NT):
                dense(n)

        pe.wait_ge(setup["const"], 3)
        for n in range(2):
            ln_transpose(0, n, lambda: None)
        attention(L0, 1)
        ffn(FF[0], 2)
        attention(L1, 3)
        ffn(FF[1], 4)
        linear_attention(5)
        ffn(FF[2], 6)
        cross_attention(7)
        clustered()

    @block.scalar
    def _(act):
        copy = lambda o, i: nc.scalar.activation(o, i, ACT.Copy)

        def ln_hi(ln, n):
            s = LNS[ln]
            act.wait_ge(s["tr"], ln_at(ln, n + 1))
            copy(lat_all(HI, n), slices(ln_bank(ln, n))).then_inc(s["hi"], 1)

        def high(what, dst, stage, in_count):
            act.wait_ge(ld[what + "_in"], in_count)
            copy(dst, stage).then_inc(ld[what + "_hi"], 1)

        def high_wq(load):
            for k in range(KT):
                high("wq", wq[:, HI, k], stage_q[:, k], (load + 1) * 16)

        def high_wo(load, n=KT):
            for k in range(n):
                high("wo", wo[:, HI, k], stage_o[:, k], (load + 1) * 16)

        def high_ctx(half):
            for k in range(KT):
                high("ctx", ctx_part(HI, k, half), stage_o[:, k].rearrange("p (n b t) -> p n b t", n=4, b=2),
                     (half + 1) * 16)

        def high_wkv(load, width=D):
            for k in range(2):
                high("wkv", wkv[:, HI, k, 0:width], stage_kv[:, k, 0:width], (load + 1) * 16)

        def gate_exp(f, t):
            act.wait_ge(FS["shift"], f.done + t + 1)
            if f.index == 1:
                nc.scalar.activation(gate[:, 0:8], psQ[:, 0:8], ACT.Exp, bias=small[:, 0:1], scale=1.0,
                                     accum_out=small[:, 1:2]).then_inc(FS["exp"], 1)
            else:
                nc.scalar.activation(small[:, 1:2], small[:, 0:1], ACT.Exp).then_inc(FS["exp"], 1)

        def attention(a, next_ln):
            s, keys = A, a.keys

            def squares(st):
                n = st.res(2)
                act.wait_ge(s["wq_used"], st.t * 4 + 4)
                for h in range(HQ):
                    i = nc.scalar.activation(junk_q[h], psQ[:, h * HD:(h + 1) * HD], ACT.Square,
                                             accum_out=ssq[:, n, h:h + 1])
                i.then_inc(s["squares"], 1)

            def next_wq(st):
                if a.rms:
                    act.wait_ge(s["wq_used"], st.t * 4 + 4)
                else:
                    act.wait_ge(s["q_units"], st.t + 2)
                high_wq(st.div(8) + (10 if a.rms else 1))

            def scores_lo(u):
                act.wait_ge(s["scores"], u.c + 1)
                need(act, s["exp"], u.c)
                copy(two_by_two(wide), score_parts(LO)).then_inc(s["s_lo"], 1)

            def exps(u):
                act.wait_ge(s["neg_max"], u.c + 1)
                need(act, s["p_tr"], u.c)
                need(act, s["rsums"], u.c)
                for j in range(4):
                    at = slice(j * keys, (j + 1) * keys)
                    if a.rms:
                        e = nc.scalar.activation(prob[:, at], s_sb[:, at], ACT.Exp,
                                                 bias=neg_mx[:, j:j + 1], scale=1.0, accum_out=sums[:, j:j + 1])
                    else:
                        e = nc.scalar.activation(prob[:, at], wide[:, at], ACT.Exp,
                                                 bias=neg_mx[:, j:j + 1], scale=a.scale,
                                                 accum_out=sums[:, j:j + 1])
                e.then_inc(s["exp"], 1)

            def unit_hi(k):
                act.wait_ge(s["q_units"], k.t + 1)
                need(act, s["scores"], k.t - 2 + k.res(2))
                copy(unit_in(HI, k), unit_out(k)).then_inc(s["qT_hi"], 1)

            def qT_hi(st):
                act.wait_ge(s["q_tr"], st.t + 1)
                need(act, s["scores"], st.c)
                copy(qT[:, HI], heads(psT[:])).then_inc(s["qT_hi"], 1)

            def kT_hi(st):
                act.wait_ge(s["k_tr"], a.kv_n(st) + 1)
                src = k_sb[:, HD:2 * HD] if a.rms else psKV[:, 0:2 * keys]
                if a.rms:
                    act.wait_ge(s["k_scaled"], st.t + 1)
                copy(a.kT[:, st.res(a.ring), HI], src).then_inc(s["kT_hi"], 1)

            def kv_read(st):
                act.wait_ge(s["kv"], a.kv_n(st) + 1)
                need(act, s["k_tr"], a.kv_n(st))
                if a.rms:
                    need(act, s["ms"], st.t - 1)
                    nc.scalar.activation(junk_k, psKV[:, 0:HD], ACT.Square, accum_out=ssq[:, st.res(2), 4:5])
                    copy(a.v[:, st.res(a.ring), HI], psKV[:, HD:2 * HD]).then_inc(s["v_hi"], 1)
                    return
                kv = psKV[:].rearrange("p (b c) -> p b c", b=2)
                copy(k_sb[:].rearrange("p (b c) -> p b c", b=2), kv[:, :, 0:HD]).then_inc(s["k_read"], 1)
                copy(a.v[:, st.res(a.ring), HI].rearrange("p (b c) -> p b c", b=2), kv[:, :, HD:256]).then_inc(s["v_hi"], 1)

            def oT_hi(u):
                act.wait_ge(s["pv"], u.c + 1)
                need(act, s["wo_used"], u.c * 4)
                copy(oT[:, HI].rearrange("p h (b t) -> p b h t", b=2),
                     o_banks(a)).then_inc(s["oT_hi"], 1)

            def pT_hi(u):
                act.wait_ge(s["p_tr"], u.c + 1)
                need(act, s["pv"], u.c)
                copy(pT[:, HI, 0:4 * keys], psP[:, 0:4 * keys]).then_inc(s["pT_hi"], 1)

            for t in steps(act, STEPS, a.unroll, a.lead, a.done):
                t1, t2 = t.back(1), t.back(2)
                units = [] if a.rms else units_of(t)
                scores_first = not a.rms and not units
                if scores_first:
                    scores_lo(t1)
                if t2.exists:
                    pT_hi(t2)
                if t.exists and a.rms:
                    squares(t)
                for k in units[:-1]:
                    unit_hi(k)
                if a.index == 0 and t.static and t.t == 0:
                    for n in first_norms(0):
                        ln_hi(0, n)
                early = not a.rms and a.kv_new(t)
                if early and t.res(8) == 6:
                    next_wq(t)
                if a.kv_new(t):
                    kv_read(t)
                if t1.exists and not a.rms and not scores_first:
                    scores_lo(t1)
                for k in units[-1:]:
                    unit_hi(k)
                if t.exists and not early and t.res(8) == (7 if a.rms else 6):
                    next_wq(t)
                if a.index == 0 and t.static and t.t > 0:
                    for n in first_norms(t.t):
                        ln_hi(0, n)
                if a.index == 1 and t.static and t.t == 0:
                    ln_hi(2, NT - 1)
                if a.norm_slot(t) == "between":
                    ln_hi(next_ln, t.t - LN_SLOT)
                if t1.exists:
                    exps(t1)
                if t2.exists and a.rms:
                    oT_hi(t2)
                if a.rms and t.res(8) == 7 and t.exists:
                    act.wait_ge(s["kv"], a.kv_n(t) + 1)
                    if t.static and t.t == STEPS - 1:
                        high_wkv(13, 144)
                    else:
                        high_wkv(t.div(8) + 6)
                if not a.rms and t.res(16) == 12 and t.exists:
                    act.wait_ge(s["kv"], t.div(16) * 8 + 8)
                    if t.static and t.t == 60:
                        high_wkv(4, 504)
                    else:
                        high_wkv(t.div(16) + 1)
                if t.res(8) == 2 and not (t.static and t.t >= STEPS):
                    need(act, s["wo_used"], t.div(8) * 32 + a.done * 4)
                    high_wo(t.div(8) + (9 if a.rms else 0))
                if t.exists:
                    if a.kv_new(t):
                        kT_hi(t)
                    if a.rms:
                        qT_hi(t)
                if t2.exists and not a.rms:
                    oT_hi(t2)
                if a.norm_slot(t) == "last":
                    ln_hi(next_ln, t.t - LN_SLOT)
                if a.index == 0 and t.static and t.t == 0:
                    high_ctx(1)
            last = Step(STEPS - 1, STEPS, done=a.done)
            pT_hi(last)
            gate_exp(FF[a.index], 0)
            oT_hi(last)
            for n in range(5, NT - 1):
                ln_hi(next_ln, n)

        high_wq(0)
        ln_hi(0, 0)
        ln_hi(0, 1)
        high_ctx(0)
        high_wkv(0)
        attention(L0, 1)

        def high_b(f, load):
            for j in range(f.parts):
                high("wo", wo[0:f.rows, HI, j], stage_o[0:f.rows, j], (load + 1) * 16)

        def ffn(f, next_ln, after):
            s, done = FS, f.done
            for t in range(NT + 3):
                u, v = t - 1, t - 3
                if 0 <= u < NT:
                    act.wait_ge(s["hid_tr"], done + t)
                    need(act, s["experts"], done + u)
                    copy(hidT[0:f.rows, HI, 0:f.parts], psP[0:f.rows, 0:f.parts * P].rearrange(
                        "p (j t) -> p j t", t=P)).then_inc(s["hidT_hi"], 1)
                if 0 <= v < NT - (f.index == 0) and next_ln != 4:
                    ln_hi(next_ln, v)
                if t < NT and (t > 0 or not f.dense):
                    gate_exp(f, t)
                if t == 1 and f.dense:
                    ln_hi(f.ln, NT - 1)
                after(t)

        def after0(t):
            if t < 8:
                hl, k = t // 4, t % 4
                copy(ctxT[:, hl, k].rearrange("p (n b t) -> p n b t", n=NT, b=2),
                     hT[:, hl, k, :, 0:4:3, :].bitcast(f32)).then_inc(setup["ctxT"], 1)
            if t == 8:
                act.wait_ge(FS["gate_a"], NT)
                high_wkv(5)
                act.wait_ge(FS["dense"], NT)
                high_wq(9)

        def ctx_exp(n):
            act.wait_ge(M["k_max"], n + 1)
            nc.scalar.activation(stage_q[:, n % 4], stage_q[:, n % 4], ACT.Exp, bias=small[:, 8 + n % 2:9 + n % 2],
                                 scale=1.0, accum_out=small[:, 10 + n % 2:11 + n % 2]).then_inc(M["e"], 1)

        def f_squares(n):
            act.wait_ge(ld[f"c{n % 4}"], (n // 4 + 3) * 16)
            need(act, N3["ms_f"], n)
            nc.scalar.activation(junk_f3, stage_q[:, n % 4], ACT.Square,
                                 accum_out=small[:, 6:7]).then_inc(N3["f_sq"], 1)

        def after1(t):
            if t == 4 :
                act.wait_ge(ld["vec_in"], 48)
                for r in bias_row.values():
                    i = copy(pT[r:r + 1, HI], wide[r:r + 1])
                i.then_inc(ld["vec_hi"], 1)
                copy(ones_r[:], ones[:]).then_inc(setup["ones_r"], 1)
            if t == 7:
                ctx_exp(0)
            if t == 8:
                act.wait_ge(FS["gate_a"], 2 * NT)
                high_wkv(14, 136)
            if t == NT + 2:
                act.wait_ge(FS["experts"], 2 * NT)
                high_b(FF[2], 18)

        def after2(t):
            if t == 8:
                f_squares(0)
                for k in (1, 2, 3):
                    high("wo", wo[:, HI, k], stage_o[:, k], 21 * 16)
                act.wait_ge(FS["gate_a"], 3 * NT)
                high_wkv(15, 128)
            if t == NT + 2:
                act.wait_ge(FS["experts"], 3 * NT)
                high("wo", wo[:, HI, 0], stage_o[:, 0], 21 * 16)

        def linear_attention(next_ln):
            s = M

            for t in range(NT + 4):
                if 0 <= t - 1 < NT:
                    act.wait_ge(s["kvs"], t)
                    need(act, s["out"], t - 2)
                    copy(kvs_r[:, (t - 1) % 2, HI], kvs).then_inc(s["kvs_hi"], 1)
                if t < NT:
                    act.wait_ge(s["e_tr"], t + 1)
                    need(act, s["kv"], t)
                    copy(eT[:, HI], slices(psS)).then_inc(s["eT_hi"], 1)
                if 0 <= t - 1 < NT:
                    act.wait_ge(s["q_tr"], t)
                    need(act, s["out"], t - 1)
                    copy(q2[:, HI], psP[:]).then_inc(s["q2_hi"], 1)
                if t < NT:
                    act.wait_ge(s["q_shift"], t + 1)
                    nc.scalar.activation(q_sb[:], q_sb[:], ACT.Exp).then_inc(s["q_exp"], 1)
                if 0 <= t - 3 < NT:
                    ln_hi(next_ln, t - 3)
                if t + 1 < NT:
                    ctx_exp(t + 1)
                if t == 4:
                    act.wait_ge(ld["wo_in"], 20 * 16)
                    for k in range(KT):
                        copy(wq[:, HI, k], stage_o[:, k]).then_inc(ld["wq_hi"], 1)

        def cross_attention(next_ln):
            s = N3

            def f_hi(n):
                act.wait_ge(s["f"], n + 1)
                need(act, s["attend"], n - 2)
                copy(f_r[:, n % 3, HI], stage_q[:, n % 4]).then_inc(s["f_hi"], 1)

            def fT_hi(n):
                act.wait_ge(s["f_tr"], n + 1)
                need(act, s["k"], n)
                copy(fT[:, HI], slices(psS)).then_inc(s["fT_hi"], 1)

            f_hi(0)
            fT_hi(0)
            for t in range(NT + 4):
                u = t - 1
                if 0 <= u < NT:
                    act.wait_ge(s["kw"], u + 1)
                    need(act, s["scores"], u)
                    copy(kT3[:, HI], slices(k3w)).then_inc(s["kT_hi"], 1)
                if t + 1 < NT:
                    f_squares(t + 1)
                if t < NT:
                    act.wait_ge(s["k"], t + 1)
                    need(act, s["ms_k"], t)
                    nc.scalar.activation(junk_k3, psKV[:], ACT.Square, accum_out=small[:, 7:8]).then_inc(s["k_sq"], 1)
                if 0 <= u < NT:
                    act.wait_ge(s["q_tr"], u + 1)
                    copy(qT3[:, HI], slices(psT)).then_inc(s["qT_hi"], 1)
                if t < NT:
                    act.wait_ge(s["pw_k"], t + 1)
                    need(act, s["kT_lo"], t)
                    nc.scalar.activation(k3[:], psKV[:], ACT.Copy, scale=small[:, 3:4]).then_inc(s["kn"], 1)
                if t + 1 < NT:
                    f_hi(t + 1)
                if 0 <= t - 4 < NT:
                    act.wait_ge(C3["neg_max"], t - 3)
                    nc.scalar.activation(hit_exp[:], psO[:, 1, P:P + 64], ACT.Exp, bias=small[:, 13:14],
                                         scale=1.0 / TEMPERATURE, accum_out=small[:, 14:15]).then_inc(C3["exp"], 1)
                if 0 <= u < NT:
                    act.wait_ge(s["neg_max"], u + 1)
                    need(act, s["p_tr"], u)
                    for b in range(2):
                        rows = slice(b * S, (b + 1) * S)
                        i = nc.scalar.activation(s_sb[rows, b * S:(b + 1) * S], psO[rows, 0, b * S:(b + 1) * S], ACT.Exp,
                                                 bias=small[rows, 10:11], scale=small[rows, 9:10],
                                                 accum_out=small[rows, 11:12])
                    i.then_inc(s["exp"], 1)
                if 0 <= t - 3 < NT:
                    ln_hi(next_ln, t - 3)
                if t + 1 < NT:
                    fT_hi(t + 1)
                if t < NT:
                    act.wait_ge(s["q"], t + 1)
                    need(act, s["q_tr"], t)
                    copy(q_sb[:], psQ[:]).then_inc(s["q_sb"], 1)
                    need(act, s["ms_q"], t)
                    nc.scalar.activation(junk_q3, psQ[:], ACT.Square, accum_out=small[:, 8:9]).then_inc(s["q_sq"], 1)
                if 0 <= u < NT:
                    act.wait_ge(s["p_tr"], u + 1)
                    need(act, s["attend"], u)
                    copy(pT3[:, HI], psO[:, 1, 0:P]).then_inc(s["pT_hi"], 1)
                if t == NT :
                    act.wait_ge(s["q"], NT)
                    act.wait_ge(ld["wo_in"], 22 * 16)
                    for k in range(KT):
                        copy(wq[:, HI, k], stage_o[:, k]).then_inc(ld["wq_hi"], 1)

        act.wait_ge(A["wo_used"], STEPS * 4)
        high_b(FF[0], 8)
        ffn(FF[0], 2, after0)
        attention(L1, 3)
        act.wait_ge(A["wo_used"], 2 * STEPS * 4)
        high_b(FF[1], 17)
        ffn(FF[1], 4, after1)
        linear_attention(5)
        ffn(FF[2], 6, after2)
        cross_attention(7)

    @block.vector
    def _(dve):
        V = nc.vector

        def sub_hi(dst_lo, src, dst_hi):
            return V.tensor_tensor(dst_lo, src, dst_hi.bitcast(f32), ALU.subtract)

        links = [0]

        def mark(instruction):
            links[0] += 1
            instruction.then_inc(chain, 1)
            return links[0]

        def link(instruction):
            dve.wait_ge(chain, mark(instruction))

        def low_wq(load, stage=stage_q):
            for k in range(2, KT):
                dve.wait_ge(ld["wq_hi"], load * 4 + (k + 1))
                sub_hi(wq[:, LO, k], stage[:, k], wq[:, HI, k]).then_inc(ld["wq_lo_v"], 1)

        def ln_stats(ln, n):
            s = LNS[ln]
            link(V.bn_stats(bn[:, n % 2], x[:, n]))
            link(V.bn_aggr(mv[:, n], bn[:, n % 2]))
            V.tensor_scalar(var_eps[:, n:n + 1], mv[:, n, 1:2], LN_EPS, None, ALU.add).then_inc(s["var"], 1)

        def x_stats(n):
            dve.wait_ge(ld[f"x{n}" if n < 2 else "x_rest"], 16)
            ln_stats(0, n)

        def low_ctx(half):
            for k in range(2, KT):
                dve.wait_ge(ld["ctx_hi"], half * 4 + k + 1)
                sub_hi(ctx_part(LO, k, half), stage_o[:, k].rearrange("p (n b t) -> p n b t", n=4, b=2),
                       ctx_part(HI, k, half)).then_inc(ld["ctx_lo_v"], 1)

        def ln_norm(ln, n):
            s = LNS[ln]
            dve.wait_ge(s["rstd"], ln_at(ln, n + 1))
            need(dve, s["tr"], ln_at(ln, n if ln in (4, 5) else n - 1))
            V.tensor_scalar(xn[:, xn_slot(ln, n)], x[:, n], mv[:, n, 0:1], rstd[:, n:n + 1], ALU.subtract,
                            ALU.mult).then_inc(s["xn"], 1)

        def ln_lo(ln, n):
            s = LNS[ln]
            dve.wait_ge(s["hi"], ln_at(ln, n + 1))
            sub_hi(lat_all(LO, n), slices(ln_bank(ln, n)), lat_all(HI, n)).then_inc(s["lo"], 1)

        def gates(f, t, u=None, next_ln=None):
            s, done, E, R = FS, f.done, f.E, f.R

            def hid():
                need(dve, s["hid_tr"], done + t)
                by_expert = lambda ap: ap.rearrange("p (e r) -> p e r", e=E)
                V.scalar_tensor_tensor(by_expert(s_sb[:, 0:E * R]), by_expert(gate_bank(f, t)[:, E:f.width]), small[:, 3:4],
                                       gate[:, 0:E].unsqueeze(2).to_broadcast([P, E, R]), ALU.mult,
                                       ALU.mult).then_inc(s["hid"], 1)

            def one_hot(c, share):
                return V.tensor_scalar(pick[:, c, 0:E], iota[:, 0:E], top_f[:, c:c + 1], share, ALU.is_equal, ALU.mult)

            def gates_of_logits():
                dve.wait_ge(chain, mark(V.tensor_scalar(small[:, 2:3], small[:, 1:2], 1.0, 1.0 / f.scale, ALU.add, ALU.mult)))
                shares = mark(V.reciprocal(small[:, 3:4], small[:, 2:3]))
                link(one_hot(1, small[:, 1:2]))
                dve.wait_ge(chain, shares)
                link(V.scalar_tensor_tensor(gate[:, 0:E], iota[:, 0:E], top_f[:, 0:1], pick[:, 1, 0:E], ALU.is_equal, ALU.add))

            def gates_of_softmax():
                link(V.reciprocal(small[:, 2:3], small[:, 1:2]))
                link(V.tensor_scalar(logits[:, 0:E], gate[:, 0:E], small[:, 2:3], None, ALU.mult))
                link(V.max(top[:], logits[:, 0:E]))
                found = mark(V.max_index(top_at[:], top[:], logits[:, 0:E]))
                total = mark(V.tensor_scalar(small[:, 2:3], top[:, 0:1], top[:, 1:2], 1.0 / f.scale, ALU.add, ALU.mult))
                dve.wait_ge(chain, found)
                copied = mark(V.tensor_copy(top_f[:], top_at[:, 0:2]))
                dve.wait_ge(chain, total)
                shares = mark(V.reciprocal(small[:, 3:4], small[:, 2:3]))
                dve.wait_ge(chain, copied)
                mark(one_hot(0, top[:, 0:1]))
                dve.wait_ge(chain, mark(one_hot(1, top[:, 1:2])))
                dve.wait_ge(chain, shares)
                link(V.tensor_tensor(gate[:, 0:E], pick[:, 0, 0:E], pick[:, 1, 0:E], ALU.add))

            adds = u is not None
            if f.index == 0 and t == 0:
                dve.wait_ge(setup["iota"], 2)
                dve.wait_ge(setup["ones"], 1)
            dve.wait_ge(s["gate_a"], done + t + 1)
            values = gate_bank(f, t)[:, 0:E]
            if E < 8:
                link(V.tensor_copy(logits[:, 0:E], values))
                values = logits[:, 0:8]
            largest = mark(V.max(top[:], values))
            if adds:
                dve.wait_ge(s["x_add"], done + u + 1)
                stats = mark(V.bn_stats(bn[:, u % 2], x[:, u]))
            dve.wait_ge(chain, largest)
            if f.index == 1:
                V.tensor_scalar(small[:, 0:1], top[:, 0:1], -1.0, None, ALU.mult).then_inc(s["shift"], 1)
            else:
                V.tensor_tensor(small[:, 0:1], top[:, 1:2], top[:, 0:1], ALU.subtract).then_inc(s["shift"], 1)
                found = mark(V.max_index(top_at[:], top[:], values))
            if adds:
                dve.wait_ge(chain, stats)
                both = mark(V.bn_aggr(mv[:, u], bn[:, u % 2]))
            if f.index != 1:
                dve.wait_ge(chain, found)
                copied = mark(V.tensor_copy(top_f[:], top_at[:, 0:2]))
            if adds:
                dve.wait_ge(chain, both)
                V.tensor_scalar(var_eps[:, u:u + 1], mv[:, u, 1:2], LN_EPS, None,
                                ALU.add).then_inc(LNS[next_ln]["var"], 1)
            dve.wait_ge(s["exp"], done + t + 1)
            if f.index == 1:
                gates_of_softmax()
            else:
                dve.wait_ge(chain, copied)
                gates_of_logits()
            hid()

        def attention(a, next_ln):
            s, keys = A, a.keys

            def blocks(t):
                return t[:, 0:4 * keys].rearrange("p (j c) -> p j c", j=4)

            def row_max(u):
                dve.wait_ge(s["scores"], u.c + 1)
                need(dve, s["exp"], u.c)
                if not a.rms:
                    dve.wait_ge(s["s_lo"], u.t + 1)
                    V.tensor_tensor(two_by_two(wide), score_parts(HI), two_by_two(wide), ALU.add).then_inc(s["added"], 1)
                    dve.wait_ge(s["added"], u.t + 1)
                    V.tensor_reduce(mx[:], blocks(wide), AX.X, ALU.max).then_inc(s["max"], 1)
                else:
                    parts = psS[:].rearrange("p (j h c) -> p h j c", j=4, h=2)
                    V.scalar_tensor_tensor(blocks(s_sb), parts[:, 0], a.scale, mask[:].unsqueeze(1).to_broadcast(
                        [P, 4, keys]), ALU.mult, ALU.add).then_inc(s["masked"], 1)
                    dve.wait_ge(s["masked"], u.t * 2 + 1)
                    V.scalar_tensor_tensor(blocks(s_sb), parts[:, 1], a.scale, blocks(s_sb), ALU.mult,
                                           ALU.add).then_inc(s["masked"], 1)
                    dve.wait_ge(s["masked"], u.t * 2 + 2)
                    V.tensor_reduce(mx[:], blocks(s_sb), AX.X, ALU.max).then_inc(s["max"], 1)
                dve.wait_ge(s["max"], u.c + 1)
                V.tensor_scalar(neg_mx[:], mx[:], -1.0 if a.rms else -a.scale, None, ALU.mult).then_inc(s["neg_max"], 1)

            def normalise(u):
                dve.wait_ge(s["exp"], u.c + 1)
                V.reciprocal(rsums[:], sums[:]).then_inc(s["rsums"], 1)
                dve.wait_ge(s["rsums"], u.c + 1)
                V.tensor_tensor(blocks(prob), blocks(prob), rsums[:].unsqueeze(2).to_broadcast([P, 4, keys]),
                                ALU.mult).then_inc(s["prob"], 1)

            def mean_squares(st):
                n = st.res(2)
                dve.wait_ge(s["squares"], st.t + 1)
                need(dve, s["rms"], st.t - 1)
                V.tensor_scalar(ms_eps[:, n], ssq[:, n], 1.0 / HD, RMS_EPS, ALU.mult,
                                ALU.add).then_inc(s["ms"], 1)

            def qk_normalise(st):
                n = st.res(2)
                dve.wait_ge(s["rms"], st.t + 1)
                need(dve, s["q_tr"], st.t)
                four = lambda t: t[:].rearrange("p (h c) -> p h c", h=HQ)
                V.tensor_tensor(four(q_sb), four(psQ), rms[:, n, 0:HQ].unsqueeze(2).to_broadcast([P, HQ, HD]),
                                ALU.mult).then_inc(s["q_read"], 1)
                need(dve, s["k_tr"], a.kv_n(st))
                V.tensor_scalar(k_sb[:, 0:HD], psKV[:, 0:HD], rms[:, n, 4:5], None, ALU.mult).then_inc(s["k_read"], 1)

            def k_scale(st):
                dve.wait_ge(s["k_tr"], a.kv_n(st) + 1)
                V.tensor_scalar(k_sb[:, HD:2 * HD], psKV[:, 0:HD], wqk[:, 2:3], None, ALU.mult).then_inc(s["k_scaled"], 1)

            def qT_lo(st):
                dve.wait_ge(s["qT_hi"], st.c + 1)
                sub_hi(qT[:, LO], heads(psT[:]), qT[:, HI]).then_inc(s["qT_lo"], 1)

            def unit_lo(k):
                dve.wait_ge(s["qT_hi"], k.t + 1)
                sub_hi(unit_in(LO, k), unit_out(k), unit_in(HI, k)).then_inc(s["qT_lo"], 1)

            def kT_lo(st):
                dve.wait_ge(s["kT_hi"], a.kv_n(st) + 1)
                src = k_sb[:, HD:2 * HD] if a.rms else psKV[:, 0:2 * keys]
                sub_hi(a.kT[:, st.res(a.ring), LO], src, a.kT[:, st.res(a.ring), HI]).then_inc(s["kT_lo"], 1)

            def v_lo(st):
                dve.wait_ge(s["v_hi"], a.kv_n(st) + 1)
                if a.rms:
                    sub_hi(a.v[:, st.res(a.ring), LO], psKV[:, HD:2 * HD], a.v[:, st.res(a.ring), HI]).then_inc(s["v_lo"], 1)
                    return
                two = lambda ap: ap.rearrange("p (b c) -> p b c", b=2)
                sub_hi(two(a.v[:, st.res(a.ring), LO]), two(psKV[:])[:, :, HD:256],
                       two(a.v[:, st.res(a.ring), HI])).then_inc(s["v_lo"], 1)

            def x_add(w):
                n = w.res(NT)
                dve.wait_ge(s["wo_used"], w.c * 4 + 4)
                V.tensor_tensor(x[:, n], x[:, n], psY[:], ALU.add).then_inc(s["x_add"], 1)

            def last_stats(w):
                if w.static and w.t >= STEPS - NT:
                    dve.wait_ge(s["x_add"], w.c + 1)
                    ln_stats(next_ln, w.res(NT))

            def oT_lo(u):
                dve.wait_ge(s["oT_hi"], u.c + 1)
                out = oT[:, LO].rearrange("p h (b t) -> p b h t", b=2)
                hi = oT[:, HI].rearrange("p h (b t) -> p b h t", b=2)
                sub_hi(out, o_banks(a), hi).then_inc(s["oT_lo"], 1)

            def pT_lo(u):
                dve.wait_ge(s["pT_hi"], u.c + 1)
                sub_hi(pT[:, LO, 0:4 * keys], psP[:, 0:4 * keys], pT[:, HI, 0:4 * keys]).then_inc(s["pT_lo"], 1)

            for t in steps(dve, STEPS, a.unroll, a.lead, a.done):
                t1, t2, t3 = t.back(1), t.back(2), t.back(3)
                first = first_norms(t.t) if a.index == 0 and t.static else ()
                units = [] if a.rms else units_of(t)
                for n in first:
                    ln_norm(0, n)
                if a.index == 1 and t.static and t.t == 0:
                    ln_norm(2, NT - 1)
                scores_first = not a.rms and not units
                if scores_first:
                    row_max(t1)
                if a.norm_slot(t):
                    ln_norm(next_ln, t.t - LN_SLOT)
                if t2.exists:
                    pT_lo(t2)
                for k in units[:-1]:
                    unit_lo(k)
                between = first if t.static and t.t == 0 else ()
                for n in between:
                    ln_lo(0, n)
                    x_stats(n + 2)
                if a.kv_new(t):
                    v_lo(t)
                if t.exists and a.rms:
                    mean_squares(t)
                if t1.exists and not scores_first:
                    row_max(t1)
                for k in units[-1:]:
                    unit_lo(k)
                for n in first if not between else ():
                    ln_lo(0, n)
                if a.norm_slot(t) == "between":
                    ln_lo(next_ln, t.t - LN_SLOT)
                if a.index == 1 and t.static and t.t == 0:
                    ln_lo(2, NT - 1)
                if t.exists and a.rms:
                    qk_normalise(t)
                if t.exists and t.res(8) == (7 if a.rms else 6):
                    low_wq(t.div(8) + (10 if a.rms else 1))
                if t1.exists:
                    normalise(t1)
                if t3.exists:
                    x_add(t3)
                if t2.exists and a.rms:
                    oT_lo(t2)
                if a.kv_new(t):
                    if a.rms:
                        k_scale(t)
                    kT_lo(t)
                if t.exists and a.rms:
                    qT_lo(t)
                if t2.exists and not a.rms:
                    oT_lo(t2)
                if a.norm_slot(t) == "last":
                    ln_lo(next_ln, t.t - LN_SLOT)
                if t3.exists:
                    last_stats(t3)
                if a.index == 0 and t.static and t.t < NT:
                    if t.t == 0:
                        low_ctx(1)
                        dve.wait_ge(ld["small"], 96)
                        V.tensor_tensor(wqk[:, 2:3], wqk[:, 0:1], wqk[:, 1:2], ALU.mult)
                        link(V.tensor_tensor(wqk3[:, 2], wqk3[:, 0], wqk3[:, 1], ALU.mult))
                    if t.t < NT - 6:
                        x_stats(t.t + 6)
            last, before = Step(STEPS - 1, STEPS, done=a.done), Step(STEPS - 2, STEPS, done=a.done)
            pT_lo(last)
            gates(FF[a.index], 0)
            ln_norm(next_ln, 5)
            x_add(before)
            oT_lo(last)
            last_stats(before)
            ln_lo(next_ln, 5)
            ln_norm(next_ln, 6)
            x_add(last)
            last_stats(last)
            ln_lo(next_ln, 6)

        col = lambda c: small[:, c:c + 1]

        def mean_square(what, n, src, dst):
            dve.wait_ge(N3[what + "_sq"], n + 1)
            V.tensor_scalar(col(dst), col(src), 1.0 / D, RMS_EPS3, ALU.mult, ALU.add).then_inc(N3["ms_" + what], 1)

        def features(n):
            if n == 0:
                dve.wait_ge(ld["fn_in"], 16)
            dve.wait_ge(N3["pw_f"], n + 1)
            V.scalar_tensor_tensor(stage_q[:, n % 4], stage_q[:, n % 4], col(1), wide[:], ALU.mult,
                                   ALU.mult).then_inc(N3["f"], 1)

        def ffn(f, next_ln):
            s, done, E = FS, f.done, f.E
            if E < 8:
                link(V.memset(logits[:, E:8], -3e38))
            for t in range(NT + 3):
                u, v = t - 2, t - 3
                adds, norms = 0 <= u < NT, 0 <= v < NT - (f.index == 0) and next_ln != 4
                if norms:
                    ln_norm(next_ln, v)
                if 0 <= t - 1 < NT:
                    dve.wait_ge(s["hidT_hi"], done + t)
                    sub_hi(hidT[0:f.rows, LO, 0:f.parts],
                           psP[0:f.rows, 0:f.parts * P].rearrange("p (j t) -> p j t", t=P),
                           hidT[0:f.rows, HI, 0:f.parts]).then_inc(s["hidT_lo"], 1)
                if norms and t < NT:
                    ln_lo(next_ln, v)
                if adds:
                    dve.wait_ge(s["experts"], done + u + 1)
                    V.tensor_tensor(x[:, u], x[:, u], ring3(u)[:], ALU.add).then_inc(s["x_add"], 1)
                if t < NT and (t > 0 or not f.dense):
                    gates(f, t, u if adds else None, next_ln)
                elif adds:
                    dve.wait_ge(s["x_add"], done + u + 1)
                    ln_stats(next_ln, u)
                if norms and t >= NT:
                    ln_lo(next_ln, v)
                if t == 0 and f.dense:
                    ln_norm(f.ln, NT - 1)
                if t == 1 and f.dense:
                    ln_lo(f.ln, NT - 1)
                if f.index == 0 and t == NT + 2:
                    low_wq(9)
                if f.index == 1 and t == 6:
                    ctx_max(0)
                    ln_norm(4, 0)
                if f.index == 1 and t == 5:
                    dve.wait_ge(ld["vec_hi"], 1)
                    for r in bias_row.values():
                        i = sub_hi(pT[r:r + 1, LO], wide[r:r + 1], pT[r:r + 1, HI])
                    i.then_inc(ld["vec_lo"], 1)
                if f.index == 2 and t == 8 :
                    mean_square("f", 0, 6, 0)
                    features(0)

        def ctx_max(n):
            dve.wait_ge(ld[f"c{n % 4}"], (n // 4 + 1) * 16)
            link(V.tensor_reduce(mx[:, 0:1], stage_q[:, n % 4], AX.X, ALU.max))
            V.tensor_scalar(small[:, 8 + n % 2:9 + n % 2], mx[:, 0:1], -1.0, None, ALU.mult).then_inc(M["k_max"], 1)

        def linear_attention(next_ln):
            s = M
            by8 = lambda ap: ap.rearrange("p (g e) -> p g e", e=8)
            group = k_sb[:, 0:S]

            dve.wait_ge(setup["b8"], 3)
            for t in range(NT + 4):
                u = t - 2
                if 0 <= u < NT:
                    dve.wait_ge(s["out"], u + 1)
                    V.tensor_tensor(x[:, u], x[:, u], psY[:], ALU.add).then_inc(s["x_add"], 1)
                if 0 <= t - 1 < NT:
                    dve.wait_ge(s["kv"], t)
                    link(V.reciprocal(small[:, 12:13], small[:, 10 + (t - 1) % 2:11 + (t - 1) % 2]))
                    V.scalar_tensor_tensor(kvs, psKV[:, 0:P], small[:, 12:13], block8[:], ALU.mult,
                                           ALU.mult).then_inc(s["kvs"], 1)
                if 0 <= u < NT:
                    dve.wait_ge(s["x_add"], u + 1)
                    ln_stats(next_ln, u)
                if t < NT:
                    dve.wait_ge(LNS[4]["tr"], ln_at(4, t + 1))
                    link(V.tensor_reduce(group, by8(psT[:]), AX.X, ALU.max))
                    V.tensor_tensor(by8(q_sb[:]), by8(psT[:]), group.unsqueeze(2).to_broadcast([P, S, 8]),
                                    ALU.subtract).then_inc(s["q_shift"], 1)
                if 0 <= t - 1 < NT:
                    dve.wait_ge(s["kvs_hi"], t)
                    sub_hi(kvs_r[:, (t - 1) % 2, LO], kvs, kvs_r[:, (t - 1) % 2, HI]).then_inc(s["kvs_lo"], 1)
                if t < NT:
                    dve.wait_ge(s["eT_hi"], t + 1)
                    sub_hi(eT[:, LO], slices(psS), eT[:, HI]).then_inc(s["eT_lo"], 1)
                if 0 <= t - 1 < NT:
                    dve.wait_ge(s["q2_hi"], t)
                    sub_hi(q2[:, LO], psP[:], q2[:, HI]).then_inc(s["q2_lo"], 1)
                if t < NT:
                    dve.wait_ge(s["q_exp"], t + 1)
                    link(V.tensor_reduce(group, by8(q_sb[:]), AX.X, ALU.add))
                    link(V.reciprocal(group, group))
                    need(dve, s["q_tr"], t)
                    V.tensor_tensor(by8(prob[:]), by8(q_sb[:]), group.unsqueeze(2).to_broadcast([P, S, 8]),
                                    ALU.mult).then_inc(s["q_soft"], 1)
                if t + 1 < NT:
                    ctx_max(t + 1)
                if 0 <= t - 3 < NT:
                    ln_lo(next_ln, t - 3)
                if t == 5:
                    low_wq(18, stage_o)

        def cross_attention(next_ln):
            s = N3
            def f_lo(n):
                dve.wait_ge(s["f_hi"], n + 1)
                sub_hi(f_r[:, n % 3, LO], stage_q[:, n % 4], f_r[:, n % 3, HI]).then_inc(s["f_lo"], 1)

            def fT_lo(n):
                dve.wait_ge(s["fT_hi"], n + 1)
                sub_hi(fT[:, LO], slices(psS), fT[:, HI]).then_inc(s["fT_lo"], 1)

            link(V.memset(s_sb[:, 0:P], 0.0))
            f_lo(0)
            fT_lo(0)
            for t in range(NT + 4):
                u = t - 1
                if 0 <= u < NT:
                    mean_square("q", u, 8, 4)
                    dve.wait_ge(s["kT_hi"], u + 1)
                    sub_hi(kT3[:, LO], slices(k3w), kT3[:, HI]).then_inc(s["kT_lo"], 1)
                if t + 1 < NT:
                    mean_square("f", t + 1, 6, 0)
                if 0 <= u < NT:
                    dve.wait_ge(s["pw_q"], u + 1)
                    link(V.tensor_scalar(col(9), col(5), D ** -0.5, None, ALU.mult))
                if 0 <= t - 3 < NT:
                    ln_norm(next_ln, t - 3)
                if t + 1 < NT:
                    features(t + 1)
                if t < NT:
                    mean_square("k", t, 7, 2)
                if 0 <= u < NT:
                    dve.wait_ge(s["qT_hi"], u + 1)
                    sub_hi(qT3[:, LO], slices(psT), qT3[:, HI]).then_inc(s["qT_lo"], 1)
                if 0 <= t - 2 < NT:
                    dve.wait_ge(s["attend"], t - 1)
                    V.tensor_tensor(x[:, t - 2], x[:, t - 2], psY[:], ALU.add).then_inc(s["x_add"], 1)
                    dve.wait_ge(s["x_add"], t - 1)
                    ln_stats(next_ln, t - 2)
                if 0 <= t - 4 < NT:
                    hits_of(t - 4)
                if 0 <= u < NT:
                    dve.wait_ge(s["scores"], u + 1)
                    for b in range(2):
                        rows = slice(b * S, (b + 1) * S)
                        i = V.tensor_reduce(mx[rows, 0:1], psO[rows, 0, rows], AX.X, ALU.max)
                    link(i)
                    V.tensor_scalar(col(10), mx[:, 0:1], col(9), -1.0, ALU.mult, ALU.mult).then_inc(s["neg_max"], 1)
                if t + 1 < NT:
                    f_lo(t + 1)
                if 0 <= u < NT:
                    dve.wait_ge(s["exp"], u + 1)
                    link(V.reciprocal(col(12), col(11)))
                    V.tensor_scalar(s_sb[:, 0:P], s_sb[:, 0:P], col(12), None, ALU.mult).then_inc(s["prob"], 1)
                if 0 <= t - 3 < NT:
                    ln_lo(next_ln, t - 3)
                if t + 1 < NT:
                    fT_lo(t + 1)
                if 0 <= u < NT:
                    dve.wait_ge(s["pT_hi"], u + 1)
                    sub_hi(pT3[:, LO], psO[:, 1, 0:P], pT3[:, HI]).then_inc(s["pT_lo"], 1)
                if t < NT:
                    dve.wait_ge(s["k_tr"], t + 1)
                    V.tensor_tensor(slices(k3w), slices(psP), wqk3[:, 2].unsqueeze(2).to_broadcast([P, KT, P]),
                                    ALU.mult).then_inc(s["kw"], 1)
                if t == NT:
                    low_wq(19, stage_o)

        def hits_of(n):
            s = C3
            dve.wait_ge(s["sim"], n + 1)
            link(V.tensor_reduce(mx[:, 1:2], psO[:, 1, P:P + 64], AX.X, ALU.max))
            V.tensor_scalar(small[:, 13:14], mx[:, 1:2], -1.0 / TEMPERATURE, None, ALU.mult).then_inc(s["neg_max"], 1)
            dve.wait_ge(s["exp"], n + 1)
            link(V.reciprocal(small[:, 15:16], small[:, 14:15]))
            V.tensor_scalar(hit(n), hit_exp[:], small[:, 15:16], THRESHOLD, ALU.mult, ALU.is_gt).then_inc(s["hits"], 1)
            dve.wait_ge(s["hits"], n + 1)
            link(V.tensor_reduce(q_any[:, n:n + 1], hit(n).bitcast(f32), AX.X, ALU.max))

        def clustered():
            s = C3
            dve.wait_ge(ld["asg_in"], 16)
            V.tensor_scalar(prob[0:64], q_sb[0:64].bitcast(i32), row_id[0:64], None, ALU.is_equal)
            dve.wait_ge(s["count"], 1)
            link(V.tensor_scalar(small[0:64, 0:1], psO[0:64, 0, 0:1], 0.5, None, ALU.is_ge))
            V.tensor_scalar(s_sb[0:64, 0:P], ones[0:64, :], small[0:64, 0:1], None, ALU.mult).then_inc(s["sel"], 1)
            dve.wait_ge(s["rows"], 1)
            link(V.tensor_copy(wide[:], psT[:]))
            for t in range(NT):
                dve.wait_ge(s["dense"], t + 1)
                need(dve, s["out"], t - 1)
                kept = (xn[:, 1], prob[:])[t % 2]
                V.scalar_tensor_tensor(kept, dense_bank(t)[:], q_any[:, t:t + 1], wide[:], ALU.mult,
                                       ALU.mult).then_inc(s["masked"], 1)
                dve.wait_ge(s["masked"], t + 1)
                V.tensor_tensor(x[:, t], x[:, t], kept, ALU.add).then_inc(s["out"], 1)

        x_stats(0)
        x_stats(1)
        ln_norm(0, 0)
        ln_norm(0, 1)
        low_wq(0)
        ln_lo(0, 0)
        ln_lo(0, 1)
        low_ctx(0)
        x_stats(2)
        x_stats(3)
        attention(L0, 1)
        ffn(FF[0], 2)
        attention(L1, 3)
        ffn(FF[1], 4)
        linear_attention(5)
        ffn(FF[2], 6)
        cross_attention(7)
        clustered()

    block_cm.__exit__(None, None, None)


def arrays_of(inputs):
    import numpy as np
    f = {k: np.asarray(a) for k, a in inputs.items()}
    c = np.ascontiguousarray

    def by_slice(w):
        return c(w.reshape(KT, P, -1).transpose(1, 0, 2))

    def head_groups(w):
        return c(w.reshape(KT, P, NHG, D).transpose(2, 1, 0, 3))

    def out_groups(w):
        return c(w.reshape(NHG, HQ, P, D).transpose(0, 2, 1, 3))

    def kv_groups(wk, wv, n):
        both = np.concatenate([wk.reshape(KT, P, n, HD), wv.reshape(KT, P, n, HD)], axis=3)
        return c(both.transpose(2, 1, 0, 3).reshape(n, P, 2, 512))

    a = {}
    a["x"] = c(f["x"].reshape(NT, P, D).transpose(1, 0, 2))
    a["ctxT"] = c(f["ctx_4096"].reshape(2, 512, KT, P).transpose(0, 3, 2, 1))
    a["wq0"] = head_groups(f["L0_xattn_Wq"])
    a["wo0"] = out_groups(f["L0_xattn_Wo"])
    a["wkv0"] = kv_groups(f["L0_xattn_Wk"], f["L0_xattn_Wv"], 4)
    a["wq1"] = head_groups(f["L1_xattn_Wq"].T)
    a["wo1"] = out_groups(f["L1_xattn_Wo"].T)
    a["wkv1"] = kv_groups(f["L1_xattn_Wk"].T, f["L1_xattn_Wv"].T, NHG)
    a["mask"] = c(f["mask_1x1xSxS2_ff0"].reshape(S, S))

    def two_slices(w):
        return c(w.reshape(2, 2, P, -1).transpose(2, 0, 1, 3).reshape(P, 2, -1))

    def gate_a(gate, lora_a):
        return two_slices(np.concatenate([gate, lora_a.reshape(-1, D)]).T)

    def ranks(lora_b):
        return lora_b.transpose(0, 2, 1).reshape(-1, D)

    a["ga0"] = gate_a(f["L0_ffn_gate_W"], f["L0_ffn_lora_A"])
    a["ga1"] = gate_a(f["L1_ffn_gate_W"], f["L1_ffn_A"])
    a["ga2"] = gate_a(f["L2_ffn_router_w"], f["L2_ffn_A"])
    a["cent"] = two_slices(f["L3_ffn_centroids"].T)
    a["base0"], a["base1"] = by_slice(f["L0_ffn_base_W"].T), by_slice(f["L1_ffn_W_base"].T)
    a["wq3"], a["wk3"] = by_slice(f["L3_xattn_Wq_w"].T), by_slice(f["L3_xattn_Wk_w"].T)
    a["w3"] = by_slice(f["L3_ffn_weight"].T)
    a["b0"] = c(ranks(f["L0_ffn_lora_B"]).reshape(2, 112, D).transpose(1, 0, 2))
    a["b1"], a["b2"] = (c(ranks(f[n])[:, None]) for n in ("L1_ffn_B", "L2_ffn_B"))
    a["ctx"] = c(f["ctx_4096"].reshape(NT, P, D).transpose(1, 0, 2))
    a["qn1"], a["kn1"] = f["L1_xattn_q_norm_w"].reshape(P, 1), f["L1_xattn_k_norm_w"].reshape(P, 1)
    a["qn3"], a["kn3"] = (c(f[n].reshape(KT, P).T) for n in ("L3_xattn_qn_w", "L3_xattn_kn_w"))
    for name, n in (("bq3", "L3_xattn_Wq_b"), ("bk3", "L3_xattn_Wk_b"), ("bias3", "L3_ffn_bias"),
                    ("fn_w", "L3_xattn_fn_w"), ("asg", "L3_ffn_assignments")):
        a[name] = f[n].reshape(1, D)
    return a


def kernel(**inputs):
    import concourse.bacc as bacc
    from concourse.bass_utils import run_bass_kernel_spmd

    nc = bacc.Bacc("TRN2", target_bir_lowering=False, num_devices=1)
    arrays, io = {}, {}
    for name, a in arrays_of(inputs).items():
        arrays["in_" + name] = a
        io[name] = nc.dram_tensor("in_" + name, a.shape, mybir.dt.from_np(a.dtype), kind="ExternalInput").ap()
    io["out"] = nc.dram_tensor("out", (P, NT, D), mybir.dt.float32, kind="ExternalOutput").ap()
    build(nc, io)
    got = run_bass_kernel_spmd(nc, [arrays], core_ids=[0]).results[0]["out"]
    return got.transpose(1, 0, 2).reshape(B, S, D)
```
